# Optimizing a Trainium2 kernel written in Bass

```python
import numpy as np
import jax
import jax.numpy as jnp

def _softmax(x, axis=-1):
    return jax.nn.softmax(x, axis=axis)

def _gelu(x):
    return jax.nn.gelu(x, approximate=True)

def _silu(x):
    return jax.nn.silu(x)

def _sigmoid(x):
    return jax.nn.sigmoid(x)

def _layernorm(x, axis=-1, eps=1e-05):
    m = jnp.mean(x, axis=axis, keepdims=True)
    v = jnp.var(x, axis=axis, keepdims=True)
    return (x - m) / jnp.sqrt(v + eps)

def _scatter_add(tgt, idx, src, axis=0):
    return tgt.at[idx].add(src)

def _segment_sum(src, seg, n):
    return jax.ops.segment_sum(src, seg, n)
kernel_name = 'mk_decoder_preln_d2_seqx_r4_a45481'

def setup_inputs(seed: int=0):
    np.random.seed(seed)
    _w = jnp.asarray

    def _rec_inputs():
        import jax
        import jax.numpy as jnp
        _rk = jax.random.key(seed)
        x = -0.0002928 + 1 * jax.random.normal(jax.random.fold_in(_rk, 1), (16, 128, 256), jnp.float32)
        _lenS = 128 - jax.random.randint(jax.random.fold_in(_rk, 7), (16,), 0, max(1, 128 // 4) + 1, jnp.int32)
        _lenS2 = 128 - jax.random.randint(jax.random.fold_in(_rk, 8), (16,), 0, max(1, 128 // 4) + 1, jnp.int32)
        _ctx_1024P = jax.random.normal(jax.random.fold_in(_rk, 11), (16, 16, 256), jnp.float32)
        _ctx_1024c = jax.random.dirichlet(jax.random.fold_in(_rk, 511), 0.3 * jnp.ones((16,), jnp.float32), (16, 128))
        _ctx_1024t = jnp.einsum('bsk,bkd->bsd', _ctx_1024c, _ctx_1024P)
        _ctx_1024t = _ctx_1024t * jax.lax.rsqrt(jnp.mean(jnp.square(_ctx_1024t)) + 1e-12) * 0.953939
        ctx_1024 = -1.39393e-06 + 0.999914 * (_ctx_1024t + 0.3 * jax.random.normal(jax.random.fold_in(_rk, 611), (16, 128, 256), jnp.float32))
        _validS = jnp.arange(128)[None, :] < _lenS[:, None]
        _validS2 = jnp.arange(128)[None, :] < _lenS2[:, None]
        _causal = jnp.tril(jnp.ones((128, 128), dtype=bool))
        mask_BxS2_bf0 = jnp.logical_not(jnp.ones((16, 128), dtype=bool))
        return (x, ctx_1024, mask_BxS2_bf0)
    x, ctx_1024, mask_BxS2_bf0 = _rec_inputs()

    def _L0_attn_setup():
        import jax, jax.numpy as jnp
        import numpy as np
        N_HEAD = 16
        BUCKET = 64
        HIDDEN = 256
        EPS = 1e-05

        def _ln(x, g, b):
            m = x.mean(-1, keepdims=True)
            v = x.var(-1, keepdims=True)
            return (x - m) * jax.lax.rsqrt(v + EPS) * g + b
        key = jax.random.key(seed)
        ks = jax.random.split(key, 6)

        def w(k, shape, s=0.02):
            return jax.random.normal(k, shape, jnp.float32) * s
        C = HIDDEN
        return {'x': jax.random.normal(ks[0], (4, 2048, C), jnp.float32), 'ln1_g': jnp.ones((C,), jnp.float32), 'ln1_b': jnp.zeros((C,), jnp.float32), 'w_qkv': w(ks[1], (C, 3 * C)), 'b_qkv': jnp.zeros((3 * C,), jnp.float32), 'w_out': w(ks[2], (C, C)), 'b_out': jnp.zeros((C,), jnp.float32), 'ln2_g': jnp.ones((C,), jnp.float32), 'ln2_b': jnp.zeros((C,), jnp.float32), 'w1': w(ks[3], (C, 4 * C)), 'b1': jnp.zeros((4 * C,), jnp.float32), 'w2': w(ks[4], (4 * C, C)), 'b2': jnp.zeros((C,), jnp.float32)}
    _L0_attn_all = _L0_attn_setup()
    _L0_attn_in = {k: v for k, v in _L0_attn_all.items() if k in ('ln1_g', 'ln1_b', 'w_qkv', 'b_qkv', 'w_out', 'b_out', 'ln2_g', 'ln2_b', 'w1', 'b1', 'w2', 'b2')}
    del _L0_attn_all

    def _L0_xattn_setup():
        import jax, jax.numpy as jnp
        import numpy as np
        EMBED = 256
        HEADS = 16
        HD = EMBED // HEADS
        SCALE_BASE = 128
        OFFSET = 0

        def _dup_interleave(m):
            return jnp.repeat(m, 2, axis=-1)

        def _rotate_every_two(x):
            x1 = x[..., ::2]
            x2 = x[..., 1::2]
            return jnp.stack([-x2, x1], axis=-1).reshape(x.shape)

        def _xpos(x, offset, downscale):
            T = x.shape[2]
            half = HD // 2
            scale_vec = (jnp.arange(0, HD, 2, dtype=jnp.float32) + 0.4 * HD) / (1.4 * HD)
            min_pos = -(T + offset) // 2
            power = jnp.arange(min_pos, min_pos + T, dtype=jnp.float32) / SCALE_BASE
            scale = scale_vec[None, :] ** power[:, None]
            inv_freq = 1.0 / 10000.0 ** (jnp.arange(half, dtype=jnp.float32) / half)
            ang = jnp.arange(T, dtype=jnp.float32)[:, None] * inv_freq[None, :]
            sin, cos = (jnp.sin(ang), jnp.cos(ang))
            if downscale:
                scale = 1.0 / scale
            sin_s = _dup_interleave(sin * scale)
            cos_s = _dup_interleave(cos * scale)
            return x * cos_s + _rotate_every_two(x) * sin_s
        rng = jax.random.key(seed)
        ks = jax.random.split(rng, 8)
        B, T, C = (2, 512, EMBED)
        s = 1.0 / np.sqrt(C)
        return {'query': jax.random.normal(ks[0], (B, T, C), jnp.float32), 'key': jax.random.normal(ks[1], (B, T, C), jnp.float32), 'value': jax.random.normal(ks[2], (B, T, C), jnp.float32), 'key_padding_mask': jnp.zeros((B, T), jnp.bool_), 'Wq': jax.random.normal(ks[3], (C, C), jnp.float32) * s, 'bq': jnp.zeros((C,), jnp.float32), 'Wk': jax.random.normal(ks[4], (C, C), jnp.float32) * s, 'bk': jnp.zeros((C,), jnp.float32), 'Wv': jax.random.normal(ks[5], (C, C), jnp.float32) * s, 'bv': jnp.zeros((C,), jnp.float32), 'Wo': jax.random.normal(ks[6], (C, C), jnp.float32) * s, 'bo': jnp.zeros((C,), jnp.float32)}
    _L0_xattn_all = _L0_xattn_setup()
    _L0_xattn_in = {k: v for k, v in _L0_xattn_all.items() if k in ('Wq', 'bq', 'Wk', 'bk', 'Wv', 'bv', 'Wo', 'bo')}
    del _L0_xattn_all

    def _L0_ffn_setup():
        import jax, jax.numpy as jnp
        import numpy as np
        D_MODEL = 256
        N_HEADS = 16
        D_HEAD = D_MODEL // N_HEADS
        N_EXPERTS = 8
        TOP_K = 2
        D_FF = 512
        EPS = 1e-06

        def rmsnorm(x, w):
            return x * jax.lax.rsqrt(jnp.mean(x * x, axis=-1, keepdims=True) + EPS) * w

        def swiglu(x, w_gate, w_up, w_down):
            return jax.nn.silu(x @ w_gate) * (x @ w_up) @ w_down
        key = jax.random.key(seed)
        ks = jax.random.split(key, 16)
        s = 0.02
        B, S = (2, 512)
        return {'X': jax.random.normal(ks[0], (B, S, D_MODEL), dtype=jnp.float32), 'norm1_w': jnp.ones((D_MODEL,), jnp.float32), 'norm2_w': jnp.ones((D_MODEL,), jnp.float32), 'wq': jax.random.normal(ks[1], (D_MODEL, D_MODEL), jnp.float32) * s, 'wk': jax.random.normal(ks[2], (D_MODEL, D_MODEL), jnp.float32) * s, 'wv': jax.random.normal(ks[3], (D_MODEL, D_MODEL), jnp.float32) * s, 'wo': jax.random.normal(ks[4], (D_MODEL, D_MODEL), jnp.float32) * s, 'router_w': jax.random.normal(ks[5], (D_MODEL, N_EXPERTS), jnp.float32) * s, 'sh_gate': jax.random.normal(ks[6], (D_MODEL, D_FF), jnp.float32) * s, 'sh_up': jax.random.normal(ks[7], (D_MODEL, D_FF), jnp.float32) * s, 'sh_down': jax.random.normal(ks[8], (D_FF, D_MODEL), jnp.float32) * s, 'e_gate': jax.random.normal(ks[9], (N_EXPERTS, D_MODEL, D_FF), jnp.float32) * s, 'e_up': jax.random.normal(ks[10], (N_EXPERTS, D_MODEL, D_FF), jnp.float32) * s, 'e_down': jax.random.normal(ks[11], (N_EXPERTS, D_FF, D_MODEL), jnp.float32) * s}
    _L0_ffn_all = _L0_ffn_setup()
    _L0_ffn_in = {k: v for k, v in _L0_ffn_all.items() if k in ('norm1_w', 'norm2_w', 'wq', 'wk', 'wv', 'wo', 'router_w', 'sh_gate', 'sh_up', 'sh_down', 'e_gate', 'e_up', 'e_down')}
    del _L0_ffn_all

    def _L1_attn_setup():
        import jax, jax.numpy as jnp
        import numpy as np
        EPS = 1e-05

        def xpos_rotate(x, offset=0, conjugate=False):
            b, s, h, dh = x.shape
            expoent = jnp.arange(0, dh, 2, dtype=jnp.float32) / dh
            angle = 10.0 ** (-4.0 * expoent)
            if conjugate:
                angle = -angle
            pos = jnp.arange(offset, s + offset, dtype=jnp.float32)
            nangle = pos[:, None] * angle[None, :]
            sin = jnp.sin(nangle)[None, :, None, :]
            cos = jnp.cos(nangle)[None, :, None, :]
            x0 = x[..., 0::2]
            x1 = x[..., 1::2]
            rot = jnp.stack([x0 * cos - x1 * sin, x0 * sin + x1 * cos], axis=-1)
            return rot.reshape(b, s, h, dh)

        def decay_mask(nseq, scale):
            idx = jnp.arange(nseq)
            diff = idx[:, None] - idx[None, :]
            mask = (diff >= 0).astype(scale.dtype)
            diff_c = jnp.maximum(diff, 0).astype(scale.dtype)
            logd = diff_c[None, :, :] * jnp.log(scale)[:, None, None]
            return jnp.exp(logd) * mask[None, :, :]

        def group_norm(R, gamma, beta, nheads):
            b, s, d = R.shape
            dh = d // nheads
            Rg = R.reshape(b, s, nheads, dh)
            mu = jnp.mean(Rg, axis=-1, keepdims=True)
            var = jnp.var(Rg, axis=-1, keepdims=True)
            Rn = (Rg - mu) * jax.lax.rsqrt(var + EPS)
            Rn = Rn * gamma.reshape(1, 1, nheads, dh) + beta.reshape(1, 1, nheads, dh)
            return Rn.reshape(b, s, d)
        key = jax.random.key(seed)
        ks = jax.random.split(key, 7)
        b, s, d, h = (2, 512, 256, 16)
        dh = d // h
        x = jax.random.normal(ks[0], (b, s, d), dtype=jnp.float32)
        std_qkv = float(np.sqrt(2.0 / (dh + d)))
        std_o = float(np.sqrt(2.0 / (d + d)))
        WQ = jax.random.normal(ks[1], (h, dh, d), dtype=jnp.float32) * std_qkv
        WK = jax.random.normal(ks[2], (h, dh, d), dtype=jnp.float32) * std_qkv
        WV = jax.random.normal(ks[3], (h, dh, d), dtype=jnp.float32) * std_qkv
        WO = jax.random.normal(ks[4], (d, d), dtype=jnp.float32) * std_o
        gamma = jnp.ones((d,), dtype=jnp.float32)
        beta = jnp.zeros((d,), dtype=jnp.float32)
        return {'x': x, 'WQ': WQ, 'WK': WK, 'WV': WV, 'WO': WO, 'gamma': gamma, 'beta': beta}
    _L1_attn_all = _L1_attn_setup()
    _L1_attn_in = {k: v for k, v in _L1_attn_all.items() if k in ('WQ', 'WK', 'WV', 'WO', 'gamma', 'beta')}
    del _L1_attn_all

    def _L1_xattn_setup():
        import jax, jax.numpy as jnp
        import numpy as np
        D_MODEL = 256
        N_HEADS = 16
        D_K = D_MODEL // N_HEADS
        WINDOW = 64
        B, S = (1, 1024)
        key = jax.random.key(seed)
        ks = jax.random.split(key, 11)
        sc = 1.0 / np.sqrt(D_MODEL)
        inp = {'query': jax.random.normal(ks[0], (B, S, D_MODEL), jnp.float32), 'key': jax.random.normal(ks[1], (B, S, D_MODEL), jnp.float32), 'value': jax.random.normal(ks[2], (B, S, D_MODEL), jnp.float32), 'Wq': jax.random.normal(ks[3], (D_MODEL, D_MODEL), jnp.float32) * sc, 'bq': jax.random.normal(ks[4], (D_MODEL,), jnp.float32) * 0.01, 'Wk': jax.random.normal(ks[5], (D_MODEL, D_MODEL), jnp.float32) * sc, 'bk': jax.random.normal(ks[6], (D_MODEL,), jnp.float32) * 0.01, 'Wv': jax.random.normal(ks[7], (D_MODEL, D_MODEL), jnp.float32) * sc, 'bv': jax.random.normal(ks[8], (D_MODEL,), jnp.float32) * 0.01, 'Wo': jax.random.normal(ks[9], (D_MODEL, D_MODEL), jnp.float32) * sc, 'bo': jax.random.normal(ks[10], (D_MODEL,), jnp.float32) * 0.01}
        return inp
    _L1_xattn_all = _L1_xattn_setup()
    _L1_xattn_in = {k: v for k, v in _L1_xattn_all.items() if k in ('Wq', 'bq', 'Wk', 'bk', 'Wv', 'bv', 'Wo', 'bo')}
    del _L1_xattn_all

    def _L1_ffn_setup():
        import jax, jax.numpy as jnp
        import numpy as np
        DIM = 256
        E = 16
        TOPK = 2
        G = 4
        TOPK_G = 2
        INTER = 128
        N_SHARED = 2
        ROUTE_SCALE = 1.0

        def _gate(xf, gate_w, gate_b):
            scores = xf @ gate_w.T
            scores = jax.nn.softmax(scores.astype(jnp.float32), axis=-1)
            orig = scores
            scores = scores + gate_b
            T = xf.shape[0]
            sg = scores.reshape(T, G, E // G)
            group_scores = jax.lax.top_k(sg, 2)[0].sum(-1)
            _, gidx = jax.lax.top_k(group_scores, TOPK_G)
            keep = jax.nn.one_hot(gidx, G).sum(axis=1) > 0
            sg = jnp.where(keep[:, :, None], sg, -jnp.inf)
            scores = sg.reshape(T, E)
            _, idx = jax.lax.top_k(scores, TOPK)
            weights = jnp.take_along_axis(orig, idx, axis=1)
            weights = (weights * ROUTE_SCALE).astype(xf.dtype)
            return (weights, idx)
        key = jax.random.key(seed)
        ks = jax.random.split(key, 16)
        s = lambda fan_in: 1.0 / np.sqrt(fan_in)
        inp = {'x': jax.random.normal(ks[0], (4, 256, DIM), dtype=jnp.float32), 'gate_w': jax.random.normal(ks[1], (E, DIM), dtype=jnp.float32) * s(DIM), 'gate_b': jnp.zeros((E,), dtype=jnp.float32), 'We1': jax.random.normal(ks[2], (E, DIM, INTER), dtype=jnp.float32) * s(DIM), 'be1': jnp.zeros((E, INTER), dtype=jnp.float32), 'We2': jax.random.normal(ks[3], (E, INTER, DIM), dtype=jnp.float32) * s(INTER), 'be2': jnp.zeros((E, DIM), dtype=jnp.float32), 'We3': jax.random.normal(ks[4], (E, DIM, INTER), dtype=jnp.float32) * s(DIM), 'be3': jnp.zeros((E, INTER), dtype=jnp.float32), 'ws1': jax.random.normal(ks[5], (DIM, N_SHARED * INTER), dtype=jnp.float32) * s(DIM), 'bs1': jnp.zeros((N_SHARED * INTER,), dtype=jnp.float32), 'ws2': jax.random.normal(ks[6], (N_SHARED * INTER, DIM), dtype=jnp.float32) * s(N_SHARED * INTER), 'bs2': jnp.zeros((DIM,), dtype=jnp.float32), 'ws3': jax.random.normal(ks[7], (DIM, N_SHARED * INTER), dtype=jnp.float32) * s(DIM), 'bs3': jnp.zeros((N_SHARED * INTER,), dtype=jnp.float32)}
        return inp
    _L1_ffn_all = _L1_ffn_setup()
    _L1_ffn_in = {k: v for k, v in _L1_ffn_all.items() if k in ('gate_w', 'gate_b', 'We1', 'be1', 'We2', 'be2', 'We3', 'be3', 'ws1', 'bs1', 'ws2', 'bs2', 'ws3', 'bs3')}
    del _L1_ffn_all
    return {'x': x, 'ctx_1024': ctx_1024, 'mask_BxS2_bf0': mask_BxS2_bf0, 'L0_attn_ln1_g': _L0_attn_in['ln1_g'], 'L0_attn_ln1_b': _L0_attn_in['ln1_b'], 'L0_attn_w_qkv': _L0_attn_in['w_qkv'], 'L0_attn_b_qkv': _L0_attn_in['b_qkv'], 'L0_attn_w_out': _L0_attn_in['w_out'], 'L0_attn_b_out': _L0_attn_in['b_out'], 'L0_attn_ln2_g': _L0_attn_in['ln2_g'], 'L0_attn_ln2_b': _L0_attn_in['ln2_b'], 'L0_attn_w1': _L0_attn_in['w1'], 'L0_attn_b1': _L0_attn_in['b1'], 'L0_attn_w2': _L0_attn_in['w2'], 'L0_attn_b2': _L0_attn_in['b2'], 'L0_xattn_Wq': _L0_xattn_in['Wq'], 'L0_xattn_bq': _L0_xattn_in['bq'], 'L0_xattn_Wk': _L0_xattn_in['Wk'], 'L0_xattn_bk': _L0_xattn_in['bk'], 'L0_xattn_Wv': _L0_xattn_in['Wv'], 'L0_xattn_bv': _L0_xattn_in['bv'], 'L0_xattn_Wo': _L0_xattn_in['Wo'], 'L0_xattn_bo': _L0_xattn_in['bo'], 'L0_ffn_norm1_w': _L0_ffn_in['norm1_w'], 'L0_ffn_norm2_w': _L0_ffn_in['norm2_w'], 'L0_ffn_wq': _L0_ffn_in['wq'], 'L0_ffn_wk': _L0_ffn_in['wk'], 'L0_ffn_wv': _L0_ffn_in['wv'], 'L0_ffn_wo': _L0_ffn_in['wo'], 'L0_ffn_router_w': _L0_ffn_in['router_w'], 'L0_ffn_sh_gate': _L0_ffn_in['sh_gate'], 'L0_ffn_sh_up': _L0_ffn_in['sh_up'], 'L0_ffn_sh_down': _L0_ffn_in['sh_down'], 'L0_ffn_e_gate': _L0_ffn_in['e_gate'], 'L0_ffn_e_up': _L0_ffn_in['e_up'], 'L0_ffn_e_down': _L0_ffn_in['e_down'], 'L1_attn_WQ': _L1_attn_in['WQ'], 'L1_attn_WK': _L1_attn_in['WK'], 'L1_attn_WV': _L1_attn_in['WV'], 'L1_attn_WO': _L1_attn_in['WO'], 'L1_attn_gamma': _L1_attn_in['gamma'], 'L1_attn_beta': _L1_attn_in['beta'], 'L1_xattn_Wq': _L1_xattn_in['Wq'], 'L1_xattn_bq': _L1_xattn_in['bq'], 'L1_xattn_Wk': _L1_xattn_in['Wk'], 'L1_xattn_bk': _L1_xattn_in['bk'], 'L1_xattn_Wv': _L1_xattn_in['Wv'], 'L1_xattn_bv': _L1_xattn_in['bv'], 'L1_xattn_Wo': _L1_xattn_in['Wo'], 'L1_xattn_bo': _L1_xattn_in['bo'], 'L1_ffn_gate_w': _L1_ffn_in['gate_w'], 'L1_ffn_gate_b': _L1_ffn_in['gate_b'], 'L1_ffn_We1': _L1_ffn_in['We1'], 'L1_ffn_be1': _L1_ffn_in['be1'], 'L1_ffn_We2': _L1_ffn_in['We2'], 'L1_ffn_be2': _L1_ffn_in['be2'], 'L1_ffn_We3': _L1_ffn_in['We3'], 'L1_ffn_be3': _L1_ffn_in['be3'], 'L1_ffn_ws1': _L1_ffn_in['ws1'], 'L1_ffn_bs1': _L1_ffn_in['bs1'], 'L1_ffn_ws2': _L1_ffn_in['ws2'], 'L1_ffn_bs2': _L1_ffn_in['bs2'], 'L1_ffn_ws3': _L1_ffn_in['ws3'], 'L1_ffn_bs3': _L1_ffn_in['bs3']}

def reference(x, ctx_1024, mask_BxS2_bf0, L0_attn_ln1_g, L0_attn_ln1_b, L0_attn_w_qkv, L0_attn_b_qkv, L0_attn_w_out, L0_attn_b_out, L0_attn_ln2_g, L0_attn_ln2_b, L0_attn_w1, L0_attn_b1, L0_attn_w2, L0_attn_b2, L0_xattn_Wq, L0_xattn_bq, L0_xattn_Wk, L0_xattn_bk, L0_xattn_Wv, L0_xattn_bv, L0_xattn_Wo, L0_xattn_bo, L0_ffn_norm1_w, L0_ffn_norm2_w, L0_ffn_wq, L0_ffn_wk, L0_ffn_wv, L0_ffn_wo, L0_ffn_router_w, L0_ffn_sh_gate, L0_ffn_sh_up, L0_ffn_sh_down, L0_ffn_e_gate, L0_ffn_e_up, L0_ffn_e_down, L1_attn_WQ, L1_attn_WK, L1_attn_WV, L1_attn_WO, L1_attn_gamma, L1_attn_beta, L1_xattn_Wq, L1_xattn_bq, L1_xattn_Wk, L1_xattn_bk, L1_xattn_Wv, L1_xattn_bv, L1_xattn_Wo, L1_xattn_bo, L1_ffn_gate_w, L1_ffn_gate_b, L1_ffn_We1, L1_ffn_be1, L1_ffn_We2, L1_ffn_be2, L1_ffn_We3, L1_ffn_be3, L1_ffn_ws1, L1_ffn_bs1, L1_ffn_ws2, L1_ffn_bs2, L1_ffn_ws3, L1_ffn_bs3):
    import jax
    import jax.numpy as jnp

    def _L0_attn_ref(x, ln1_g, ln1_b, w_qkv, b_qkv, w_out, b_out, ln2_g, ln2_b, w1, b1, w2, b2):
        import jax, jax.numpy as jnp
        import numpy as np
        N_HEAD = 16
        BUCKET = 64
        HIDDEN = 256
        EPS = 1e-05

        def _ln(x, g, b):
            m = x.mean(-1, keepdims=True)
            v = x.var(-1, keepdims=True)
            return (x - m) * jax.lax.rsqrt(v + EPS) * g + b
        B, T, C = x.shape
        nb = T // BUCKET
        hd = C // N_HEAD
        scale = 1.0 / np.sqrt(hd)
        h = _ln(x, ln1_g, ln1_b)
        qkv = h @ w_qkv + b_qkv
        q, k, v = jnp.split(qkv, 3, axis=-1)

        def buck(t):
            return t.reshape(B, nb, BUCKET, N_HEAD, hd)
        qb, kb, vb = (buck(q), buck(k), buck(v))
        kp = jnp.concatenate([jnp.zeros_like(kb[:, :1]), kb[:, :-1]], axis=1)
        vp = jnp.concatenate([jnp.zeros_like(vb[:, :1]), vb[:, :-1]], axis=1)
        kc = jnp.concatenate([kp, kb], axis=2)
        vc = jnp.concatenate([vp, vb], axis=2)
        scores = jnp.einsum('bnihd,bnjhd->bnhij', qb, kc) * scale
        i = jnp.arange(BUCKET)[:, None]
        j = jnp.arange(2 * BUCKET)[None, :]
        mask = (j < BUCKET) | (j - BUCKET <= i)
        scores = jnp.where(mask, scores, -jnp.inf)
        attn = jax.nn.softmax(scores, axis=-1)
        ob = jnp.einsum('bnhij,bnjhd->bnihd', attn, vc).reshape(B, T, C)
        x = x + ob @ w_out + b_out
        h2 = _ln(x, ln2_g, ln2_b)
        m = jax.nn.gelu(h2 @ w1 + b1, approximate=False) @ w2 + b2
        return x + m

    def _L0_xattn_ref(query, key, value, key_padding_mask, Wq, bq, Wk, bk, Wv, bv, Wo, bo):
        import jax, jax.numpy as jnp
        import numpy as np
        EMBED = 256
        HEADS = 16
        HD = EMBED // HEADS
        SCALE_BASE = 128
        OFFSET = 0

        def _dup_interleave(m):
            return jnp.repeat(m, 2, axis=-1)

        def _rotate_every_two(x):
            x1 = x[..., ::2]
            x2 = x[..., 1::2]
            return jnp.stack([-x2, x1], axis=-1).reshape(x.shape)

        def _xpos(x, offset, downscale):
            T = x.shape[2]
            half = HD // 2
            scale_vec = (jnp.arange(0, HD, 2, dtype=jnp.float32) + 0.4 * HD) / (1.4 * HD)
            min_pos = -(T + offset) // 2
            power = jnp.arange(min_pos, min_pos + T, dtype=jnp.float32) / SCALE_BASE
            scale = scale_vec[None, :] ** power[:, None]
            inv_freq = 1.0 / 10000.0 ** (jnp.arange(half, dtype=jnp.float32) / half)
            ang = jnp.arange(T, dtype=jnp.float32)[:, None] * inv_freq[None, :]
            sin, cos = (jnp.sin(ang), jnp.cos(ang))
            if downscale:
                scale = 1.0 / scale
            sin_s = _dup_interleave(sin * scale)
            cos_s = _dup_interleave(cos * scale)
            return x * cos_s + _rotate_every_two(x) * sin_s
        B, T, C = query.shape

        def split(x):
            return x.reshape(B, T, HEADS, HD).transpose(0, 2, 1, 3)
        q = split(query @ Wq + bq)
        k = split(key @ Wk + bk)
        v = split(value @ Wv + bv)
        k = _xpos(k, 0, True)
        q = _xpos(q, OFFSET, False)
        scores = jnp.einsum('bhtd,bhsd->bhts', q * HD ** (-0.5), k)
        scores = jnp.where(key_padding_mask[:, None, None, :], -jnp.inf, scores)
        probs = jax.nn.softmax(scores.astype(jnp.float32), axis=-1).astype(scores.dtype)
        out = jnp.einsum('bhts,bhsd->bhtd', probs, v)
        out = out.transpose(0, 2, 1, 3).reshape(B, T, C)
        return out @ Wo + bo

    def _L0_ffn_ref(X, norm1_w, norm2_w, wq, wk, wv, wo, router_w, sh_gate, sh_up, sh_down, e_gate, e_up, e_down):
        import jax, jax.numpy as jnp
        import numpy as np
        D_MODEL = 256
        N_HEADS = 16
        D_HEAD = D_MODEL // N_HEADS
        N_EXPERTS = 8
        TOP_K = 2
        D_FF = 512
        EPS = 1e-06

        def rmsnorm(x, w):
            return x * jax.lax.rsqrt(jnp.mean(x * x, axis=-1, keepdims=True) + EPS) * w

        def swiglu(x, w_gate, w_up, w_down):
            return jax.nn.silu(x @ w_gate) * (x @ w_up) @ w_down
        B, S, d = X.shape
        scale = 1.0 / jnp.sqrt(jnp.asarray(D_HEAD, X.dtype))
        h = rmsnorm(X, norm1_w)
        q = (h @ wq).reshape(B, S, N_HEADS, D_HEAD)
        k = (h @ wk).reshape(B, S, N_HEADS, D_HEAD)
        v = (h @ wv).reshape(B, S, N_HEADS, D_HEAD)
        scores = jnp.einsum('bshd,bthd->bhst', q, k) * scale
        attn = jax.nn.softmax(scores, axis=-1)
        ctx = jnp.einsum('bhst,bthd->bshd', attn, v).reshape(B, S, d)
        X = X + ctx @ wo
        h2 = rmsnorm(X, norm2_w).reshape(B * S, d)
        logits = h2 @ router_w
        probs = jax.nn.softmax(logits, axis=-1)
        topw, topi = jax.lax.top_k(probs, TOP_K)
        topw = jax.nn.softmax(topw, axis=-1)
        combine = jnp.sum(jax.nn.one_hot(topi, N_EXPERTS, dtype=h2.dtype) * topw[..., None], axis=1)
        shared = swiglu(h2, sh_gate, sh_up, sh_down)
        gate = jnp.einsum('td,edf->etf', h2, e_gate)
        up = jnp.einsum('td,edf->etf', h2, e_up)
        eout = jnp.einsum('etf,efd->etd', jax.nn.silu(gate) * up, e_down)
        spec = jnp.einsum('etd,te->td', eout, combine)
        moe_out = (shared + spec).reshape(B, S, d)
        return X + moe_out

    def _L1_attn_ref(x, WQ, WK, WV, WO, gamma, beta):
        import jax, jax.numpy as jnp
        import numpy as np
        EPS = 1e-05

        def xpos_rotate(x, offset=0, conjugate=False):
            b, s, h, dh = x.shape
            expoent = jnp.arange(0, dh, 2, dtype=jnp.float32) / dh
            angle = 10.0 ** (-4.0 * expoent)
            if conjugate:
                angle = -angle
            pos = jnp.arange(offset, s + offset, dtype=jnp.float32)
            nangle = pos[:, None] * angle[None, :]
            sin = jnp.sin(nangle)[None, :, None, :]
            cos = jnp.cos(nangle)[None, :, None, :]
            x0 = x[..., 0::2]
            x1 = x[..., 1::2]
            rot = jnp.stack([x0 * cos - x1 * sin, x0 * sin + x1 * cos], axis=-1)
            return rot.reshape(b, s, h, dh)

        def decay_mask(nseq, scale):
            idx = jnp.arange(nseq)
            diff = idx[:, None] - idx[None, :]
            mask = (diff >= 0).astype(scale.dtype)
            diff_c = jnp.maximum(diff, 0).astype(scale.dtype)
            logd = diff_c[None, :, :] * jnp.log(scale)[:, None, None]
            return jnp.exp(logd) * mask[None, :, :]

        def group_norm(R, gamma, beta, nheads):
            b, s, d = R.shape
            dh = d // nheads
            Rg = R.reshape(b, s, nheads, dh)
            mu = jnp.mean(Rg, axis=-1, keepdims=True)
            var = jnp.var(Rg, axis=-1, keepdims=True)
            Rn = (Rg - mu) * jax.lax.rsqrt(var + EPS)
            Rn = Rn * gamma.reshape(1, 1, nheads, dh) + beta.reshape(1, 1, nheads, dh)
            return Rn.reshape(b, s, d)
        b, s, d = x.shape
        h, dh, _ = WQ.shape
        Q = jnp.einsum('bsd,hud->bshu', x, WQ)
        K = jnp.einsum('bsd,hud->bshu', x, WK)
        V = jnp.einsum('bsd,hud->bshu', x, WV)
        Q = xpos_rotate(Q)
        K = xpos_rotate(K)
        QK = jnp.einsum('bihd,bjhd->bhij', Q, K)
        scale = 1.0 - 2.0 ** (-5.0 - jnp.arange(h, dtype=jnp.float32))
        D = decay_mask(s, scale)
        QKD = QK * D[None]
        R = jnp.einsum('bhij,bjhd->bihd', QKD, V)
        R = R.reshape(b, s, d)
        R = group_norm(R, gamma, beta, h)
        y = R @ WO
        return y

    def _L1_xattn_ref(query, key, value, Wq, bq, Wk, bk, Wv, bv, Wo, bo):
        import jax, jax.numpy as jnp
        import numpy as np
        D_MODEL = 256
        N_HEADS = 16
        D_K = D_MODEL // N_HEADS
        WINDOW = 64
        B, S = (1, 1024)
        b, s, _ = query.shape

        def proj(x, W, bias):
            return (x @ W.T + bias).reshape(b, s, N_HEADS, D_K).transpose(0, 2, 1, 3)
        q = proj(query, Wq, bq)
        k = proj(key, Wk, bk)
        v = proj(value, Wv, bv)
        scores = jnp.einsum('bhqd,bhkd->bhqk', q, k) / np.sqrt(D_K)
        i = jnp.arange(s)[:, None]
        j = jnp.arange(s)[None, :]
        keep = (jnp.abs(i - j) <= WINDOW) & (j <= i)
        scores = jnp.where(keep[None, None], scores, -jnp.inf)
        attn = jax.nn.softmax(scores, axis=-1)
        out = jnp.einsum('bhqk,bhkd->bhqd', attn, v)
        out = out.transpose(0, 2, 1, 3).reshape(b, s, D_MODEL)
        return out @ Wo.T + bo

    def _L1_ffn_ref(x, gate_w, gate_b, We1, be1, We2, be2, We3, be3, ws1, bs1, ws2, bs2, ws3, bs3):
        import jax, jax.numpy as jnp
        import numpy as np
        DIM = 256
        E = 16
        TOPK = 2
        G = 4
        TOPK_G = 2
        INTER = 128
        N_SHARED = 2
        ROUTE_SCALE = 1.0

        def _gate(xf, gate_w, gate_b):
            scores = xf @ gate_w.T
            scores = jax.nn.softmax(scores.astype(jnp.float32), axis=-1)
            orig = scores
            scores = scores + gate_b
            T = xf.shape[0]
            sg = scores.reshape(T, G, E // G)
            group_scores = jax.lax.top_k(sg, 2)[0].sum(-1)
            _, gidx = jax.lax.top_k(group_scores, TOPK_G)
            keep = jax.nn.one_hot(gidx, G).sum(axis=1) > 0
            sg = jnp.where(keep[:, :, None], sg, -jnp.inf)
            scores = sg.reshape(T, E)
            _, idx = jax.lax.top_k(scores, TOPK)
            weights = jnp.take_along_axis(orig, idx, axis=1)
            weights = (weights * ROUTE_SCALE).astype(xf.dtype)
            return (weights, idx)
        shape = x.shape
        xf = x.reshape(-1, DIM)
        weights, idx = _gate(xf, gate_w, gate_b)
        combine = (jax.nn.one_hot(idx, E, dtype=xf.dtype) * weights[..., None]).sum(1)
        h1 = jnp.einsum('td,edi->tei', xf, We1) + be1
        h3 = jnp.einsum('td,edi->tei', xf, We3) + be3
        h = jax.nn.silu(h1) * h3
        yo = jnp.einsum('tei,eid->ted', h, We2) + be2
        y = jnp.einsum('te,ted->td', combine, yo)
        z = jax.nn.silu(xf @ ws1 + bs1) * (xf @ ws3 + bs3) @ ws2 + bs2
        return (y + z).reshape(shape)
    x = x + _L0_attn_ref(_layernorm(x, axis=-1), L0_attn_ln1_g, L0_attn_ln1_b, L0_attn_w_qkv, L0_attn_b_qkv, L0_attn_w_out, L0_attn_b_out, L0_attn_ln2_g, L0_attn_ln2_b, L0_attn_w1, L0_attn_b1, L0_attn_w2, L0_attn_b2)
    x = x + _L0_xattn_ref(_layernorm(x, axis=-1), ctx_1024, ctx_1024, mask_BxS2_bf0, L0_xattn_Wq, L0_xattn_bq, L0_xattn_Wk, L0_xattn_bk, L0_xattn_Wv, L0_xattn_bv, L0_xattn_Wo, L0_xattn_bo)
    x = x + _L0_ffn_ref(_layernorm(x, axis=-1), L0_ffn_norm1_w, L0_ffn_norm2_w, L0_ffn_wq, L0_ffn_wk, L0_ffn_wv, L0_ffn_wo, L0_ffn_router_w, L0_ffn_sh_gate, L0_ffn_sh_up, L0_ffn_sh_down, L0_ffn_e_gate, L0_ffn_e_up, L0_ffn_e_down)
    x = x + _L1_attn_ref(_layernorm(x, axis=-1), L1_attn_WQ, L1_attn_WK, L1_attn_WV, L1_attn_WO, L1_attn_gamma, L1_attn_beta)
    x = x + _L1_xattn_ref(_layernorm(x, axis=-1), ctx_1024, ctx_1024, L1_xattn_Wq, L1_xattn_bq, L1_xattn_Wk, L1_xattn_bk, L1_xattn_Wv, L1_xattn_bv, L1_xattn_Wo, L1_xattn_bo)
    x = x + _L1_ffn_ref(_layernorm(x, axis=-1), L1_ffn_gate_w, L1_ffn_gate_b, L1_ffn_We1, L1_ffn_be1, L1_ffn_We2, L1_ffn_be2, L1_ffn_We3, L1_ffn_be3, L1_ffn_ws1, L1_ffn_bs1, L1_ffn_ws2, L1_ffn_bs2, L1_ffn_ws3, L1_ffn_bs3)
    return x

_drawn_inputs = setup_inputs


def setup_inputs(seed=0):
    import zlib

    import numpy as np

    out = dict(_drawn_inputs(seed))
    spreads = {'L0_attn_ln1_g': (1.0, 0.6),
     'L0_attn_ln1_b': (0.0, 0.8),
     'L0_attn_b_qkv': (0.0, 0.575),
     'L0_attn_b_out': (0.0, 0.1),
     'L0_attn_ln2_g': (1.0, 0.6),
     'L0_attn_ln2_b': (0.0, 0.8),
     'L0_attn_b1': (0.0, 0.359),
     'L0_attn_b2': (0.0, 0.1),
     'L0_xattn_bq': (0.0, 0.486),
     'L0_xattn_bk': (0.0, 0.769),
     'L0_xattn_bv': (0.0, 0.1),
     'L0_xattn_bo': (0.0, 0.1),
     'L0_ffn_norm1_w': (1.0, 0.6),
     'L0_ffn_norm2_w': (1.0, 0.6),
     'L1_attn_gamma': (1.0, 0.6),
     'L1_attn_beta': (0.0, 0.8),
     'L1_ffn_gate_b': (0.0, 0.8),
     'L1_ffn_be1': (0.0, 2.0),
     'L1_ffn_be2': (0.0, 2.0),
     'L1_ffn_be3': (0.0, 2.0),
     'L1_ffn_bs1': (0.0, 2.0),
     'L1_ffn_bs2': (0.0, 2.0),
     'L1_ffn_bs3': (0.0, 2.0)}
    factors = {'L0_attn_w_qkv': 8.0,
     'L0_attn_w_out': 3.966,
     'L0_ffn_wq': 8.0,
     'L0_ffn_wk': 8.0,
     'L0_ffn_wv': 4.504,
     'L0_ffn_wo': 4.614,
     'L0_ffn_router_w': 8.0,
     'L0_ffn_sh_gate': 5.514,
     'L0_ffn_sh_up': 5.305,
     'L0_ffn_sh_down': 5.119,
     'L0_ffn_e_gate': 7.661,
     'L0_ffn_e_up': 7.616,
     'L0_ffn_e_down': 7.68,
     'L1_xattn_bq': 64.0,
     'L1_xattn_bk': 64.0,
     'L1_xattn_bv': 64.0,
     'L1_xattn_bo': 64.0,
     'L1_xattn_Wq': 7.087,
     'L1_xattn_Wk': 7.096,
     'L1_xattn_Wv': 2.873,
     'L1_xattn_Wo': 2.805,
     'L1_ffn_gate_w': 5.016,
     'L1_ffn_We1': 8.0,
     'L1_ffn_We2': 6.116,
     'L1_ffn_We3': 7.809,
     'L1_ffn_ws1': 2.725,
     'L1_ffn_ws3': 2.677}
    for name, (base, spread) in spreads.items():
        noise = np.random.default_rng([zlib.crc32(name.encode()), seed]).standard_normal(out[name].shape)
        drawn = base * np.exp(spread * noise) if base else spread * noise
        out[name] = jnp.asarray(drawn.astype(out[name].dtype))
    for name, factor in factors.items():
        out[name] = (out[name] * factor).astype(out[name].dtype)
    return out
```

```python
import numpy as np
import concourse.bass as bass
from concourse import mybir
from contextlib import ExitStack

P = 128
D = 256
KC = D // P
NT = 16
H = 16
HD = D // H
HB = 4
NG = H // HB
VW = HD + 1
BIG = 1e30
FAR = 3e38

W_QKV, W_O = 0, KC * 3 * D
W_COLS = W_O + KC * D

ATT0, XATT0, ATT1, RET, XATT1 = range(5)
CROSS = (XATT0, XATT1)
ROTARY = (XATT0, RET)
TWO_NORMS = (ATT0, ATT1)
BRANCH = (ATT0, ATT1)
OUT_BIAS = (ATT0, XATT0, XATT1)
MLP, MOE0, MOE1 = range(3)

F_EXPERTS = {MLP: 2, MOE0: 9, MOE1: 18}
F_CHUNKS = {MLP: 4, MOE0: 4, MOE1: 1}
F_ROUTED = {MLP: 0, MOE0: 8, MOE1: 16}
GROUPS, GT = 4, 4
GN = GT * P

VEC = ["ln1_g", "ln1_b", "bq0", "bk0", "ln2_g", "ln2_b", "xbq", "xbk", "n1_w", "n2_w", "gamma",
       "beta", "ybq", "ybk"]
ROW = ["bv0", "bo0", "b2", "xbv", "xbo", "ybv", "ybo"]

C_ID, C_CAUSAL, C_BAND, C_HEAD, C_IOTA, C_CLAMP, C_ZKEYS = 0, 128, 256, 384, 388, 404, 405
C_ROT = 406
C_DECAY = C_ROT + 2 * 2 * 4 * P
C_COLS = C_DECAY + H * P


def f_cols(f):
    c, gates = F_CHUNKS[f], 1 if f == MLP else 2
    return gates * KC * c * P + c * D + (c * gates if f != MOE0 else 0)


def constants():
    c = np.zeros((P, C_COLS), np.float32)
    i = np.arange(P)
    c[:, C_ID:C_ID + P] = np.eye(P)
    c[:, C_CAUSAL:C_CAUSAL + P] = np.where(i[None] <= i[:, None], 0.0, -BIG)
    c[:, C_BAND:C_BAND + P] = np.where((i[None] <= i[:, None]) & (i[:, None] - i[None] <= 64), 0.0, -BIG)
    for j in range(HB):
        c[:, C_HEAD + j] = (i // HD) % HB == j
    c[:, C_IOTA:C_IOTA + 16] = np.arange(16)
    c[:, C_CLAMP] = np.where(i < 64, 0.0, FAR)
    c[:, C_ZKEYS] = np.where(i < 64, 64.0, 0.0)
    half = HD // 2
    pos = np.arange(P, dtype=np.float32)
    pair = (i % HD) // 2
    sign = np.where(i % 2 == 0, -1.0, 1.0).astype(np.float32)
    vec = (np.arange(0, HD, 2, dtype=np.float32) + np.float32(0.4 * HD)) / np.float32(1.4 * HD)
    power = (np.arange(-(P // 2), P - P // 2, dtype=np.float32)) / np.float32(128)
    scale = (vec[None] ** power[:, None]).astype(np.float32)
    inv = (1.0 / np.float32(10000.0) ** (np.arange(half, dtype=np.float32) / np.float32(half))).astype(np.float32)
    ang = pos[:, None] * inv[None]
    rot = c[:, C_ROT:C_DECAY].reshape(P, 2, 2, 4, P)
    for m, sc in ((0, scale), (1, scale), (2, 1 / scale), (3, 1 / scale)):
        rot[:, 0, 0, m] = (np.cos(ang) * sc).T[pair]
        rot[:, 0, 1, m] = (np.sin(ang) * sc).T[pair] * sign[:, None]
    angle = (np.float32(10.0) ** (np.float32(-4.0) * (np.arange(0, HD, 2, dtype=np.float32) / HD))).astype(np.float32)
    ang = pos[:, None] * angle[None]
    rot[:, 1, 0, :] = np.cos(ang).T[pair][:, None]
    rot[:, 1, 1, :] = (np.sin(ang).T[pair] * sign[:, None])[:, None]
    g = (1.0 - 2.0 ** (-5.0 - np.arange(H))).astype(np.float32)
    diff = i[None, :] - i[:, None]
    dec = np.exp(np.maximum(diff, 0)[:, None, :].astype(np.float32) * np.log(g)[None, :, None])
    c[:, C_DECAY:] = (dec * (diff >= 0)[:, None, :]).reshape(P, H * P)
    return c


class Tile:

    def __init__(self, l, t, p):
        self.l, self.t, self.p = l, t, p

    def back(self, d):
        if isinstance(self.t, int) and self.t < d:
            return Tile(self.l - 1, self.t - d + NT, (self.p + d) % 2) if self.l else None
        return Tile(self.l, self.t - d, (self.p + d) % 2)


SOME = {"var2": TWO_NORMS, "rstd2": TWO_NORMS, "v_norm": TWO_NORMS, "base_sb": (ATT0, XATT0, ATT1, XATT1),
        "swapped": ROTARY, "zmax_sb": (ATT0,), "zero_exp": (ATT0,), "pad_mask": (XATT0,), "pad_in": (XATT0,), "gn_var": (RET,),
        "gn_eps": (RET,), "gn_rstd": (RET,)}
PER_TILE = {"scores_out": (NG,) * 5, "p_sub": (NG, NG, NG, 0, NG), "probs": (NG, NG, NG, 0, NG),
            "pT_out": (NG, NG, NG, 0, NG), "pT_sb": (NG, NG, NG, 0, NG), "ret_sb": (0, 0, 0, NG, 0),
            "dve_ln": (2, 1, 1, 1, 1), "dve_sm": (2 * NG, NG, NG, 0, NG),
            "dve_o": (2, 1, 1, 4, 1), "pool_r": (2, 1, 2, 1, 1), "pool_m": (0, 3, 0, 3, 0)}


def increments(name, l):
    if name in PER_TILE:
        return PER_TILE[name][l]
    return int(l in SOME.get(name, range(5)))


def reached(name, tile, k=None):
    per = increments(name, tile.l)
    base = sum(increments(name, l) * NT for l in range(tile.l))
    return tile.t * per + (base + (per if k is None else k))


def build(nc, A):
    f32, bf16, u32, u8 = mybir.dt.float32, mybir.dt.bfloat16, mybir.dt.uint32, mybir.dt.uint8
    ALU, ACT, AX = mybir.AluOpType, mybir.ActivationFunctionType, mybir.AxisListType
    ctx = ExitStack()
    with ctx:
        def sb(name, shape, dt=f32):
            return ctx.enter_context(nc.sbuf_tensor(name, shape, dt))

        x_all = sb("x_all", [P, NT, D])
        r_all = sb("r_all", [P, NT, D])
        fT = sb("fT", [P, KC, NT * P])
        w_att = sb("w_att", [P, 5, W_COLS])
        w_ffn = sb("w_ffn", [P, 2, f_cols(MOE0)])
        const = sb("const", [P, C_COLS])
        vecs = sb("vecs", [P, len(VEC), KC])
        rows = sb("rows", [P, len(ROW), D])
        router = sb("router", [P, KC, 8 + 16])
        gate_b = sb("gate_b", [P, 16])
        be2 = sb("be2", [18, D])
        pad_u8 = sb("pad_u8", [P, NT, P], u8)
        id_bf = sb("id_bf", [P, P], bf16)
        mask_bf = sb("mask_bf", [P, 2, P], bf16)
        pad_bf = sb("pad_bf", [P, 2, P], bf16)
        half_neg = sb("half_neg", [P, H])
        stats = sb("stats", [P, 2, 6])
        mv = sb("mv", [P, 2, 2])
        rstd = sb("rstd", [P, 2, 2])
        eps_sum = sb("eps_sum", [P, 2, 1])
        u = sb("u", [P, 2, D])
        v = sb("v", [P, 2, D])
        hT = sb("hT", [P, 2, KC, P])
        ctxT = sb("ctxT", [P, 2, KC, P])
        qk = sb("qk", [P, 2, 2 * KC, P])
        qk_swap = sb("qk_swap", [P, 2 * KC, P])
        qk_cos = sb("qk_cos", [P, 2 * KC, P])
        km = sb("km", [P, 2, KC, HB, P])
        va = sb("va", [P, 2, H, VW])
        negmax = sb("negmax", [P, 2, H])
        zmax = sb("zmax", [P, 2, H])
        wide = sb("wide", [P, 2, 4 * GN])
        den = sb("den", [P, 2, H])
        gn = sb("gn", [P, 2, 3, H])
        gsq = sb("gsq", [P, D])
        o = sb("o", [P, 2, D])
        oT = sb("oT", [P, 2, KC, P])
        act_sb = sb("act_sb", [P, 2, GN])
        lg = sb("lg", [P, NT, 16])
        pr = sb("pr", [P, NT, 16])
        sc = sb("sc", [P, NT, 16])
        pairs = sb("pairs", [P, NT * 4, 6])
        top = sb("top", [P, NT, 8])
        grp = sb("grp", [P, NT, 8])
        idx = sb("idx", [P, NT, 8], u32)
        idx_f = sb("idx_f", [P, NT, 2])
        w12 = sb("w12", [P, NT, 4])
        hot = sb("hot", [P, NT, 16])
        comb = sb("comb", [P, NT, 18])
        comb_e = sb("comb_e", [P, 2, NT])
        red = sb("red", [P, NT])
        combT = sb("combT", [18, GT, P])
        probs = wide[:, 0, :].rearrange("p (g h k) -> p g h k", g=NG, h=HB)
        probsT = wide[:, 1, :].rearrange("p (g h k) -> p g h k", g=NG, h=HB)

        ps = ctx.enter_context(nc.psum_tensor("ps", [P, 8, 512], f32))
        B_O, B_T, B_QK, B_VY = 4, 5, 6, 7

        ident = const[:, C_ID:C_ID + P]
        head_mask = const[:, C_HEAD:C_HEAD + HB]
        iota = const[:, C_IOTA:C_IOTA + 16]

        def vec(name, c):
            return vecs[:, VEC.index(name), c:c + 1]

        def row(name):
            return rows[:, ROW.index(name), :]

        S = {}

        def sem(name):
            if name not in S:
                S[name] = ctx.enter_context(nc.semaphore(name))
            return S[name]

        for name in ("var1 rstd1 u_norm var2 rstd2 v_norm base_sb uT_out hT_sb qk_out v_out qk_sb swapped km_sb va_sb "
                     "scores_out p_sub probs pT_out pT_sb ret_sb pv_out zero_exp o_norm oT_out oT_sb y_out x_done "
                     "ctx_in0 ctx_in1 pad_mask pad_in gn_var gn_rstd zmax_sb gn_eps dve_ln dve_sm dve_o pool_r pool_m "
                     "n_sq n_var n_rstd n_norm n_base n_out n_sb fT_sb lg_out lg_sb dve_n pool_n "
                     "x_in0 x_in1 x_in2 x_in3 const_in late_in w_att0 w_att1 w_att2 w_att3 w_att4 w_ffn0 w_ffn1 setup passed gate gate_p gate_done comb_out comb_sb bias_out bias_done "
                     "gate_out up_out act_done hid_done down_out acc_done comb_e_sb act_gate stored").split():
            sem(name)

        def wait(eng, name, tile, k=None):
            if tile is not None:
                eng.wait_ge(S[name], reached(name, tile, k))

        def wait_apart(eng, *waits):
            for name, n in waits:
                eng.wait_ge(S[name], n)
            eng.sem_inc(S["passed"], 1)

        def n_reached(name, f, t, k=None):
            per = {"dve_n": 1}.get(name, 1)
            layers = {"n_base": (MLP, MOE0), "lg_out": (MOE0, MOE1), "lg_sb": (MOE0, MOE1)}.get(name, (MLP, MOE0, MOE1))
            return t * per + NT * per * sum(1 for g in layers if g < f) + (per if k is None else k)

        def pipeline(eng, layers, step):
            first, end = NT * layers[0], NT * (layers[-1] + 1)

            def written_out(a, b):
                for s in range(a, b):
                    step({d: Tile((s + d) // NT, (s + d) % NT, (s + d) % 2) for d in range(-1, 4) if first <= s + d < end})

            for l in layers:
                written_out(NT * l - 3 if l == layers[0] else NT * l, NT * l + 3)
                with eng.Fori(0, 5) as i:
                    for j in range(2):
                        step({d: Tile(l, i * 2 + (3 + j + d), (3 + j + d) % 2) for d in range(-1, 4)})
                written_out(NT * l + 13, NT * (l + 1))
            written_out(end, end + 1)

        def norm_pipeline(eng, step):
            for s in range(-1, 3):
                step({d: (s + d, (s + d) % 2) for d in (-1, 0, 1) if 0 <= s + d < NT})
            with eng.Fori(0, 6) as i:
                for j in range(2):
                    step({d: (i * 2 + (3 + j + d), (3 + j + d) % 2) for d in (-1, 0, 1)})
            for s in range(15, 17):
                step({d: (s + d, (s + d) % 2) for d in (-1, 0, 1) if 0 <= s + d < NT})

        def experts(eng, f, body):
            n = F_EXPERTS[f]
            body(0, 0)
            pairs_ = (n - 1) // 2
            if pairs_ > 1:
                with eng.Fori(0, pairs_) as i:
                    for j in range(2):
                        body(i * 2 + (1 + j), (1 + j) % 2)
            else:
                pairs_ = 0
            for e in range(1 + 2 * pairs_, n):
                body(e, e % 2)

        def before(f):
            return sum(F_EXPERTS[g] for g in range(f))

        def buffer(f, p):
            return (before(f) + p) % 2

        def weights_in(eng, f, e, p):
            b = buffer(f, p)
            if isinstance(e, int):
                eng.wait_ge(S["w_ffn%d" % b], 16 * ((before(f) + e - b) // 2 + 1))
            else:
                eng.wait_ge(S["w_ffn%d" % b], (e - p) * 8 + 16 * ((before(f) + p - b) // 2 + 1))

        def units(name, f, e, g, k):
            def per(fl):
                c = F_CHUNKS[fl]
                return {"gate_out": c, "up_out": 0 if fl == MLP else c, "act_done": c, "hid_done": 0 if fl == MLP else c,
                        "down_out": GT, "acc_done": GT}[name]
            base = sum(per(fl) * F_EXPERTS[fl] * GROUPS for fl in range(f))
            return e * (per(f) * GROUPS) + (base + per(f) * g + k)

        def tiles_of(l, t):
            return Tile(l, t, t % 2)

        def at_tile(t):
            return bass.ds(t, 1)

        def columns(t):
            return bass.ds(t * P, P)

        LAST = {MLP: ATT0, MOE0: ATT1, MOE1: XATT1}
        block = ctx.enter_context(nc.Block())

        @block.sync
        def _(sp):
            xv = A["x"].rearrange("s t d -> t s d")
            sp.dma_start(x_all[:, 0:GT, :], xv[:, 0:GT, :]).then_inc(S["x_in0"], 16)
            sp.dma_start(const[:, 0:C_ROT], A["const"][:, 0:C_ROT]).then_inc(S["const_in"], 16)
            sp.dma_start(vecs[:], A["vecs"].rearrange("p (v c) -> p v c", c=KC)).then_inc(S["const_in"], 16)
            sp.dma_start(rows[:], A["rows"].rearrange("a (r d) -> a r d", d=D).to_broadcast([P, len(ROW), D])).then_inc(S["const_in"], 16)
            sp.dma_start(w_att[:, ATT0, :], A["w_att"][ATT0]).then_inc(S["w_att0"], 16)
            for g in range(1, GROUPS):
                sp.dma_start(x_all[:, g * GT:(g + 1) * GT, :], xv[:, g * GT:(g + 1) * GT, :]).then_inc(S["x_in%d" % g], 16)
            sp.dma_start(const[:, C_ROT:C_COLS], A["const"][:, C_ROT:C_COLS]).then_inc(S["late_in"], 16)
            sp.dma_start(router[:], A["router"].rearrange("p (c e) -> p c e", c=KC)).then_inc(S["late_in"], 16)
            sp.dma_start(gate_b[:], A["gate_b"].to_broadcast([P, 16])).then_inc(S["late_in"], 16)
            sp.dma_start(be2[:], A["be2"]).then_inc(S["late_in"], 16)
            sp.dma_start(pad_u8[:], A["pad"].rearrange("(a s) k -> a s k", a=1).to_broadcast([P, NT, P])).then_inc(S["late_in"], 16)
            for l in range(1, 5):
                sp.dma_start(w_att[:, l, :], A["w_att"][l]).then_inc(S["w_att%d" % l], 16)

            def load_experts(f):
                def load(e, p):
                    if not isinstance(e, int) or before(f) + e >= 2:
                        if isinstance(e, int) and e < 2:
                            q = f - 1
                            sp.wait_ge(S["down_out"], units("down_out", q, F_EXPERTS[q] - 2 + e, GROUPS - 1, GT))
                        else:
                            sp.wait_ge(S["down_out"], units("down_out", f, e - 2, GROUPS - 1, GT))
                    src = A["w_f%d" % f]
                    src = src[e] if isinstance(e, int) else src[bass.ds(e, 1)].rearrange("a p n -> (a p) n")
                    sp.dma_start(w_ffn[:, buffer(f, p), 0:f_cols(f)], src).then_inc(S["w_ffn%d" % buffer(f, p)], 16)
                return load

            def load_ctx(layers):
                def step(at):
                    if 2 in at and at[2].l in CROSS:
                        wait(sp, "v_out", at[2].back(2))
                        src = A["ctxT"][at[2].t] if isinstance(at[2].t, int) else \
                            A["ctxT"][bass.ds(at[2].t, 1)].rearrange("a p n -> (a p) n")
                        sp.dma_start(ctxT[:, at[2].p].rearrange("p c k -> p (c k)"), src).then_inc(S["ctx_in%d" % at[2].p], 16)
                pipeline(sp, layers, step)

            experts(sp, MLP, load_experts(MLP))
            load_ctx((XATT0, ATT1))
            experts(sp, MOE0, load_experts(MOE0))
            load_ctx((RET, XATT1))
            experts(sp, MOE1, load_experts(MOE1))
            out = A["out"].rearrange("s t d -> t s d")
            for g in range(GROUPS):
                sp.wait_ge(S["acc_done"], units("acc_done", MOE1, F_EXPERTS[MOE1] - 1, g, GT))
                sp.dma_start(out[:, g * GT:(g + 1) * GT, :], x_all[:, g * GT:(g + 1) * GT, :]).then_inc(S["stored"], 16)
            sp.wait_ge(S["stored"], 16 * GROUPS)

        @block.gpsimd
        def _(pool):
            pool.wait_ge(S["const_in"], 48)
            for ins in (nc.gpsimd.memset(half_neg[:], -0.5), nc.gpsimd.memset(va[:], 1.0), nc.gpsimd.memset(grp[:], -FAR),
                        nc.gpsimd.memset(comb[:], 1.0), nc.gpsimd.tensor_copy(id_bf[:], ident),
                        nc.gpsimd.tensor_copy(mask_bf[:, 0], const[:, C_CAUSAL:C_CAUSAL + P]),
                        nc.gpsimd.tensor_copy(mask_bf[:, 1], const[:, C_BAND:C_BAND + P])):
                ins.then_inc(S["setup"], 1)
            pool.wait_ge(S["setup"], 7)

            def inverse_root(tile, which, p):
                var_, eps = ("var1", 1e-5) if which == 0 else ("var2", 1e-6 if tile.l == ATT1 else 1e-5)
                wait_apart(pool, (var_, reached(var_, tile)))
                nc.gpsimd.tensor_scalar(eps_sum[:, p], mv[:, p, 1:2], eps, None, ALU.add).then_inc(S["pool_r"], 1)
                wait(pool, "pool_r", tile, which + 1)
                nc.gpsimd.tensor_tensor(rstd[:, p, which:which + 1], eps_sum[:, p], half_neg[:, 0:1],
                                        ALU.pow).then_inc(S["rstd1" if which == 0 else "rstd2"], 1)

            def keys(tile):
                p = tile.p
                if tile.l in ROTARY:
                    r = const[:, C_ROT:C_DECAY].rearrange("p (l s m k) -> p l s m k", l=2, s=2, m=2 * KC)[:, ROTARY.index(tile.l)]
                    wait(pool, "qk_sb", tile)
                    nc.gpsimd.tensor_tensor(qk_cos[:], qk[:, p], r[:, 0], ALU.mult).then_inc(S["pool_m"], 1)
                    wait(pool, "swapped", tile)
                    nc.gpsimd.tensor_tensor(qk_swap[:], qk_swap[:], r[:, 1], ALU.mult).then_inc(S["pool_m"], 1)
                    wait(pool, "pool_m", tile, 2)
                    nc.gpsimd.tensor_tensor(qk[:, p], qk_cos[:], qk_swap[:], ALU.add).then_inc(S["pool_m"], 1)
                    wait_apart(pool, ("pool_m", reached("pool_m", tile, 3)))
                two = tile.back(2)
                wait_apart(pool, *[(n, reached(n, q)) for n, q in (("qk_sb", tile), ("scores_out", two)) if q is not None])
                src = qk[:, p, 0:KC] if tile.l == RET else qk[:, p, KC:2 * KC]
                for j in range(HB):
                    last = nc.gpsimd.tensor_scalar(km[:, p, :, j, :], src, head_mask[:, j:j + 1], None, ALU.mult)
                last.then_inc(S["km_sb"], 1)
                if tile.l == XATT0:
                    nc.gpsimd.tensor_copy(pad_bf[:, p:p + 1], pad_u8[:, at_tile(tile.t), :]).then_inc(S["pad_in"], 1)
                    wait_apart(pool, ("pad_in", reached("pad_in", tile)))
                    nc.gpsimd.tensor_scalar(pad_bf[:, p], pad_bf[:, p], -BIG, None, ALU.mult).then_inc(S["pad_mask"], 1)

            def base(tile):
                if tile.l == RET:
                    return
                t = at_tile(tile.t)
                wait_apart(pool, ("u_norm", reached("u_norm", tile)))
                dst = r_all if tile.l in BRANCH else x_all
                src = u[:, tile.p:tile.p + 1] if tile.l in BRANCH else x_all[:, t]
                if tile.l == ATT1:
                    nc.gpsimd.tensor_copy(dst[:, t], src).then_inc(S["base_sb"], 1)
                else:
                    b = {ATT0: "bo0", XATT0: "xbo", XATT1: "ybo"}[tile.l]
                    nc.gpsimd.tensor_tensor(dst[:, t], src, row(b).unsqueeze(1), ALU.add).then_inc(S["base_sb"], 1)

            def step(at):
                if -1 in at and at[-1].l == RET:
                    tile = at[-1]
                    wait_apart(pool, ("gn_var", reached("gn_var", tile)))
                    nc.gpsimd.tensor_scalar(gn[:, tile.p, 1], gn[:, tile.p, 0], 1.0 / HD, 1e-5, ALU.mult,
                                            ALU.add).then_inc(S["gn_eps"], 1)
                    wait(pool, "gn_eps", tile)
                    nc.gpsimd.tensor_tensor(gn[:, tile.p, 2], gn[:, tile.p, 1], half_neg[:], ALU.pow).then_inc(S["gn_rstd"], 1)
                if 3 in at:
                    inverse_root(at[3], 0, at[3].p)
                    base(at[3])
                    if at[3].l in TWO_NORMS:
                        inverse_root(at[3], 1, at[3].p)
                if 1 in at:
                    keys(at[1])

            def norm_stage(f):
                def step(at):
                    if 1 in at:
                        t, p = at[1]
                        wait_apart(pool, ("n_var", n_reached("n_var", f, t)))
                        per, eps = (1.0 / D, 1e-6) if f == MOE0 else (1.0, 1e-5)
                        nc.gpsimd.tensor_scalar(eps_sum[:, p], mv[:, p, 1:2], per, eps, ALU.mult,
                                                ALU.add).then_inc(S["pool_n"], 1)
                        pool.wait_ge(S["pool_n"], n_reached("pool_n", f, t))
                        nc.gpsimd.tensor_tensor(rstd[:, p, 0:1], eps_sum[:, p], half_neg[:, 0:1], ALU.pow).then_inc(S["n_rstd"], 1)
                    if 0 in at:
                        t, p = at[0]
                        tt = at_tile(t)
                        wait_apart(pool, ("n_sb", n_reached("n_sb", f, t)))
                        nc.gpsimd.tensor_copy(fT[:, :, columns(t)], hT[:, p]).then_inc(S["fT_sb"], 1)
                        if f == MLP:
                            nc.gpsimd.tensor_tensor(x_all[:, tt], x_all[:, tt], r_all[:, tt], ALU.add).then_inc(S["gate_p"], 1)
                            wait_apart(pool, ("gate_p", t + 1))
                            nc.gpsimd.tensor_tensor(x_all[:, tt], x_all[:, tt], row("b2").unsqueeze(1), ALU.add).then_inc(S["n_base"], 1)
                        if f == MOE0:
                            nc.gpsimd.tensor_tensor(x_all[:, tt], x_all[:, tt], r_all[:, tt], ALU.add).then_inc(S["n_base"], 1)
                wait(pool, "x_done", tiles_of(LAST[f], NT - 1))
                norm_pipeline(pool, step)

            pipeline(pool, (ATT0,), step)
            norm_stage(MLP)
            pool.wait_ge(S["late_in"], 80)
            pool.wait_ge(S["acc_done"], units("acc_done", MLP, F_EXPERTS[MLP] - 1, GROUPS - 1, GT))
            pipeline(pool, (XATT0, ATT1), step)
            norm_stage(MOE0)
            pool.wait_ge(S["acc_done"], units("acc_done", MOE0, F_EXPERTS[MOE0] - 1, GROUPS - 1, GT))
            pipeline(pool, (RET, XATT1), step)
            norm_stage(MOE1)

        @block.tensor
        def _(pe):
            mm, tr = nc.tensor.matmul, nc.tensor.transpose

            def scores(tile):
                p, last = tile.p, tile.back(1)
                mask = {ATT0: mask_bf[:, 0:1], XATT0: pad_bf[:, p:p + 1], XATT1: mask_bf[:, 1:2]}.get(tile.l)
                wait(pe, "km_sb", tile)
                if tile.l == XATT0:
                    wait(pe, "pad_mask", tile)
                stationary = KC if tile.l == RET else 0
                for g in range(NG):
                    if last is not None:
                        wait(pe, "ret_sb" if last.l == RET else "pT_sb", last, g + 1)
                    c, r = g // 2, 64 * (g % 2)
                    if mask is not None:
                        mm(ps[:, g, :].rearrange("p (h k) -> p h k", h=HB), id_bf[:], mask.to_broadcast([P, HB, P]),
                           start=True, stop=False)
                    mm(ps[:, g, :], qk[r:r + 64, p, stationary + c, :], km[r:r + 64, p, c].rearrange("p h k -> p (h k)"),
                       start=mask is None, stop=True).then_inc(S["scores_out"], 1)

            def turn_in(tile):
                wait(pe, "v_norm" if tile.l in TWO_NORMS else "u_norm", tile)
                wait(pe, "hT_sb", tile.back(1))
                wait(pe, "oT_sb", tile.back(4))
                src = v if tile.l in TWO_NORMS else u
                for c in range(KC):
                    last = tr(ps[:, B_T, c * P:(c + 1) * P], src[:, tile.p, c * P:(c + 1) * P], ident)
                last.then_inc(S["uT_out"], 1)

            def turn_out(tile, at):
                wait(pe, "o_norm", tile)
                if 2 not in at:
                    wait(pe, "hT_sb", last_of(tile))
                    wait(pe, "oT_sb", tile.back(1))
                for c in range(KC):
                    last = tr(ps[:, B_T, D + c * P:D + (c + 1) * P], o[:, tile.p, c * P:(c + 1) * P], ident)
                last.then_inc(S["oT_out"], 1)

            def last_of(tile):
                return tiles_of({ATT0: ATT0, XATT0: ATT1, ATT1: ATT1}.get(tile.l, XATT1), NT - 1)

            def project(tile):
                p = tile.p
                w = w_att[:, tile.l, W_QKV:W_O].rearrange("p (c n) -> p c n", c=KC)
                if isinstance(tile.t, int) and tile.t == 0:
                    pe.wait_ge(S["w_att%d" % tile.l], 16)
                wait(pe, "hT_sb", tile)
                if tile.l in CROSS:
                    pe.wait_ge(S["ctx_in%d" % p], (tile.t - p) * 8 + 16 + 16 * (NT // 2) * CROSS.index(tile.l))
                wait(pe, "qk_sb", tile.back(1))
                kv = ctxT if tile.l in CROSS else hT
                for m in range(2 * KC):
                    for c in range(KC):
                        src = hT if m < KC else kv
                        last = mm(ps[:, B_QK, m * P:(m + 1) * P], w[:, c, m * P:(m + 1) * P], src[:, p, c, :],
                                  start=(c == 0), stop=(c == KC - 1))
                last.then_inc(S["qk_out"], 1)
                wait(pe, "va_sb", tile.back(1))
                wait(pe, "x_done", tile.back(3))
                for c in range(KC):
                    last = mm(ps[:, B_VY, 0:D], kv[:, p, c, :], w[:, c, 2 * D:3 * D], start=(c == 0), stop=(c == KC - 1))
                last.then_inc(S["v_out"], 1)

            def out_project(tile, at):
                w = w_att[:, tile.l, W_O:W_COLS].rearrange("p (c n) -> p c n", c=KC)
                wait(pe, "oT_sb", tile)
                if 1 not in at:
                    wait(pe, "va_sb", last_of(tile))
                    wait(pe, "x_done", tile.back(1))
                for c in range(KC):
                    last = mm(ps[:, B_VY, D:2 * D], oT[:, tile.p, c, :], w[:, c, :], start=(c == 0), stop=(c == KC - 1))
                last.then_inc(S["y_out"], 1)

            def weigh_values(tile):
                p = tile.p

                def values(g):
                    wait(pe, "ret_sb" if tile.l == RET else "pT_sb", tile, g + 1)
                    for j in range(HB):
                        h = g * HB + j
                        last = mm(ps[:, B_O, h * VW:(h + 1) * VW], probsT[:, g, j, :], va[:, p, h, :], start=True, stop=True)
                    if g == NG - 1:
                        last.then_inc(S["pv_out"], 1)

                for g in range(NG):
                    if tile.l != RET:
                        wait(pe, "probs", tile, g + 1)
                        for j in range(HB):
                            last = tr(ps[:, g, j * P:(j + 1) * P], probs[:, g, j, :], ident)
                        last.then_inc(S["pT_out"], 1)
                    if g == 0:
                        wait(pe, "va_sb", tile)
                        wait(pe, "o_norm", tile.back(1))
                    if g:
                        values(g - 1)
                values(NG - 1)

            def step(at):
                if 0 in at:
                    scores(at[0])
                if 2 in at:
                    turn_in(at[2])
                if -1 in at:
                    turn_out(at[-1], at)
                if 1 in at:
                    project(at[1])
                if -1 in at:
                    out_project(at[-1], at)
                if 0 in at:
                    weigh_values(at[0])

            def norm_stage(f):
                def step(at):
                    if 0 in at:
                        t, p = at[0]
                        pe.wait_ge(S["n_norm"], n_reached("n_norm", f, t))
                        if not (isinstance(t, int) and t == 0):
                            pe.wait_ge(S["n_sb"], n_reached("n_sb", f, t - 1))
                        for c in range(KC):
                            last = tr(ps[:, B_T, c * P:(c + 1) * P], v[:, p, c * P:(c + 1) * P], ident)
                        last.then_inc(S["n_out"], 1)
                    if -1 in at and f != MLP:
                        t, p = at[-1]
                        w = router[:, :, 0:8] if f == MOE0 else router[:, :, 8:24]
                        pe.wait_ge(S["n_sb"], n_reached("n_sb", f, t))
                        if not (isinstance(t, int) and t == 0):
                            pe.wait_ge(S["lg_sb"], n_reached("lg_sb", f, t - 1))
                        for c in range(KC):
                            last = mm(ps[:, B_O, 0:F_ROUTED[f]], hT[:, p, c, :], w[:, c, :], start=(c == 0), stop=(c == KC - 1))
                        last.then_inc(S["lg_out"], 1)
                wait(pe, "x_done", tiles_of(LAST[f], NT - 1))
                norm_pipeline(pe, step)

            def expert_biases():
                pe.wait_ge(S["gate_done"], 2)
                for g in range(GROUPS):
                    if g:
                        pe.wait_ge(S["comb_sb"], g)
                    for j in range(GT):
                        last = tr(ps[0:18, B_T, j * P:(j + 1) * P], comb[:, g * GT + j, :], ident)
                    last.then_inc(S["comb_out"], 1)
                    pe.wait_ge(S["comb_sb"], g + 1)
                    if g:
                        pe.wait_ge(S["bias_done"], GT * g)
                    for j in range(GT):
                        last = mm(ps[:, B_QK + j // 2, (j % 2) * D:(j % 2 + 1) * D], combT[:, j, :], be2[:], start=True, stop=True)
                    last.then_inc(S["bias_out"], 1)

            def feed_forward(f):
                n = F_CHUNKS[f]
                ready = "act_done" if f == MLP else "hid_done"

                def up(e, p, g):
                    w = w_ffn[:, buffer(f, p), :]
                    if g == 0:
                        weights_in(pe, f, e, p)
                    for fc in range(n):
                        q = g * n + fc
                        for which, name, free in ((0, "gate_out", "act_done"), (1, "up_out", "hid_done"))[:1 if f == MLP else 2]:
                            before_two = units(free, f, e, g, fc + 1 - 2)
                            if not (isinstance(before_two, int) and before_two <= 0):
                                pe.wait_ge(S[free], before_two)
                            for c in range(KC):
                                at = (which * KC + c) * n * P + fc * P
                                last = mm(ps[:, 2 * which + q % 2, :], w[:, at:at + P], fT[:, c, g * GN:(g + 1) * GN],
                                          start=(c == 0), stop=(c == KC - 1))
                            last.then_inc(S[name], 1)

                def down(e, p, g):
                    w = w_ffn[:, buffer(f, p), :]
                    at = (1 if f == MLP else 2) * KC * n * P
                    hid = wide[:, g % 2, :].rearrange("p (c k) -> p c k", c=4)
                    pe.wait_ge(S[ready], units(ready, f, e, g, n))
                    for j in range(GT):
                        free = units("acc_done", f, e, g, j + 1 - GT)
                        if not (isinstance(free, int) and free <= 0):
                            pe.wait_ge(S["acc_done"], free)
                        for fc in range(n):
                            last = mm(ps[:, 4 + j, 0:D], hid[:, fc, j * P:(j + 1) * P], w[:, at + fc * D:at + (fc + 1) * D],
                                      start=(fc == 0), stop=(fc == n - 1))
                        last.then_inc(S["down_out"], 1)

                def body(e, p):
                    for g in range(GROUPS):
                        up(e, p, g)
                        if g:
                            down(e, p, g - 1)
                        elif not (isinstance(e, int) and e == 0):
                            down(e - 1, 1 - p, GROUPS - 1)

                pe.wait_ge(S["fT_sb"], NT * (f + 1))
                if f != MLP:
                    pe.wait_ge(S["lg_sb"], NT * f)
                if f == MOE1:
                    pe.wait_ge(S["bias_done"], NT)
                experts(pe, f, body)
                n_e = F_EXPERTS[f] - 1
                down(n_e, n_e % 2, GROUPS - 1)
                pe.wait_ge(S["acc_done"], units("acc_done", f, n_e, GROUPS - 1, GT))

            pe.wait_ge(S["const_in"], 48)
            pe.wait_ge(S["setup"], 7)
            pipeline(pe, (ATT0,), step)
            norm_stage(MLP)
            feed_forward(MLP)
            pe.wait_ge(S["late_in"], 80)
            pipeline(pe, (XATT0, ATT1), step)
            norm_stage(MOE0)
            feed_forward(MOE0)
            pipeline(pe, (RET, XATT1), step)
            norm_stage(MOE1)
            expert_biases()
            feed_forward(MOE1)

        @block.scalar
        def _(act):
            def copy(dst, src, scale=None, bias=None):
                if scale is None and bias is None:
                    return nc.scalar.activation(dst, src, ACT.Copy)
                return nc.scalar.activation(dst, src, ACT.Identity, scale=1.0 if scale is None else scale,
                                            bias=0.0 if bias is None else bias)

            def exp(tile, g):
                if tile.l != RET:
                    wait(act, "p_sub", tile, g + 1)
                    nc.scalar.activation(probs[:, g], probs[:, g], ACT.Exp, scale=HD ** -0.5).then_inc(S["probs"], 1)

            def exp_zero_keys(tile):
                if tile.l == ATT0:
                    wait(act, "zmax_sb", tile)
                    nc.scalar.activation(den[:, tile.p], zmax[:, tile.p], ACT.Exp, scale=HD ** -0.5).then_inc(S["zero_exp"], 1)

            def turn_in(tile):
                p = tile.p
                wait(act, "uT_out", tile)
                wait(act, "oT_out", tile.back(3))
                wait(act, "v_out", tile.back(2))
                gain, shift = {ATT0: ("ln1_g", "ln1_b"), ATT1: ("n1_w", None)}.get(tile.l, (None, None))
                if gain is None:
                    last = copy(hT[:, p].rearrange("p c k -> p (c k)"), ps[:, B_T, 0:D])
                else:
                    for c in range(KC):
                        last = copy(hT[:, p, c], ps[:, B_T, c * P:(c + 1) * P], vec(gain, c), shift and vec(shift, c))
                last.then_inc(S["hT_sb"], 1)

            def turn_out(tile):
                p = tile.p
                wait(act, "oT_out", tile)
                wait(act, "y_out", tile.back(2))
                if tile.l == RET:
                    for c in range(KC):
                        last = copy(oT[:, p, c], ps[:, B_T, D + c * P:D + (c + 1) * P], vec("gamma", c), vec("beta", c))
                else:
                    last = copy(oT[:, p].rearrange("p c k -> p (c k)"), ps[:, B_T, D:2 * D])
                last.then_inc(S["oT_sb"], 1)

            def queries_keys(tile):
                p = tile.p
                wait(act, "qk_out", tile)
                wait(act, "scores_out", tile.back(2))
                names = {ATT0: ("bq0", "bk0"), XATT0: ("xbq", "xbk"), XATT1: ("ybq", "ybk")}.get(tile.l)
                if names is None:
                    last = copy(qk[:, p].rearrange("p c k -> p (c k)"), ps[:, B_QK, :])
                else:
                    for m in range(2 * KC):
                        last = copy(qk[:, p, m], ps[:, B_QK, m * P:(m + 1) * P], None, vec(names[m // KC], m % KC))
                last.then_inc(S["qk_sb"], 1)

            def turned_probs(tile, g):
                if tile.l != RET:
                    last = tile.back(1)
                    wait(act, "pT_out", tile, g + 1)
                    if g == 0:
                        wait(act, "pv_out", last)
                    copy(probsT[:, g].rearrange("p h k -> p (h k)"), ps[:, g, :]).then_inc(S["pT_sb"], 1)

            def step(at):
                if 0 in at:
                    exp(at[0], 0)
                    exp(at[0], 1)
                if 2 in at:
                    turn_in(at[2])
                if -1 in at:
                    turn_out(at[-1])
                if 0 in at:
                    exp(at[0], 2)
                    exp(at[0], 3)
                    exp_zero_keys(at[0])
                if 1 in at:
                    queries_keys(at[1])
                if 0 in at:
                    for g in range(NG):
                        turned_probs(at[0], g)

            def norm_stage(f):
                def step(at):
                    if 0 in at:
                        t, p = at[0]
                        act.wait_ge(S["n_out"], n_reached("n_out", f, t))
                        if not isinstance(t, int) or t >= 2:
                            act.wait_ge(S["fT_sb"], n_reached("fT_sb", f, t - 2))
                            if f != MLP:
                                act.wait_ge(S["lg_out"], n_reached("lg_out", f, t - 2))
                        if f == MOE1:
                            last = copy(hT[:, p].rearrange("p c k -> p (c k)"), ps[:, B_T, 0:D])
                        else:
                            for c in range(KC):
                                last = copy(hT[:, p, c], ps[:, B_T, c * P:(c + 1) * P], vec("ln2_g" if f == MLP else "n2_w", c),
                                            vec("ln2_b", c) if f == MLP else None)
                        last.then_inc(S["n_sb"], 1)
                norm_pipeline(act, step)

            def gate(f):
                E = F_ROUTED[f]
                act.wait_ge(S["gate_p"], NT + (1 if f == MOE0 else 3))
                nc.scalar.activation(sc[:, :, 0:E], pr[:, :, 0:E], ACT.Exp).then_inc(S["act_gate"], 1)
                if f == MOE0:
                    act.wait_ge(S["gate_p"], NT + 2)
                    nc.scalar.activation(w12[:, :, 1:2], w12[:, :, 0:1], ACT.Exp).then_inc(S["act_gate"], 1)

            def feed_forward(f):
                n = F_CHUNKS[f]

                def body(e, p):
                    for g in range(GROUPS):
                        for fc in range(n):
                            q = g * n + fc
                            act.wait_ge(S["gate_out"], units("gate_out", f, e, g, fc + 1))
                            src = ps[:, q % 2, :]
                            b = KC * P * n + n * D if f == MLP else 2 * KC * P + D
                            bias = w_ffn[:, buffer(f, p), b + fc:b + fc + 1]
                            if f == MLP:
                                used = units("down_out", f, e, g, 0) - GT
                                if fc == 0 and not (isinstance(used, int) and used <= 0):
                                    act.wait_ge(S["down_out"], used)
                                nc.scalar.activation(wide[:, g % 2, fc * GN:(fc + 1) * GN], src, ACT.Gelu,
                                                     bias=bias).then_inc(S["act_done"], 1)
                            else:
                                used = units("hid_done", f, e, g, fc + 1 - 2)
                                if not (isinstance(used, int) and used <= 0):
                                    act.wait_ge(S["hid_done"], used)
                                nc.scalar.activation(act_sb[:, q % 2, :], src, ACT.Silu,
                                                     bias=bias if f == MOE1 else 0.0).then_inc(S["act_done"], 1)
                experts(act, f, body)
                act.wait_ge(S["acc_done"], units("acc_done", f, F_EXPERTS[f] - 1, GROUPS - 1, GT))

            act.wait_ge(S["const_in"], 48)
            pipeline(act, (ATT0,), step)
            norm_stage(MLP)
            feed_forward(MLP)
            pipeline(act, (XATT0, ATT1), step)
            norm_stage(MOE0)
            gate(MOE0)
            feed_forward(MOE0)
            pipeline(act, (RET, XATT1), step)
            norm_stage(MOE1)
            gate(MOE1)
            for g in range(GROUPS):
                act.wait_ge(S["comb_out"], g + 1)
                if g:
                    act.wait_ge(S["bias_out"], g)
                copy(combT[:].rearrange("p j k -> p (j k)"), ps[0:18, B_T, :]).then_inc(S["comb_sb"], 1)
            feed_forward(MOE1)

        @block.vector
        def _(dve):
            tt, ts, stt = nc.vector.tensor_tensor, nc.vector.tensor_scalar, nc.vector.scalar_tensor_tensor

            def moments(x, p, done, own, value):
                nc.vector.bn_stats(stats[:, p], x).then_inc(S[own], 1)
                wait_apart(dve, (own, value))
                nc.vector.bn_aggr(mv[:, p], stats[:, p]).then_inc(S[done], 1)

            def variance(tile):
                l, t = tile.l, tile.t
                if l == ATT0 and isinstance(t, int):
                    if t in (0, 4):
                        dve.wait_ge(S["x_in%d" % (t // 4)], 16)
                    if t == 5:
                        dve.wait_ge(S["x_in2"], 16)
                        dve.wait_ge(S["x_in3"], 16)
                if l in (ATT1, XATT1):
                    wait(dve, "x_done", Tile(l - 1, t, tile.p))
                moments(x_tile(t), tile.p, "var1", "dve_ln", reached("dve_ln", tile, 1))

            def x_tile(t):
                return x_all[:, t] if isinstance(t, int) else x_all[:, at_tile(t)].rearrange("p a d -> p (a d)")

            def r_tile(t):
                return r_all[:, t] if isinstance(t, int) else r_all[:, at_tile(t)].rearrange("p a d -> p (a d)")

            def normalise(tile):
                p, two = tile.p, tile.back(2)
                wait(dve, "rstd1", tile)
                if two is not None:
                    wait(dve, "uT_out", two)
                    if two.l != RET:
                        wait(dve, "base_sb", two)
                ts(u[:, p], x_tile(tile.t), mv[:, p, 0:1], rstd[:, p, 0:1], ALU.subtract, ALU.mult).then_inc(S["u_norm"], 1)

            def second_variance(tile):
                p = tile.p
                wait(dve, "u_norm", tile)
                if tile.l == ATT0:
                    moments(u[:, p], p, "var2", "dve_ln", reached("dve_ln", tile, 2))
                elif tile.l == ATT1:
                    nc.vector.tensor_tensor_reduce(v[:, p], u[:, p], u[:, p], 1.0 / D, 0.0, ALU.mult, ALU.add,
                                                   mv[:, p, 1:2]).then_inc(S["var2"], 1)

            def second_norm(tile):
                p = tile.p
                if tile.l in TWO_NORMS:
                    wait(dve, "rstd2", tile)
                    if tile.l == ATT0:
                        ts(v[:, p], u[:, p], mv[:, p, 0:1], rstd[:, p, 1:2], ALU.subtract, ALU.mult).then_inc(S["v_norm"], 1)
                    else:
                        ts(v[:, p], u[:, p], rstd[:, p, 1:2], None, ALU.mult).then_inc(S["v_norm"], 1)

            def shift(tile, g):
                p = tile.p
                bank = ps[:, g, :].rearrange("p (h k) -> p h k", h=HB)
                wait(dve, "scores_out", tile, g + 1)
                if tile.l == RET:
                    if g == 0:
                        wait(dve, "pv_out", tile.back(1))
                    tt(probsT[:, g], bank, const[:, C_DECAY + g * GN:C_DECAY + (g + 1) * GN].rearrange("p (h k) -> p h k", h=HB),
                       ALU.mult).then_inc(S["ret_sb"], 1)
                    return
                m = negmax[:, p, g * HB:(g + 1) * HB]
                k = 2 if tile.l == ATT0 else 1
                nc.vector.tensor_reduce(m, bank, AX.X, ALU.max, negate=True).then_inc(S["dve_sm"], 1)
                wait(dve, "dve_sm", tile, k * g + 1)
                if tile.l == ATT0:
                    ts(m, m, const[:, C_CLAMP:C_CLAMP + 1], None, ALU.min).then_inc(S["dve_sm"], 1)
                    wait(dve, "dve_sm", tile, k * g + 2)
                last = tile.back(1)
                if last is not None and last.l != RET:
                    wait(dve, "pT_out", last, g + 1)
                tt(probs[:, g], bank, m.unsqueeze(2).to_broadcast([P, HB, P]), ALU.add).then_inc(S["p_sub"], 1)

            def zero_keys(tile):
                if tile.l == ATT0:
                    wait(dve, "zero_exp", tile.back(2))
                    ts(zmax[:, tile.p], negmax[:, tile.p], 0.0, None, ALU.min).then_inc(S["zmax_sb"], 1)

            def values(tile):
                p = tile.p
                wait(dve, "v_out", tile)
                wait(dve, "y_out", tile.back(2))
                wait(dve, "pv_out", tile.back(2))
                dst = va[:, p, :, 0:HD]
                src = ps[:, B_VY, 0:D].rearrange("p (h d) -> p h d", h=H)
                b = {ATT0: "bv0", XATT0: "xbv", XATT1: "ybv"}.get(tile.l)
                if b is None:
                    nc.vector.tensor_copy(dst, src).then_inc(S["va_sb"], 1)
                else:
                    tt(dst, src, row(b).rearrange("p (h d) -> p h d", h=H), ALU.add).then_inc(S["va_sb"], 1)

            def swap(tile):
                if tile.l in ROTARY:
                    prev = tile.back(1)
                    free = [("pool_m", reached("pool_m", prev, 3))] if prev is not None and prev.l in ROTARY else []
                    wait_apart(dve, ("qk_sb", reached("qk_sb", tile)), *free)
                    nc.vector.stream_shuffle(qk_swap[:], qk[:, tile.p], [i ^ 1 for i in range(32)]).then_inc(S["swapped"], 1)

            def attended(tile):
                p = tile.p
                O = ps[:, B_O, 0:H * VW].rearrange("p (h d) -> p h d", h=H)
                oh = o[:, p].rearrange("p (h d) -> p h d", h=H)
                wait(dve, "pv_out", tile)
                wait(dve, "oT_out", tile.back(2))

                def link(ins, k):
                    ins.then_inc(S["dve_o"], 1)
                    wait(dve, "dve_o", tile, k)

                if tile.l == RET:
                    g = gn[:, p]
                    link(nc.vector.tensor_reduce(g[:, 0], O[:, :, 0:HD], AX.X, ALU.add), 1)
                    link(ts(g[:, 1], g[:, 0], -1.0 / HD, None, ALU.mult), 2)
                    link(tt(oh, O[:, :, 0:HD], g[:, 1].unsqueeze(2).to_broadcast([P, H, HD]), ALU.add), 3)
                    link(tt(gsq[:], o[:, p], o[:, p], ALU.mult), 4)
                    nc.vector.tensor_reduce(g[:, 0], gsq[:].rearrange("p (h d) -> p h d", h=H), AX.X,
                                            ALU.add).then_inc(S["gn_var"], 1)
                    return
                total, k = O[:, :, HD], 1
                if tile.l == ATT0:
                    wait(dve, "zero_exp", tile)
                    total = den[:, p]
                    link(stt(out=total, in0=total, scalar=const[:, C_ZKEYS:C_ZKEYS + 1], in1=O[:, :, HD], op0=ALU.mult,
                             op1=ALU.add), 1)
                    k = 2
                link(nc.vector.reciprocal(zmax[:, p] if tile.l == ATT0 else den[:, p], total), k)
                inv = zmax[:, p] if tile.l == ATT0 else den[:, p]
                tt(oh, O[:, :, 0:HD], inv.unsqueeze(2).to_broadcast([P, H, HD]), ALU.mult).then_inc(S["o_norm"], 1)

            def head_norm(tile):
                if tile.l == RET:
                    oh = o[:, tile.p].rearrange("p (h d) -> p h d", h=H)
                    wait(dve, "gn_rstd", tile)
                    tt(oh, oh, gn[:, tile.p, 2].unsqueeze(2).to_broadcast([P, H, HD]), ALU.mult).then_inc(S["o_norm"], 1)

            def residual(tile):
                dst = (r_tile if tile.l in BRANCH else x_tile)(tile.t)
                wait(dve, "y_out", tile)
                if tile.l != RET:
                    wait(dve, "base_sb", tile)
                tt(dst, ps[:, B_VY, D:2 * D], dst, ALU.add).then_inc(S["x_done"], 1)

            def step(at):
                if -1 in at:
                    attended(at[-1])
                if 3 in at:
                    variance(at[3])
                if 0 in at:
                    shift(at[0], 0)
                if -1 in at:
                    head_norm(at[-1])
                if 0 in at:
                    shift(at[0], 1)
                if 3 in at:
                    normalise(at[3])
                    if at[3].l in TWO_NORMS:
                        second_variance(at[3])
                if 0 in at:
                    shift(at[0], 2)
                    shift(at[0], 3)
                    zero_keys(at[0])
                if 3 in at:
                    second_norm(at[3])
                if 1 in at:
                    swap(at[1])
                    values(at[1])
                if -1 in at:
                    residual(at[-1])

            def norm_stage(f):
                def step(at):
                    src = x_tile if f == MOE1 else r_tile
                    if 1 in at:
                        t, p = at[1]
                        if f == MOE0:
                            if not isinstance(t, int) or t >= 2:
                                dve.wait_ge(S["n_out"], n_reached("n_out", f, t - 2))
                            tt(v[:, p], src(t), src(t), ALU.mult).then_inc(S["n_sq"], 1)
                            dve.wait_ge(S["n_sq"], t + 1)
                            nc.vector.tensor_reduce(mv[:, p, 1:2], v[:, p], AX.X, ALU.add).then_inc(S["n_var"], 1)
                        else:
                            moments(src(t), p, "n_var", "dve_n", (f // 2) * NT + t + 1)
                    if 0 in at:
                        t, p = at[0]
                        dve.wait_ge(S["n_rstd"], n_reached("n_rstd", f, t))
                        if not isinstance(t, int) or t >= 2:
                            dve.wait_ge(S["n_out"], n_reached("n_out", f, t - 2))
                        if f == MOE0:
                            ins = ts(v[:, p], src(t), rstd[:, p, 0:1], None, ALU.mult)
                        else:
                            ins = ts(v[:, p], src(t), mv[:, p, 0:1], rstd[:, p, 0:1], ALU.subtract, ALU.mult)
                        ins.then_inc(S["n_norm"], 1)
                    if -1 in at and f != MLP:
                        t, p = at[-1]
                        E = F_ROUTED[f]
                        dve.wait_ge(S["lg_out"], n_reached("lg_out", f, t))
                        dst = lg[:, t, 0:E] if isinstance(t, int) else lg[:, at_tile(t), 0:E].rearrange("p a e -> p (a e)")
                        nc.vector.tensor_copy(dst, ps[:, B_O, 0:E]).then_inc(S["lg_sb"], 1)
                wait(dve, "x_done", tiles_of(LAST[f], NT - 1))
                norm_pipeline(dve, step)

            chain = [0]

            def link(ins):
                ins.then_inc(S["gate"], 1)
                chain[0] += 1
                dve.wait_ge(S["gate"], chain[0])

            def over(a, n):
                return a.unsqueeze(2).to_broadcast([P, NT, n])

            def softmax(f):
                E = F_ROUTED[f]
                L, pe_, se = lg[:, :, 0:E], pr[:, :, 0:E], sc[:, :, 0:E]
                dve.wait_ge(S["lg_sb"], NT * f)
                link(nc.vector.tensor_reduce(red[:], L, AX.X, ALU.max))
                tt(pe_, L, over(red[:], E), ALU.subtract).then_inc(S["gate_p"], 1)
                dve.wait_ge(S["act_gate"], 1 if f == MOE0 else 3)
                link(nc.vector.tensor_reduce(red[:], se, AX.X, ALU.add))
                link(nc.vector.reciprocal(red[:], red[:]))
                link(tt(pe_, se, over(red[:], E), ALU.mult))

            def best(values_):
                for t in range(NT):
                    last = nc.vector.max(top[:, t], values_[:, t])
                link(last)
                for t in range(NT):
                    last = nc.vector.max_index(idx[:, t], top[:, t], values_[:, t])
                link(last)
                link(nc.vector.tensor_copy(idx_f[:], idx[:, :, 0:2]))

            def one_hot(dst, k, n):
                link(tt(dst, iota[:, 0:n].unsqueeze(1).to_broadcast([P, NT, n]), over(idx_f[:, :, k], n), ALU.is_equal))

            def gate_moe0():
                softmax(MOE0)
                best(pr[:, :, 0:8])
                tt(w12[:, :, 0], top[:, :, 1], top[:, :, 0], ALU.subtract).then_inc(S["gate_p"], 1)
                dve.wait_ge(S["act_gate"], 2)
                link(ts(w12[:, :, 2], w12[:, :, 1], 1.0, None, ALU.add))
                link(nc.vector.reciprocal(w12[:, :, 3], w12[:, :, 2]))
                link(tt(w12[:, :, 2], w12[:, :, 1], w12[:, :, 3], ALU.mult))
                h = hot[:, :, 0:8]
                one_hot(h, 0, 8)
                link(tt(comb[:, :, 0:8], h, over(w12[:, :, 3], 8), ALU.mult))
                one_hot(h, 1, 8)
                link(tt(h, h, over(w12[:, :, 2], 8), ALU.mult))
                tt(comb[:, :, 0:8], comb[:, :, 0:8], h, ALU.add).then_inc(S["gate_done"], 1)
                dve.wait_ge(S["gate_done"], 1)

            def gate_moe1():
                softmax(MOE1)
                link(tt(sc[:], pr[:], gate_b[:].unsqueeze(1).to_broadcast([P, NT, 16]), ALU.add))
                s4 = sc[:].rearrange("p t (g e) -> p (t g) e", g=4)
                tt(pairs[:, :, 0:3], s4[:, :, 0:3], s4[:, :, 1:4], ALU.add)
                tt(pairs[:, :, 3:5], s4[:, :, 0:2], s4[:, :, 2:4], ALU.add)
                link(tt(pairs[:, :, 5:6], s4[:, :, 0:1], s4[:, :, 3:4], ALU.add))
                link(nc.vector.tensor_reduce(grp[:, :, 0:4], pairs[:].rearrange("p (t g) e -> p t g e", g=4), AX.X, ALU.max))
                best(grp)
                keep = hot[:, :, 0:4]
                one_hot(keep, 0, 4)
                one_hot(hot[:, :, 4:8], 1, 4)
                link(tt(keep, keep, hot[:, :, 4:8], ALU.add))
                link(ts(keep, keep, -1.0, BIG, ALU.add, ALU.mult))
                k4 = keep.unsqueeze(3).to_broadcast([P, NT, 4, 4])
                link(tt(sc[:].rearrange("p t (g e) -> p t g e", g=4), sc[:].rearrange("p t (g e) -> p t g e", g=4), k4, ALU.add))
                best(sc)
                one_hot(hot[:], 0, 16)
                one_hot(sc[:], 1, 16)
                link(tt(hot[:], hot[:], sc[:], ALU.add))
                tt(comb[:, :, 0:16], hot[:], pr[:], ALU.mult).then_inc(S["gate_done"], 1)
                dve.wait_ge(S["gate_done"], 2)

            def expert_biases():
                for g in range(GROUPS):
                    dve.wait_ge(S["bias_out"], g + 1)
                    for j in range(GT):
                        x = x_all[:, g * GT + j]
                        tt(x, ps[:, B_QK + j // 2, (j % 2) * D:(j % 2 + 1) * D], x, ALU.add).then_inc(S["bias_done"], 1)
                dve.wait_ge(S["bias_done"], NT)

            def feed_forward(f):
                n = F_CHUNKS[f]

                def hidden(e, p, g):
                    for fc in range(n):
                        q = g * n + fc
                        dst = wide[:, g % 2, fc * GN:(fc + 1) * GN]
                        dve.wait_ge(S["up_out"], units("up_out", f, e, g, fc + 1))
                        dve.wait_ge(S["act_done"], units("act_done", f, e, g, fc + 1))
                        used = units("down_out", f, e, g, 0) - GT
                        if fc == 0 and not (isinstance(used, int) and used <= 0):
                            dve.wait_ge(S["down_out"], used)
                        if f == MOE0:
                            ins = tt(dst, ps[:, 2 + q % 2, :], act_sb[:, q % 2, :], ALU.mult)
                        else:
                            b = 2 * KC * P + D + 1
                            ins = stt(out=dst, in0=ps[:, 2 + q % 2, :], scalar=w_ffn[:, buffer(f, p), b:b + 1],
                                      in1=act_sb[:, q % 2, :], op0=ALU.add, op1=ALU.mult)
                        ins.then_inc(S["hid_done"], 1)

                def add(e, p, g):
                    for j in range(GT):
                        t = g * GT + j
                        dve.wait_ge(S["down_out"], units("down_out", f, e, g, j + 1))
                        if not (isinstance(e, int) and e == 0):
                            dve.wait_ge(S["acc_done"], units("acc_done", f, e - 1, g, j + 1))
                        y = ps[:, 4 + j, 0:D]
                        if f == MLP:
                            ins = tt(x_all[:, t], y, x_all[:, t], ALU.add)
                        else:
                            ins = stt(out=x_all[:, t], in0=y, scalar=comb_e[:, p, t:t + 1], in1=x_all[:, t], op0=ALU.mult, op1=ALU.add)
                        ins.then_inc(S["acc_done"], 1)

                def body(e, p):
                    if f != MLP:
                        src = comb[:, :, e:e + 1] if isinstance(e, int) else comb[:, :, bass.ds(e, 1)]
                        nc.vector.tensor_copy(comb_e[:, p].unsqueeze(2), src).then_inc(S["comb_e_sb"], 1)
                    for g in range(GROUPS):
                        if f != MLP:
                            hidden(e, p, g)
                        if g:
                            if g == 1 and f != MLP:
                                dve.wait_ge(S["comb_e_sb"], e + (before(f) - F_EXPERTS[MLP] + 1))
                            add(e, p, g - 1)
                        elif not (isinstance(e, int) and e == 0):
                            add(e - 1, 1 - p, GROUPS - 1)

                if f != MOE1:
                    dve.wait_ge(S["n_base"], NT * (f + 1))
                experts(dve, f, body)
                n_e = F_EXPERTS[f] - 1
                add(n_e, n_e % 2, GROUPS - 1)
                dve.wait_ge(S["acc_done"], units("acc_done", f, n_e, GROUPS - 1, GT))

            dve.wait_ge(S["const_in"], 48)
            dve.wait_ge(S["setup"], 7)
            pipeline(dve, (ATT0,), step)
            norm_stage(MLP)
            feed_forward(MLP)
            dve.wait_ge(S["late_in"], 80)
            pipeline(dve, (XATT0, ATT1), step)
            norm_stage(MOE0)
            gate_moe0()
            feed_forward(MOE0)
            pipeline(dve, (RET, XATT1), step)
            norm_stage(MOE1)
            gate_moe1()
            expert_biases()
            feed_forward(MOE1)


def kernel(**inputs):
    import concourse.bacc as _bacc
    from concourse.bass_utils import run_bass_kernel_spmd as _run

    a = {k: np.asarray(v) for k, v in inputs.items()}

    def chunked(w):
        return w.reshape(-1, P, w.shape[-1]).transpose(1, 0, 2).reshape(P, -1)

    def attention(q, k, v, o):
        return np.concatenate([chunked(np.concatenate([q, k, v], 1)), chunked(o)], 1)

    def heads_last(w):
        return w.reshape(D, D).T

    n = "L0_ffn_"
    w_att = np.stack([
        np.concatenate([chunked(a["L0_attn_w_qkv"]), chunked(a["L0_attn_w_out"])], 1),
        attention(a["L0_xattn_Wq"], a["L0_xattn_Wk"], a["L0_xattn_Wv"], a["L0_xattn_Wo"]),
        attention(a[n + "wq"], a[n + "wk"], a[n + "wv"], a[n + "wo"]),
        attention(heads_last(a["L1_attn_WQ"]), heads_last(a["L1_attn_WK"]), heads_last(a["L1_attn_WV"]), a["L1_attn_WO"]),
        attention(a["L1_xattn_Wq"].T, a["L1_xattn_Wk"].T, a["L1_xattn_Wv"].T, a["L1_xattn_Wo"].T)])
    w1, w2, b1 = a["L0_attn_w1"], a["L0_attn_w2"], a["L0_attn_b1"]
    w_mlp = np.stack([np.concatenate([chunked(w1[:, s]), chunked(w2[s]), b1[s].reshape(-1, P).T], 1)
                      for s in (slice(0, 512), slice(512, 1024))])
    w_moe0 = np.stack([np.concatenate([chunked(g), chunked(u), chunked(d)], 1) for g, u, d in
                       [(a[n + "e_gate"][e], a[n + "e_up"][e], a[n + "e_down"][e]) for e in range(8)]
                       + [(a[n + "sh_gate"], a[n + "sh_up"], a[n + "sh_down"])]])
    n = "L1_ffn_"
    halves = (slice(0, P), slice(P, 2 * P))
    w_moe1 = np.stack([np.concatenate([chunked(g), chunked(u), chunked(d), bg[:, None], bu[:, None]], 1) for g, u, d, bg, bu in
                       [(a[n + "We1"][e], a[n + "We3"][e], a[n + "We2"][e], a[n + "be1"][e], a[n + "be3"][e]) for e in range(16)]
                       + [(a[n + "ws1"][:, s], a[n + "ws3"][:, s], a[n + "ws2"][s], a[n + "bs1"][s], a[n + "bs3"][s]) for s in halves]])
    be2 = np.concatenate([a[n + "be2"], a[n + "bs2"][None], np.zeros((1, D), np.float32)])
    bq = a["L0_attn_b_qkv"]
    vectors = [a["L0_attn_ln1_g"], a["L0_attn_ln1_b"], bq[0:D], bq[D:2 * D], a["L0_attn_ln2_g"], a["L0_attn_ln2_b"],
               a["L0_xattn_bq"], a["L0_xattn_bk"], a["L0_ffn_norm1_w"], a["L0_ffn_norm2_w"], a["L1_attn_gamma"],
               a["L1_attn_beta"], a["L1_xattn_bq"], a["L1_xattn_bk"]]
    vecs = np.stack(vectors).reshape(len(VEC), KC, P).transpose(2, 0, 1).reshape(P, -1)
    rows = np.concatenate([bq[2 * D:], a["L0_attn_b_out"], a["L0_attn_b2"], a["L0_xattn_bv"], a["L0_xattn_bo"],
                           a["L1_xattn_bv"], a["L1_xattn_bo"]])[None]
    router = np.concatenate([a["L0_ffn_router_w"], a["L1_ffn_gate_w"].T], 1).reshape(KC, P, 24).transpose(1, 0, 2).reshape(P, -1)
    ctxT = a["ctx_1024"].transpose(0, 2, 1).reshape(NT, KC, P, P).transpose(0, 2, 1, 3).reshape(NT, P, KC * P)
    arrays = {"x": a["x"], "const": constants(), "vecs": vecs, "rows": rows, "router": router,
              "gate_b": a["L1_ffn_gate_b"][None], "be2": be2, "pad": a["mask_BxS2_bf0"], "w_att": w_att,
              "w_f0": w_mlp, "w_f1": w_moe0, "w_f2": w_moe1, "ctxT": ctxT}
    nc = _bacc.Bacc("TRN2", target_bir_lowering=False, num_devices=1)
    arrays = {"in_" + k: np.ascontiguousarray(v) for k, v in arrays.items()}
    A = {k[3:]: nc.dram_tensor(k, v.shape, mybir.dt.from_np(v.dtype), kind="ExternalInput").ap() for k, v in arrays.items()}
    A["out"] = nc.dram_tensor("out_0", (NT, P, D), mybir.dt.float32, kind="ExternalOutput").ap()
    build(nc, A)
    r = _run(nc, [arrays], core_ids=[0])
    return r.results[0]["out_0"]
```

```python
import numpy as np
import concourse.bass as bass
from concourse import mybir
from contextlib import ExitStack

P = 128
D = 256
KC = D // P
NT = 16
H = 16
HD = D // H
HB = 4
NG = H // HB
VW = 32
HC = P // HD
BIG = 1e30
FAR = 3e38

W_QKV, W_O = 0, KC * 3 * D
W_COLS = W_O + KC * D

ATT0, XATT0, ATT1, RET, XATT1 = range(5)
CROSS = (XATT0, XATT1)
ROTARY = (XATT0, RET)
TWO_NORMS = (ATT0, ATT1)
BRANCH = (ATT0, ATT1)
OUT_BIAS = (ATT0, XATT0, XATT1)
MLP, MOE0, MOE1 = range(3)

F_EXPERTS = {MLP: 2, MOE0: 9, MOE1: 18}
F_CHUNKS = {MLP: 4, MOE0: 4, MOE1: 1}
F_ROUTED = {MLP: 0, MOE0: 8, MOE1: 16}
GROUPS, GT = 4, 4
GN = GT * P

VEC = ["ln1_g", "ln1_b", "bq0", "bk0", "ln2_g", "ln2_b", "xbq", "xbk", "n1_w", "n2_w", "gamma",
       "beta", "ybq", "ybk"]
ROW = ["bv0", "bo0", "b2", "xbv", "xbo", "ybv", "ybo"]

C_ID, C_CAUSAL, C_BAND, C_HEAD, C_IOTA, C_CLAMP, C_ZKEYS = 0, 128, 256, 384, 392, 408, 409
C_ROT = 410
C_DECAY = C_ROT + 2 * 2 * 4 * P
C_COLS = C_DECAY + H * P


def f_cols(f):
    c, gates = F_CHUNKS[f], 1 if f == MLP else 2
    return gates * KC * c * P + c * D + (c * gates if f != MOE0 else 0)


def constants():
    c = np.zeros((P, C_COLS), np.float32)
    i = np.arange(P)
    c[:, C_ID:C_ID + P] = np.eye(P)
    c[:, C_CAUSAL:C_CAUSAL + P] = np.where(i[None] <= i[:, None], 0.0, -BIG)
    c[:, C_BAND:C_BAND + P] = np.where((i[None] <= i[:, None]) & (i[:, None] - i[None] <= 64), 0.0, -BIG)
    for j in range(HC):
        c[:, C_HEAD + j] = i // HD == j
    c[:, C_IOTA:C_IOTA + 16] = np.arange(16)
    c[:, C_CLAMP] = np.where(i < 64, 0.0, FAR)
    c[:, C_ZKEYS] = np.where(i < 64, 64.0, 0.0)
    half = HD // 2
    pos = np.arange(P, dtype=np.float32)
    pair = (i % HD) // 2
    sign = np.where(i % 2 == 0, -1.0, 1.0).astype(np.float32)
    vec = (np.arange(0, HD, 2, dtype=np.float32) + np.float32(0.4 * HD)) / np.float32(1.4 * HD)
    power = (np.arange(-(P // 2), P - P // 2, dtype=np.float32)) / np.float32(128)
    scale = (vec[None] ** power[:, None]).astype(np.float32)
    inv = (1.0 / np.float32(10000.0) ** (np.arange(half, dtype=np.float32) / np.float32(half))).astype(np.float32)
    ang = pos[:, None] * inv[None]
    rot = c[:, C_ROT:C_DECAY].reshape(P, 2, 2, 4, P)
    for m, sc in ((0, scale), (1, scale), (2, 1 / scale), (3, 1 / scale)):
        rot[:, 0, 0, m] = (np.cos(ang) * sc).T[pair]
        rot[:, 0, 1, m] = (np.sin(ang) * sc).T[pair] * sign[:, None]
    angle = (np.float32(10.0) ** (np.float32(-4.0) * (np.arange(0, HD, 2, dtype=np.float32) / HD))).astype(np.float32)
    ang = pos[:, None] * angle[None]
    rot[:, 1, 0, :] = np.cos(ang).T[pair][:, None]
    rot[:, 1, 1, :] = (np.sin(ang).T[pair] * sign[:, None])[:, None]
    g = (1.0 - 2.0 ** (-5.0 - np.arange(H))).astype(np.float32)
    diff = i[None, :] - i[:, None]
    dec = np.exp(np.maximum(diff, 0)[:, None, :].astype(np.float32) * np.log(g)[None, :, None])
    c[:, C_DECAY:] = (dec * (diff >= 0)[:, None, :]).reshape(P, H * P)
    return c


class Tile:

    def __init__(self, l, t, p):
        self.l, self.t, self.p = l, t, p

    def back(self, d):
        if isinstance(self.t, int) and self.t < d:
            return Tile(self.l - 1, self.t - d + NT, (self.p + d) % 2) if self.l else None
        return Tile(self.l, self.t - d, (self.p + d) % 2)


SOME = {"var2": TWO_NORMS, "rstd2": TWO_NORMS, "v_norm": TWO_NORMS, "base_sb": (ATT0, XATT0, ATT1, XATT1),
        "swapped": ROTARY, "zmax_sb": (ATT0,), "zero_exp": (ATT0,), "pad_mask": (XATT0,), "pad_in": (XATT0,), "gn_var": (RET,),
        "gn_eps": (RET,), "gn_rstd": (RET,)}
PER_TILE = {"scores_out": (NG,) * 5, "p_sub": (NG, NG, NG, 0, NG), "probs": (NG, NG, NG, 0, NG),
            "pT_out": (NG, NG, NG, 0, NG), "pT_sb": (NG, NG, NG, 0, NG), "ret_sb": (0, 0, 0, NG, 0),
            "dve_ln": (2, 1, 1, 1, 1), "dve_sm": (2 * NG, NG, NG, 0, NG),
            "dve_o": (2, 1, 1, 4, 1), "pool_r": (2, 1, 2, 1, 1), "pool_m": (0, 3, 0, 3, 0)}


def increments(name, l):
    if name in PER_TILE:
        return PER_TILE[name][l]
    return int(l in SOME.get(name, range(5)))


def reached(name, tile, k=None):
    per = increments(name, tile.l)
    base = sum(increments(name, l) * NT for l in range(tile.l))
    return tile.t * per + (base + (per if k is None else k))


def build(nc, A):
    f32, f32r, bf16, u32, u8 = mybir.dt.float32, mybir.dt.float32r, mybir.dt.bfloat16, mybir.dt.uint32, mybir.dt.uint8
    ALU, ACT, AX = mybir.AluOpType, mybir.ActivationFunctionType, mybir.AxisListType
    ctx = ExitStack()
    with ctx:
        def sb(name, shape, dt=f32):
            return ctx.enter_context(nc.sbuf_tensor(name, shape, dt))

        x_all = sb("x_all", [P, NT, D])
        const = sb("const", [P, C_COLS])
        vecs = sb("vecs", [P, len(VEC), KC])
        rows = sb("rows", [P, len(ROW), D])
        router = sb("router", [P, KC, 8 + 16])
        gate_b = sb("gate_b", [P, 16])
        be2 = sb("be2", [18, D])
        pad_u8 = sb("pad_u8", [P, NT, P], u8)
        id_bf = sb("id_bf", [P, P], bf16)
        mask_bf = sb("mask_bf", [P, 2, P], bf16)
        pad_bf = sb("pad_bf", [P, 2, P], bf16)
        half_neg = sb("half_neg", [P, H])
        stats = sb("stats", [P, 2, 6])
        mv = sb("mv", [P, 2, 2])
        rstd = sb("rstd", [P, 2, 2])
        eps_sum = sb("eps_sum", [P, 2, 1])
        v = sb("v", [P, 2, D])
        hT = sb("hT", [P, 2, KC, P])
        va = sb("va", [P, 2, H, VW])
        negmax = sb("negmax", [P, 2, H])
        zmax = sb("zmax", [P, 2, H])
        den = sb("den", [P, 2, H])
        gn = sb("gn", [P, 2, 3, H])
        gsq = sb("gsq", [P, D])
        sumT = sb("sumT", [P, 4 * P])
        fT_hi = sb("fT_hi", [P, NT, KC, P], f32r)
        w_hi = sb("w_hi", [P, 2, f_cols(MOE0)], f32r)
        w_lo = sb("w_lo", [P, 2, f_cols(MOE0)], f32r)
        f_bias = sb("f_bias", [P, 2, 4])
        act_sb = sb("act_sb", [P, 2, GN])
        lg = sb("lg", [P, NT, 16])
        pr = sb("pr", [P, NT, 16])
        sc = sb("sc", [P, NT, 16])
        pairs = sb("pairs", [P, NT * 4, 6])
        top = sb("top", [P, NT, 8])
        grp = sb("grp", [P, NT, 8])
        idx = sb("idx", [P, NT, 8], u32)
        idx_f = sb("idx_f", [P, NT, 2])
        w12 = sb("w12", [P, NT, 4])
        hot = sb("hot", [P, NT, 16])
        comb = sb("comb", [P, NT, 18])
        comb_e = sb("comb_e", [P, 2, NT])
        red = sb("red", [P, NT])
        w_odd = sb("w_odd", [P, W_COLS])
        with ExitStack() as shared:
            def at_attention(name, shape):
                return shared.enter_context(nc.sbuf_tensor(name, shape, f32))
            r_all = at_attention("r_all", [P, NT, D])
            w_even = at_attention("w_even", [P, W_COLS])
            o = at_attention("o", [P, 2, D])
            oT = at_attention("oT", [P, 2, KC, P])
            probs_all = at_attention("probs_all", [P, H * P])
            probsT_all = at_attention("probsT_all", [P, H * P])
            km = at_attention("km", [P, KC, HC, P])
            qk = at_attention("qk", [P, 2, 2 * KC, P])
            u = at_attention("u", [P, 2, D])
            ctxT = at_attention("ctxT", [P, 2, KC, P])
            qk_swap = at_attention("qk_swap", [P, 2 * KC, P])
            qk_cos = at_attention("qk_cos", [P, 2 * KC, P])
        fT_lo = sb("fT_lo", [P, NT, KC, P], f32r)
        w_raw = sb("w_raw", [P, f_cols(MOE0)])
        hid_hi = sb("hid_hi", [P, 2, 4, GN], f32r)
        hid_lo = sb("hid_lo", [P, 2, 4, GN], f32r)
        h_tmp = sb("h_tmp", [P, 2, GN])
        w_of = (w_even, w_odd)
        combT = sumT[0:18, :].rearrange("e (j k) -> e j k", j=GT)
        probs = probs_all[:].rearrange("p (g h k) -> p g h k", g=NG, h=HB)
        probsT = probsT_all[:].rearrange("p (g h k) -> p g h k", g=NG, h=HB)

        ps = ctx.enter_context(nc.psum_tensor("ps", [P, 8, 512], f32))
        B_O, B_T, B_QK, B_V = 4, 5, 6, 7

        ident = const[:, C_ID:C_ID + P]
        head_mask = const[:, C_HEAD:C_HEAD + HC]
        iota = const[:, C_IOTA:C_IOTA + 16]

        def vec(name, c):
            return vecs[:, VEC.index(name), c:c + 1]

        def row(name):
            return rows[:, ROW.index(name), :]

        S = {}

        def sem(name):
            if name not in S:
                S[name] = ctx.enter_context(nc.semaphore(name))
            return S[name]

        for name in ("var1 rstd1 u_norm var2 rstd2 v_norm base_sb uT_out hT_sb qk_out v_out qk_sb swapped km_sb va_sb "
                     "scores_out p_sub probs pT_out pT_sb ret_sb pv_out zero_exp o_norm oT_out oT_sb y_out x_done "
                     "sum_sb sum_out ctx_in0 ctx_in1 pad_mask pad_in gn_var gn_rstd zmax_sb gn_eps dve_ln dve_sm dve_o pool_r pool_m "
                     "n_sq n_var n_rstd n_norm n_base n_out n_sb fT_hi_sb fT_sb lg_out lg_sb dve_n pool_n "
                     "x_in0 x_in1 x_in2 x_in3 const_in late_in w_att0 w_att1 w_att2 w_att3 w_att4 w_raw_in f_bias_sb w_hi_sb w_lo_sb setup passed gate gate_p gate_done comb_out comb_sb bias_out bias_done "
                     "gate_out up_out act_done h_done hi_done hid_done down_out acc_done comb_e_sb act_gate stored").split():
            sem(name)

        def wait(eng, name, tile, k=None):
            if tile is not None:
                eng.wait_ge(S[name], reached(name, tile, k))

        def wait_apart(eng, *waits):
            for name, n in waits:
                eng.wait_ge(S[name], n)
            eng.sem_inc(S["passed"], 1)

        def n_reached(name, f, t, k=None):
            per = {"dve_n": 1}.get(name, 1)
            layers = {"n_base": (MLP, MOE0), "lg_out": (MOE0, MOE1), "lg_sb": (MOE0, MOE1)}.get(name, (MLP, MOE0, MOE1))
            return t * per + NT * per * sum(1 for g in layers if g < f) + (per if k is None else k)

        def pipeline(eng, layers, step):
            first, end = NT * layers[0], NT * (layers[-1] + 1)

            def written_out(a, b):
                for s in range(a, b):
                    step({d: Tile((s + d) // NT, (s + d) % NT, (s + d) % 2) for d in range(-1, 4) if first <= s + d < end})

            for l in layers:
                written_out(NT * l - 3 if l == layers[0] else NT * l, NT * l + 3)
                with eng.Fori(0, 5) as i:
                    for j in range(2):
                        step({d: Tile(l, i * 2 + (3 + j + d), (3 + j + d) % 2) for d in range(-1, 4)})
                written_out(NT * l + 13, NT * (l + 1))
            written_out(end, end + 1)

        def norm_pipeline(eng, step):
            for s in range(-1, 3):
                step({d: (s + d, (s + d) % 2) for d in (-1, 0, 1) if 0 <= s + d < NT})
            with eng.Fori(0, 6) as i:
                for j in range(2):
                    step({d: (i * 2 + (3 + j + d), (3 + j + d) % 2) for d in (-1, 0, 1)})
            for s in range(15, 17):
                step({d: (s + d, (s + d) % 2) for d in (-1, 0, 1) if 0 <= s + d < NT})

        def experts(eng, f, body):
            n = F_EXPERTS[f]
            body(0, 0)
            pairs_ = (n - 2) // 2
            if pairs_ > 1:
                with eng.Fori(0, pairs_) as i:
                    for j in range(2):
                        body(i * 2 + (1 + j), (1 + j) % 2)
            else:
                pairs_ = 0
            for e in range(1 + 2 * pairs_, n):
                body(e, e % 2)

        def before(f):
            return sum(F_EXPERTS[g] for g in range(f))

        def buffer(f, p):
            return (before(f) + p) % 2

        def weights_reached(f, e):
            return e + (before(f) + 1)

        def units(name, f, e, g, k):
            def per(fl):
                c = F_CHUNKS[fl]
                return {"gate_out": c, "up_out": 0 if fl == MLP else c, "act_done": c, "h_done": 0 if fl == MLP else c,
                        "hi_done": c, "hid_done": c,
                        "down_out": GT, "acc_done": GT}[name]
            base = sum(per(fl) * F_EXPERTS[fl] * GROUPS for fl in range(f))
            return e * (per(f) * GROUPS) + (base + per(f) * g + k)

        def tiles_of(l, t):
            return Tile(l, t, t % 2)

        def at_tile(t):
            return bass.ds(t, 1)

        LAST = {MLP: ATT0, MOE0: ATT1, MOE1: XATT1}
        block = ctx.enter_context(nc.Block())

        @block.sync
        def _(sp):
            def load_attention(l):
                sp.dma_start(w_of[l % 2][:], A["w_att"][l]).then_inc(S["w_att%d" % l], 16)

            xv = A["x"].rearrange("s t d -> t s d")
            sp.dma_start(x_all[:, 0:GT, :], xv[:, 0:GT, :]).then_inc(S["x_in0"], 16)
            sp.dma_start(const[:, 0:C_ROT], A["const"][:, 0:C_ROT]).then_inc(S["const_in"], 16)
            sp.dma_start(vecs[:], A["vecs"].rearrange("p (v c) -> p v c", c=KC)).then_inc(S["const_in"], 16)
            sp.dma_start(rows[:], A["rows"].rearrange("a (r d) -> a r d", d=D).to_broadcast([P, len(ROW), D])).then_inc(S["const_in"], 16)
            load_attention(ATT0)
            for g in range(1, GROUPS):
                sp.dma_start(x_all[:, g * GT:(g + 1) * GT, :], xv[:, g * GT:(g + 1) * GT, :]).then_inc(S["x_in%d" % g], 16)
            sp.dma_start(const[:, C_ROT:C_COLS], A["const"][:, C_ROT:C_COLS]).then_inc(S["late_in"], 16)
            sp.dma_start(router[:], A["router"].rearrange("p (c e) -> p c e", c=KC)).then_inc(S["late_in"], 16)
            sp.dma_start(gate_b[:], A["gate_b"].to_broadcast([P, 16])).then_inc(S["late_in"], 16)
            sp.dma_start(be2[:], A["be2"]).then_inc(S["late_in"], 16)
            sp.dma_start(pad_u8[:], A["pad"].rearrange("(a s) k -> a s k", a=1).to_broadcast([P, NT, P])).then_inc(S["late_in"], 16)
            load_attention(XATT0)

            def load_experts(f):
                def load(e, p):
                    if isinstance(e, int) and e == 0:
                        wait(sp, "x_done", tiles_of(LAST[f], NT - 1))
                    else:
                        sp.wait_ge(S["w_lo_sb"], weights_reached(f, e - 1))
                    src = A["w_f%d" % f]
                    src = src[e] if isinstance(e, int) else src[bass.ds(e, 1)].rearrange("a p n -> (a p) n")
                    sp.dma_start(w_raw[:, 0:f_cols(f)], src).then_inc(S["w_raw_in"], 16)
                experts(sp, f, load)
                sp.wait_ge(S["acc_done"], units("acc_done", f, F_EXPERTS[f] - 1, GROUPS - 1, GT))

            def load_ctx(layers):
                def step(at):
                    if 2 in at and at[2].l in CROSS:
                        wait(sp, "v_out", at[2].back(2))
                        src = A["ctxT"][at[2].t] if isinstance(at[2].t, int) else \
                            A["ctxT"][bass.ds(at[2].t, 1)].rearrange("a p n -> (a p) n")
                        sp.dma_start(ctxT[:, at[2].p].rearrange("p c k -> p (c k)"), src).then_inc(S["ctx_in%d" % at[2].p], 16)
                pipeline(sp, layers, step)

            load_experts(MLP)
            load_attention(ATT1)
            load_ctx((XATT0, ATT1))
            wait(sp, "x_done", tiles_of(XATT0, NT - 1))
            load_attention(RET)
            load_experts(MOE0)
            load_attention(XATT1)
            load_ctx((RET, XATT1))
            load_experts(MOE1)
            out = A["out"].rearrange("s t d -> t s d")
            for g in range(GROUPS):
                sp.dma_start(out[:, g * GT:(g + 1) * GT, :], x_all[:, g * GT:(g + 1) * GT, :]).then_inc(S["stored"], 16)
            sp.wait_ge(S["stored"], 16 * GROUPS)

        @block.gpsimd
        def _(pool):
            pool.wait_ge(S["const_in"], 48)
            for ins in (nc.gpsimd.memset(half_neg[:], -0.5), nc.gpsimd.memset(va[:], 1.0), nc.gpsimd.memset(grp[:], -FAR),
                        nc.gpsimd.memset(comb[:], 1.0), nc.gpsimd.tensor_copy(id_bf[:], ident),
                        nc.gpsimd.tensor_copy(mask_bf[:, 0], const[:, C_CAUSAL:C_CAUSAL + P]),
                        nc.gpsimd.tensor_copy(mask_bf[:, 1], const[:, C_BAND:C_BAND + P])):
                ins.then_inc(S["setup"], 1)
            pool.wait_ge(S["setup"], 7)

            def inverse_root(tile, which, p):
                var_, eps = ("var1", 1e-5) if which == 0 else ("var2", 1e-6 if tile.l == ATT1 else 1e-5)
                wait_apart(pool, (var_, reached(var_, tile)))
                nc.gpsimd.tensor_scalar(eps_sum[:, p], mv[:, p, 1:2], eps, None, ALU.add).then_inc(S["pool_r"], 1)
                wait(pool, "pool_r", tile, which + 1)
                nc.gpsimd.tensor_tensor(rstd[:, p, which:which + 1], eps_sum[:, p], half_neg[:, 0:1],
                                        ALU.pow).then_inc(S["rstd1" if which == 0 else "rstd2"], 1)

            def keys(tile):
                p = tile.p
                if tile.l in ROTARY:
                    r = const[:, C_ROT:C_DECAY].rearrange("p (l s m k) -> p l s m k", l=2, s=2, m=2 * KC)[:, ROTARY.index(tile.l)]
                    wait(pool, "qk_sb", tile)
                    nc.gpsimd.tensor_tensor(qk_cos[:], qk[:, p], r[:, 0], ALU.mult).then_inc(S["pool_m"], 1)
                    wait(pool, "swapped", tile)
                    nc.gpsimd.tensor_tensor(qk_swap[:], qk_swap[:], r[:, 1], ALU.mult).then_inc(S["pool_m"], 1)
                    wait(pool, "pool_m", tile, 2)
                    nc.gpsimd.tensor_tensor(qk[:, p], qk_cos[:], qk_swap[:], ALU.add).then_inc(S["pool_m"], 1)
                if tile.l == XATT0:
                    two = tile.back(2)
                    if two is not None:
                        wait_apart(pool, ("scores_out", reached("scores_out", two)))
                    nc.gpsimd.tensor_copy(pad_bf[:, p:p + 1], pad_u8[:, at_tile(tile.t), :]).then_inc(S["pad_in"], 1)
                    wait_apart(pool, ("pad_in", reached("pad_in", tile)))
                    nc.gpsimd.tensor_scalar(pad_bf[:, p], pad_bf[:, p], -BIG, None, ALU.mult).then_inc(S["pad_mask"], 1)

            def base(tile):
                if tile.l == RET:
                    return
                t = at_tile(tile.t)
                wait_apart(pool, ("u_norm", reached("u_norm", tile)))
                dst = r_all if tile.l in BRANCH else x_all
                src = u[:, tile.p:tile.p + 1] if tile.l in BRANCH else x_all[:, t]
                if tile.l == ATT1:
                    nc.gpsimd.tensor_copy(dst[:, t], src).then_inc(S["base_sb"], 1)
                else:
                    b = {ATT0: "bo0", XATT0: "xbo", XATT1: "ybo"}[tile.l]
                    nc.gpsimd.tensor_tensor(dst[:, t], src, row(b).unsqueeze(1), ALU.add).then_inc(S["base_sb"], 1)

            def step(at):
                if 1 in at:
                    keys(at[1])
                if -1 in at and at[-1].l == RET:
                    tile = at[-1]
                    wait_apart(pool, ("gn_var", reached("gn_var", tile)))
                    nc.gpsimd.tensor_scalar(gn[:, tile.p, 1], gn[:, tile.p, 0], 1.0 / HD, 1e-5, ALU.mult,
                                            ALU.add).then_inc(S["gn_eps"], 1)
                    wait(pool, "gn_eps", tile)
                    nc.gpsimd.tensor_tensor(gn[:, tile.p, 2], gn[:, tile.p, 1], half_neg[:], ALU.pow).then_inc(S["gn_rstd"], 1)
                if 3 in at:
                    inverse_root(at[3], 0, at[3].p)
                    if at[3].l in TWO_NORMS:
                        inverse_root(at[3], 1, at[3].p)
                    base(at[3])

            def norm_stage(f):
                def step(at):
                    if 1 in at:
                        t, p = at[1]
                        wait_apart(pool, ("n_var", n_reached("n_var", f, t)))
                        per, eps = (1.0 / D, 1e-6) if f == MOE0 else (1.0, 1e-5)
                        nc.gpsimd.tensor_scalar(eps_sum[:, p], mv[:, p, 1:2], per, eps, ALU.mult,
                                                ALU.add).then_inc(S["pool_n"], 1)
                        pool.wait_ge(S["pool_n"], n_reached("pool_n", f, t))
                        nc.gpsimd.tensor_tensor(rstd[:, p, 0:1], eps_sum[:, p], half_neg[:, 0:1], ALU.pow).then_inc(S["n_rstd"], 1)
                    if 0 in at:
                        t, p = at[0]
                        tt = at_tile(t)
                        wait_apart(pool, ("n_sb", n_reached("n_sb", f, t)))
                        nc.gpsimd.tensor_copy(fT_hi[:, tt], hT[:, p:p + 1]).then_inc(S["fT_hi_sb"], 1)
                        if f == MLP:
                            wait_apart(pool, ("gate_p", t + 1))
                            nc.gpsimd.tensor_tensor(x_all[:, tt], x_all[:, tt], row("b2").unsqueeze(1), ALU.add).then_inc(S["n_base"], 1)
                wait(pool, "x_done", tiles_of(LAST[f], NT - 1))
                norm_pipeline(pool, step)

            def split_weights(f):
                def body(e, p):
                    if isinstance(e, int) and e == F_EXPERTS[f] - 1:
                        return
                    b, n = buffer(f, 1 - p), f_cols(f)
                    pool.wait_ge(S["w_hi_sb"], weights_reached(f, e + 1))
                    nc.gpsimd.tensor_tensor(w_lo[:, b, 0:n], w_raw[:, 0:n], w_hi[:, b, 0:n].bitcast(f32),
                                            ALU.subtract).then_inc(S["w_lo_sb"], 1)
                experts(pool, f, body)

            pipeline(pool, (ATT0,), step)
            norm_stage(MLP)
            split_weights(MLP)
            pool.wait_ge(S["late_in"], 80)
            pool.wait_ge(S["acc_done"], units("acc_done", MLP, F_EXPERTS[MLP] - 1, GROUPS - 1, GT))
            pipeline(pool, (XATT0, ATT1), step)
            norm_stage(MOE0)
            split_weights(MOE0)
            pool.wait_ge(S["acc_done"], units("acc_done", MOE0, F_EXPERTS[MOE0] - 1, GROUPS - 1, GT))
            pipeline(pool, (RET, XATT1), step)
            norm_stage(MOE1)
            split_weights(MOE1)

        @block.tensor
        def _(pe):
            mm, tr = nc.tensor.matmul, nc.tensor.transpose

            def scores(tile, groups):
                p, last = tile.p, tile.back(1)
                mask = {ATT0: mask_bf[:, 0:1], XATT0: pad_bf[:, p:p + 1], XATT1: mask_bf[:, 1:2]}.get(tile.l)
                stationary = KC if tile.l == RET else 0
                for g in groups:
                    if g == 0:
                        wait(pe, "km_sb", tile)
                        if tile.l == XATT0:
                            wait(pe, "pad_mask", tile)
                    if last is not None:
                        wait(pe, "ret_sb" if last.l == RET else "pT_sb", last, g + 1)
                    c, j = g // 2, HB * (g % 2)
                    if mask is not None:
                        mm(ps[:, g, :].rearrange("p (h k) -> p h k", h=HB), id_bf[:], mask.to_broadcast([P, HB, P]),
                           start=True, stop=False)
                    mm(ps[:, g, :], qk[:, p, stationary + c, :], km[:, c, j:j + HB, :].rearrange("p h k -> p (h k)"),
                       start=mask is None, stop=True).then_inc(S["scores_out"], 1)

            def turn_in(tile):
                wait(pe, "v_norm" if tile.l in TWO_NORMS else "u_norm", tile)
                wait(pe, "hT_sb", tile.back(1))
                wait(pe, "oT_sb", tile.back(4))
                src = v if tile.l in TWO_NORMS else u
                for c in range(KC):
                    last = tr(ps[:, B_T, c * P:(c + 1) * P], src[:, tile.p, c * P:(c + 1) * P], ident)
                last.then_inc(S["uT_out"], 1)

            def turn_out(tile, at):
                wait(pe, "o_norm", tile)
                if 2 not in at:
                    wait(pe, "hT_sb", last_of(tile))
                    wait(pe, "oT_sb", tile.back(1))
                for c in range(KC):
                    last = tr(ps[:, B_T, D + c * P:D + (c + 1) * P], o[:, tile.p, c * P:(c + 1) * P], ident)
                last.then_inc(S["oT_out"], 1)

            def last_of(tile):
                return tiles_of({ATT0: ATT0, XATT0: ATT1, ATT1: ATT1}.get(tile.l, XATT1), NT - 1)

            def project(tile):
                p = tile.p
                w = w_of[tile.l % 2][:, W_QKV:W_O].rearrange("p (c n) -> p c n", c=KC)
                if isinstance(tile.t, int) and tile.t == 0:
                    pe.wait_ge(S["w_att%d" % tile.l], 16)
                wait(pe, "hT_sb", tile)
                if tile.l in CROSS:
                    pe.wait_ge(S["ctx_in%d" % p], (tile.t - p) * 8 + 16 + 16 * (NT // 2) * CROSS.index(tile.l))
                wait(pe, "qk_sb", tile.back(1))
                wait(pe, "x_done", tile.back(3))
                kv = ctxT if tile.l in CROSS else hT
                for m in range(2 * KC):
                    for c in range(KC):
                        src = hT if m < KC else kv
                        last = mm(ps[:, B_QK, m * P:(m + 1) * P], w[:, c, m * P:(m + 1) * P], src[:, p, c, :],
                                  start=(c == 0), stop=(c == KC - 1))
                last.then_inc(S["qk_out"], 1)
                wait(pe, "va_sb", tile.back(1))
                for c in range(KC):
                    last = mm(ps[:, B_V, 0:D], kv[:, p, c, :], w[:, c, 2 * D:3 * D], start=(c == 0), stop=(c == KC - 1))
                last.then_inc(S["v_out"], 1)

            def out_project(tile, at):
                w = w_of[tile.l % 2][:, W_O:W_COLS].rearrange("p (c n) -> p c n", c=KC)
                wait(pe, "oT_sb", tile)
                wait(pe, "qk_sb", at[1] if 1 in at else last_of(tile))
                if 1 not in at:
                    wait(pe, "x_done", tile.back(1))
                for c in range(KC):
                    last = mm(ps[:, B_QK, 0:D], oT[:, tile.p, c, :], w[:, c, :], start=(c == 0), stop=(c == KC - 1))
                last.then_inc(S["y_out"], 1)

            def turn_probs(tile, g):
                if tile.l != RET:
                    wait(pe, "probs", tile, g + 1)
                    for j in range(HB):
                        last = tr(ps[:, g, j * P:(j + 1) * P], probs[:, g, j, :], ident)
                    last.then_inc(S["pT_out"], 1)

            def weigh_values(tile, g):
                if g == 0:
                    wait(pe, "va_sb", tile)
                    wait(pe, "o_norm", tile.back(1))
                wait(pe, "ret_sb" if tile.l == RET else "pT_sb", tile, g + 1)
                for j in range(HB):
                    last = mm(ps[VW * j:VW * (j + 1), B_O, g * P:(g + 1) * P], va[:, tile.p, g * HB + j, :],
                              probsT[:, g, j, :], start=True, stop=True)
                if g == NG - 1:
                    last.then_inc(S["pv_out"], 1)

            def turn_sums(tile):
                wait(pe, "sum_sb", tile)
                for g in range(NG):
                    last = tr(ps[:, B_O, g * P:(g + 1) * P], sumT[:, g * P:(g + 1) * P], ident)
                last.then_inc(S["sum_out"], 1)

            def step(at):
                now, out = at.get(0), at.get(-1)
                if 1 in at:
                    project(at[1])
                if now:
                    scores(now, (0, 1))
                if out:
                    turn_sums(out)
                if now:
                    scores(now, (2, 3))
                if 2 in at:
                    turn_in(at[2])
                if out:
                    turn_out(out, at)
                if now:
                    turn_probs(now, 0)
                    turn_probs(now, 1)
                    weigh_values(now, 0)
                if out:
                    out_project(out, at)
                if now:
                    turn_probs(now, 2)
                    weigh_values(now, 1)
                    turn_probs(now, 3)
                    weigh_values(now, 2)
                    weigh_values(now, 3)

            def norm_stage(f):
                def step(at):
                    if 0 in at:
                        t, p = at[0]
                        pe.wait_ge(S["n_norm"], n_reached("n_norm", f, t))
                        if not (isinstance(t, int) and t == 0):
                            pe.wait_ge(S["n_sb"], n_reached("n_sb", f, t - 1))
                        for c in range(KC):
                            last = tr(ps[:, B_T, c * P:(c + 1) * P], v[:, p, c * P:(c + 1) * P], ident)
                        last.then_inc(S["n_out"], 1)
                    if -1 in at and f != MLP:
                        t, p = at[-1]
                        w = router[:, :, 0:8] if f == MOE0 else router[:, :, 8:24]
                        pe.wait_ge(S["n_sb"], n_reached("n_sb", f, t))
                        if not (isinstance(t, int) and t == 0):
                            pe.wait_ge(S["lg_sb"], n_reached("lg_sb", f, t - 1))
                        for c in range(KC):
                            last = mm(ps[:, B_O, 0:F_ROUTED[f]], hT[:, p, c, :], w[:, c, :], start=(c == 0), stop=(c == KC - 1))
                        last.then_inc(S["lg_out"], 1)
                wait(pe, "x_done", tiles_of(LAST[f], NT - 1))
                norm_pipeline(pe, step)

            def expert_biases():
                pe.wait_ge(S["gate_done"], 2)
                for g in range(GROUPS):
                    if g:
                        pe.wait_ge(S["comb_sb"], g)
                    for j in range(GT):
                        last = tr(ps[0:18, B_T, j * P:(j + 1) * P], comb[:, g * GT + j, :], ident)
                    last.then_inc(S["comb_out"], 1)
                    pe.wait_ge(S["comb_sb"], g + 1)
                    if g:
                        pe.wait_ge(S["bias_done"], GT * g)
                    for j in range(GT):
                        last = mm(ps[:, B_QK + j // 2, (j % 2) * D:(j % 2 + 1) * D], combT[:, j, :], be2[:], start=True, stop=True)
                    last.then_inc(S["bias_out"], 1)

            def feed_forward(f):
                n = F_CHUNKS[f]

                def three(out, parts, first, last):
                    for k, (a, b) in enumerate(parts):
                        ins = mm(out, a, b, start=first and k == 0, stop=last and k == 2)
                    return ins

                def up(e, p, g):
                    b = buffer(f, p)
                    if g == 0:
                        pe.wait_ge(S["w_lo_sb"], weights_reached(f, e))
                    for fc in range(n):
                        q = g * n + fc
                        for which, name, free in ((0, "gate_out", "act_done"), (1, "up_out", "h_done"))[:1 if f == MLP else 2]:
                            before_two = units(free, f, e, g, fc + 1 - 2)
                            if not (isinstance(before_two, int) and before_two <= 0):
                                pe.wait_ge(S[free], before_two)
                            for c in range(KC):
                                at = (which * KC + c) * n * P + fc * P
                                wh, wl = w_hi[:, b, at:at + P], w_lo[:, b, at:at + P]
                                xh, xl = fT_hi[:, g * GT:(g + 1) * GT, c, :], fT_lo[:, g * GT:(g + 1) * GT, c, :]
                                last = three(ps[:, 2 * which + q % 2, :].rearrange("p (t k) -> p t k", t=GT),
                                             ((wh, xh), (wh, xl), (wl, xh)), c == 0, c == KC - 1)
                            last.then_inc(S[name], 1)

                def down(e, p, g):
                    b = buffer(f, p)
                    at = (1 if f == MLP else 2) * KC * n * P
                    pe.wait_ge(S["hid_done"], units("hid_done", f, e, g, n))
                    for j in range(GT):
                        free = units("acc_done", f, e, g, j + 1 - GT)
                        if not (isinstance(free, int) and free <= 0):
                            pe.wait_ge(S["acc_done"], free)
                        for fc in range(n):
                            hh, hl = hid_hi[:, g % 2, fc, j * P:(j + 1) * P], hid_lo[:, g % 2, fc, j * P:(j + 1) * P]
                            wh, wl = w_hi[:, b, at + fc * D:at + (fc + 1) * D], w_lo[:, b, at + fc * D:at + (fc + 1) * D]
                            last = three(ps[:, 4 + j, 0:D], ((hh, wh), (hh, wl), (hl, wh)), fc == 0, fc == n - 1)
                        last.then_inc(S["down_out"], 1)

                def body(e, p):
                    for g in range(GROUPS):
                        up(e, p, g)
                        if g:
                            down(e, p, g - 1)
                        elif not (isinstance(e, int) and e == 0):
                            down(e - 1, 1 - p, GROUPS - 1)

                pe.wait_ge(S["fT_sb"], NT * (f + 1))
                if f != MLP:
                    pe.wait_ge(S["lg_sb"], NT * f)
                if f == MOE1:
                    pe.wait_ge(S["bias_done"], NT)
                experts(pe, f, body)
                n_e = F_EXPERTS[f] - 1
                down(n_e, n_e % 2, GROUPS - 1)
                pe.wait_ge(S["acc_done"], units("acc_done", f, n_e, GROUPS - 1, GT))

            pe.wait_ge(S["const_in"], 48)
            pe.wait_ge(S["setup"], 7)
            pipeline(pe, (ATT0,), step)
            norm_stage(MLP)
            feed_forward(MLP)
            pe.wait_ge(S["late_in"], 80)
            pipeline(pe, (XATT0, ATT1), step)
            norm_stage(MOE0)
            feed_forward(MOE0)
            pipeline(pe, (RET, XATT1), step)
            norm_stage(MOE1)
            expert_biases()
            feed_forward(MOE1)

        @block.scalar
        def _(act):
            def copy(dst, src, scale=None, bias=None):
                if scale is None and bias is None:
                    return nc.scalar.activation(dst, src, ACT.Copy)
                return nc.scalar.activation(dst, src, ACT.Identity, scale=1.0 if scale is None else scale,
                                            bias=0.0 if bias is None else bias)

            def exp(tile, g):
                if tile.l != RET:
                    wait(act, "p_sub", tile, g + 1)
                    nc.scalar.activation(probs[:, g], probs[:, g], ACT.Exp, scale=HD ** -0.5).then_inc(S["probs"], 1)

            def exp_zero_keys(tile):
                if tile.l == ATT0:
                    wait(act, "zmax_sb", tile)
                    nc.scalar.activation(den[:, tile.p], zmax[:, tile.p], ACT.Exp, scale=HD ** -0.5).then_inc(S["zero_exp"], 1)

            def turn_in(tile):
                p = tile.p
                wait(act, "uT_out", tile)
                wait(act, "oT_out", tile.back(3))
                wait(act, "v_out", tile.back(2))
                gain, shift = {ATT0: ("ln1_g", "ln1_b"), ATT1: ("n1_w", None)}.get(tile.l, (None, None))
                if gain is None:
                    last = copy(hT[:, p].rearrange("p c k -> p (c k)"), ps[:, B_T, 0:D])
                else:
                    for c in range(KC):
                        last = copy(hT[:, p, c], ps[:, B_T, c * P:(c + 1) * P], vec(gain, c), shift and vec(shift, c))
                last.then_inc(S["hT_sb"], 1)

            def turn_out(tile):
                p = tile.p
                wait(act, "oT_out", tile)
                wait(act, "y_out", tile.back(2))
                if tile.l == RET:
                    for c in range(KC):
                        last = copy(oT[:, p, c], ps[:, B_T, D + c * P:D + (c + 1) * P], vec("gamma", c), vec("beta", c))
                else:
                    last = copy(oT[:, p].rearrange("p c k -> p (c k)"), ps[:, B_T, D:2 * D])
                last.then_inc(S["oT_sb"], 1)

            def queries_keys(tile):
                p = tile.p
                wait(act, "qk_out", tile)
                wait(act, "scores_out", tile.back(2))
                wait(act, "km_sb", tile.back(2))
                names = {ATT0: ("bq0", "bk0"), XATT0: ("xbq", "xbk"), XATT1: ("ybq", "ybk")}.get(tile.l)
                if names is None:
                    last = copy(qk[:, p].rearrange("p c k -> p (c k)"), ps[:, B_QK, :])
                else:
                    for m in range(2 * KC):
                        last = copy(qk[:, p, m], ps[:, B_QK, m * P:(m + 1) * P], None, vec(names[m // KC], m % KC))
                last.then_inc(S["qk_sb"], 1)

            def turned_probs(tile, g):
                if tile.l != RET:
                    last = tile.back(1)
                    wait(act, "pT_out", tile, g + 1)
                    if g == 0:
                        wait(act, "pv_out", last)
                    copy(probsT[:, g].rearrange("p h k -> p (h k)"), ps[:, g, :]).then_inc(S["pT_sb"], 1)

            def weighed(tile):
                wait(act, "pv_out", tile)
                wait(act, "sum_out", tile.back(1))
                copy(sumT[:], ps[:, B_O, :]).then_inc(S["sum_sb"], 1)

            def step(at):
                now = at.get(0)
                if 1 in at:
                    queries_keys(at[1])
                if now:
                    exp(now, 0)
                    exp(now, 1)
                if 2 in at:
                    turn_in(at[2])
                if -1 in at:
                    turn_out(at[-1])
                if now:
                    exp(now, 2)
                    turned_probs(now, 0)
                    exp(now, 3)
                    turned_probs(now, 1)
                    exp_zero_keys(now)
                    turned_probs(now, 2)
                    turned_probs(now, 3)
                    weighed(now)

            def norm_stage(f):
                def step(at):
                    if 0 in at:
                        t, p = at[0]
                        act.wait_ge(S["n_out"], n_reached("n_out", f, t))
                        if not isinstance(t, int) or t >= 2:
                            act.wait_ge(S["fT_sb"], n_reached("fT_sb", f, t - 2))
                            if f != MLP:
                                act.wait_ge(S["lg_out"], n_reached("lg_out", f, t - 2))
                        if f == MOE1:
                            last = copy(hT[:, p].rearrange("p c k -> p (c k)"), ps[:, B_T, 0:D])
                        else:
                            for c in range(KC):
                                last = copy(hT[:, p, c], ps[:, B_T, c * P:(c + 1) * P], vec("ln2_g" if f == MLP else "n2_w", c),
                                            vec("ln2_b", c) if f == MLP else None)
                        last.then_inc(S["n_sb"], 1)
                norm_pipeline(act, step)
                high_weights(f, 0, 0, 0, 1)

            def gate(f):
                E = F_ROUTED[f]
                act.wait_ge(S["gate_p"], NT + (1 if f == MOE0 else 3))
                nc.scalar.activation(sc[:, :, 0:E], pr[:, :, 0:E], ACT.Exp).then_inc(S["act_gate"], 1)
                if f == MOE0:
                    act.wait_ge(S["gate_p"], NT + 2)
                    nc.scalar.activation(w12[:, :, 1:2], w12[:, :, 0:1], ACT.Exp).then_inc(S["act_gate"], 1)

            def high_weights(f, e, p, piece, pieces):
                b, n = buffer(f, p), f_cols(f)
                if piece == 0:
                    act.wait_ge(S["w_raw_in"], e * 16 + 16 * (before(f) + 1))
                    if not isinstance(e, int) or e >= 2:
                        act.wait_ge(S["down_out"], units("down_out", f, e - 2, GROUPS - 1, GT))
                    if f != MOE0:
                        k = F_CHUNKS[f] * (1 if f == MLP else 2)
                        copy(f_bias[:, b, 0:k], w_raw[:, n - k:n]).then_inc(S["f_bias_sb"], 1)
                step_ = n // pieces
                last = copy(w_hi[:, b, piece * step_:(piece + 1) * step_], w_raw[:, piece * step_:(piece + 1) * step_])
                if piece == pieces - 1:
                    last.then_inc(S["w_hi_sb"], 1)

            def feed_forward(f):
                n = F_CHUNKS[f]

                def body(e, p):
                    last_expert = isinstance(e, int) and e == F_EXPERTS[f] - 1
                    for g in range(GROUPS):
                        for fc in range(n):
                            q = g * n + fc
                            act.wait_ge(S["gate_out"], units("gate_out", f, e, g, fc + 1))
                            src = ps[:, q % 2, :]
                            bias = f_bias[:, buffer(f, p), fc:fc + 1]
                            free = "hid_done" if f == MLP else "h_done"
                            used = units(free, f, e, g, fc + 1 - 2)
                            if not (isinstance(used, int) and used <= 0):
                                act.wait_ge(S[free], used)
                            if f == MLP:
                                nc.scalar.activation(h_tmp[:, q % 2, :], src, ACT.Gelu, bias=bias).then_inc(S["act_done"], 1)
                                act.wait_ge(S["act_done"], units("act_done", f, e, g, fc + 1))
                            else:
                                nc.scalar.activation(act_sb[:, q % 2, :], src, ACT.Silu,
                                                     bias=bias if f == MOE1 else 0.0).then_inc(S["act_done"], 1)
                                act.wait_ge(S["h_done"], units("h_done", f, e, g, fc + 1))
                            used = units("down_out", f, e, g, 0) - GT
                            if fc == 0 and not (isinstance(used, int) and used <= 0):
                                act.wait_ge(S["down_out"], used)
                            copy(hid_hi[:, g % 2, fc], h_tmp[:, q % 2, :]).then_inc(S["hi_done"], 1)
                        if g in (1, 2) and not last_expert:
                            high_weights(f, e + 1, 1 - p, g - 1, 2)
                if f != MOE0:
                    act.wait_ge(S["f_bias_sb"], 1 if f == MLP else F_EXPERTS[MLP] + 1)
                experts(act, f, body)
                act.wait_ge(S["acc_done"], units("acc_done", f, F_EXPERTS[f] - 1, GROUPS - 1, GT))

            act.wait_ge(S["const_in"], 48)
            pipeline(act, (ATT0,), step)
            norm_stage(MLP)
            feed_forward(MLP)
            pipeline(act, (XATT0, ATT1), step)
            norm_stage(MOE0)
            gate(MOE0)
            feed_forward(MOE0)
            pipeline(act, (RET, XATT1), step)
            norm_stage(MOE1)
            gate(MOE1)
            for g in range(GROUPS):
                act.wait_ge(S["comb_out"], g + 1)
                if g:
                    act.wait_ge(S["bias_out"], g)
                copy(combT.rearrange("p j k -> p (j k)"), ps[0:18, B_T, :]).then_inc(S["comb_sb"], 1)
            feed_forward(MOE1)

        @block.vector
        def _(dve):
            tt, ts, stt = nc.vector.tensor_tensor, nc.vector.tensor_scalar, nc.vector.scalar_tensor_tensor

            def moments(x, p, done, own, value):
                nc.vector.bn_stats(stats[:, p], x).then_inc(S[own], 1)
                wait_apart(dve, (own, value))
                nc.vector.bn_aggr(mv[:, p], stats[:, p]).then_inc(S[done], 1)

            def variance(tile):
                l, t = tile.l, tile.t
                if l == ATT0 and isinstance(t, int):
                    if t in (0, 4):
                        dve.wait_ge(S["x_in%d" % (t // 4)], 16)
                    if t == 5:
                        dve.wait_ge(S["x_in2"], 16)
                        dve.wait_ge(S["x_in3"], 16)
                if l in (ATT1, XATT1):
                    wait(dve, "x_done", Tile(l - 1, t, tile.p))
                moments(x_tile(t), tile.p, "var1", "dve_ln", reached("dve_ln", tile, 1))

            def x_tile(t):
                return x_all[:, t] if isinstance(t, int) else x_all[:, at_tile(t)].rearrange("p a d -> p (a d)")

            def r_tile(t):
                return r_all[:, t] if isinstance(t, int) else r_all[:, at_tile(t)].rearrange("p a d -> p (a d)")

            def normalise(tile):
                p, two = tile.p, tile.back(2)
                wait(dve, "rstd1", tile)
                if two is not None:
                    wait(dve, "uT_out", two)
                    if two.l != RET:
                        wait(dve, "base_sb", two)
                ts(u[:, p], x_tile(tile.t), mv[:, p, 0:1], rstd[:, p, 0:1], ALU.subtract, ALU.mult).then_inc(S["u_norm"], 1)

            def second_variance(tile):
                p = tile.p
                wait(dve, "u_norm", tile)
                if tile.l == ATT0:
                    moments(u[:, p], p, "var2", "dve_ln", reached("dve_ln", tile, 2))
                elif tile.l == ATT1:
                    nc.vector.tensor_tensor_reduce(v[:, p], u[:, p], u[:, p], 1.0 / D, 0.0, ALU.mult, ALU.add,
                                                   mv[:, p, 1:2]).then_inc(S["var2"], 1)

            def second_norm(tile):
                p = tile.p
                if tile.l in TWO_NORMS:
                    wait(dve, "rstd2", tile)
                    if tile.l == ATT0:
                        ts(v[:, p], u[:, p], mv[:, p, 0:1], rstd[:, p, 1:2], ALU.subtract, ALU.mult).then_inc(S["v_norm"], 1)
                    else:
                        ts(v[:, p], u[:, p], rstd[:, p, 1:2], None, ALU.mult).then_inc(S["v_norm"], 1)

            def shift(tile, g):
                p = tile.p
                bank = ps[:, g, :].rearrange("p (h k) -> p h k", h=HB)
                wait(dve, "scores_out", tile, g + 1)
                if tile.l == RET:
                    if g == 0:
                        wait(dve, "pv_out", tile.back(1))
                    tt(probsT[:, g], bank, const[:, C_DECAY + g * GN:C_DECAY + (g + 1) * GN].rearrange("p (h k) -> p h k", h=HB),
                       ALU.mult).then_inc(S["ret_sb"], 1)
                    return
                m = negmax[:, p, g * HB:(g + 1) * HB]
                k = 2 if tile.l == ATT0 else 1
                nc.vector.tensor_reduce(m, bank, AX.X, ALU.max, negate=True).then_inc(S["dve_sm"], 1)
                wait(dve, "dve_sm", tile, k * g + 1)
                if tile.l == ATT0:
                    ts(m, m, const[:, C_CLAMP:C_CLAMP + 1], None, ALU.min).then_inc(S["dve_sm"], 1)
                    wait(dve, "dve_sm", tile, k * g + 2)
                last = tile.back(1)
                if last is not None and last.l != RET:
                    wait(dve, "pT_out", last, g + 1)
                tt(probs[:, g], bank, m.unsqueeze(2).to_broadcast([P, HB, P]), ALU.add).then_inc(S["p_sub"], 1)

            def zero_keys(tile):
                if tile.l == ATT0:
                    wait(dve, "zero_exp", tile.back(2))
                    ts(zmax[:, tile.p], negmax[:, tile.p], 0.0, None, ALU.min).then_inc(S["zmax_sb"], 1)

            def values(tile):
                p = tile.p
                wait(dve, "v_out", tile)
                wait(dve, "pv_out", tile.back(2))
                dst = va[:, p, :, 0:HD]
                src = ps[:, B_V, 0:D].rearrange("p (h d) -> p h d", h=H)
                b = {ATT0: "bv0", XATT0: "xbv", XATT1: "ybv"}.get(tile.l)
                if b is None:
                    nc.vector.tensor_copy(dst, src).then_inc(S["va_sb"], 1)
                else:
                    tt(dst, src, row(b).rearrange("p (h d) -> p h d", h=H), ALU.add).then_inc(S["va_sb"], 1)

            def swap(tile):
                if tile.l in ROTARY:
                    prev = tile.back(1)
                    free = [("pool_m", reached("pool_m", prev, 3))] if prev is not None and prev.l in ROTARY else []
                    wait_apart(dve, ("qk_sb", reached("qk_sb", tile)), *free)
                    nc.vector.stream_shuffle(qk_swap[:], qk[:, tile.p], [i ^ 1 for i in range(32)]).then_inc(S["swapped"], 1)

            def keys(tile):
                if tile.l in ROTARY:
                    wait(dve, "pool_m", tile, 3)
                wait(dve, "qk_sb", tile)
                wait(dve, "scores_out", tile.back(1))
                src = qk[:, tile.p, 0:KC] if tile.l == RET else qk[:, tile.p, KC:2 * KC]
                for j in range(HC):
                    last = ts(km[:, :, j, :], src, head_mask[:, j:j + 1], None, ALU.mult)
                last.then_inc(S["km_sb"], 1)

            def attended(tile):
                p = tile.p
                O = ps[:, B_O, 0:H * VW].rearrange("p (h d) -> p h d", h=H)
                oh = o[:, p].rearrange("p (h d) -> p h d", h=H)
                wait(dve, "sum_out", tile)
                wait(dve, "oT_out", tile.back(2))

                def link(ins, k):
                    ins.then_inc(S["dve_o"], 1)
                    wait(dve, "dve_o", tile, k)

                if tile.l == RET:
                    g = gn[:, p]
                    link(nc.vector.tensor_reduce(g[:, 0], O[:, :, 0:HD], AX.X, ALU.add), 1)
                    link(ts(g[:, 1], g[:, 0], -1.0 / HD, None, ALU.mult), 2)
                    link(tt(oh, O[:, :, 0:HD], g[:, 1].unsqueeze(2).to_broadcast([P, H, HD]), ALU.add), 3)
                    link(tt(gsq[:], o[:, p], o[:, p], ALU.mult), 4)
                    nc.vector.tensor_reduce(g[:, 0], gsq[:].rearrange("p (h d) -> p h d", h=H), AX.X,
                                            ALU.add).then_inc(S["gn_var"], 1)
                    return
                total, k = O[:, :, HD], 1
                if tile.l == ATT0:
                    wait(dve, "zero_exp", tile)
                    total = den[:, p]
                    link(stt(out=total, in0=total, scalar=const[:, C_ZKEYS:C_ZKEYS + 1], in1=O[:, :, HD], op0=ALU.mult,
                             op1=ALU.add), 1)
                    k = 2
                link(nc.vector.reciprocal(zmax[:, p] if tile.l == ATT0 else den[:, p], total), k)
                inv = zmax[:, p] if tile.l == ATT0 else den[:, p]
                tt(oh, O[:, :, 0:HD], inv.unsqueeze(2).to_broadcast([P, H, HD]), ALU.mult).then_inc(S["o_norm"], 1)

            def head_norm(tile):
                if tile.l == RET:
                    oh = o[:, tile.p].rearrange("p (h d) -> p h d", h=H)
                    wait(dve, "gn_rstd", tile)
                    tt(oh, oh, gn[:, tile.p, 2].unsqueeze(2).to_broadcast([P, H, HD]), ALU.mult).then_inc(S["o_norm"], 1)

            def residual(tile):
                dst = (r_tile if tile.l in BRANCH else x_tile)(tile.t)
                wait(dve, "y_out", tile)
                if tile.l != RET:
                    wait(dve, "base_sb", tile)
                tt(dst, ps[:, B_QK, 0:D], dst, ALU.add).then_inc(S["x_done"], 1)

            def step(at):
                now, out = at.get(0), at.get(-1)
                if 1 in at:
                    swap(at[1])
                if now:
                    shift(now, 0)
                    shift(now, 1)
                if out:
                    attended(out)
                if now:
                    shift(now, 2)
                if out:
                    head_norm(out)
                if now:
                    shift(now, 3)
                    zero_keys(now)
                if 1 in at:
                    values(at[1])
                if 3 in at:
                    variance(at[3])
                if out:
                    residual(out)
                if 3 in at:
                    normalise(at[3])
                    if at[3].l in TWO_NORMS:
                        second_variance(at[3])
                if 1 in at:
                    keys(at[1])
                if 3 in at:
                    second_norm(at[3])

            def norm_stage(f):
                def step(at):
                    src = x_tile if f == MOE1 else r_tile
                    if 1 in at:
                        t, p = at[1]
                        if f == MOE0:
                            if not isinstance(t, int) or t >= 2:
                                dve.wait_ge(S["n_out"], n_reached("n_out", f, t - 2))
                            tt(v[:, p], src(t), src(t), ALU.mult).then_inc(S["n_sq"], 1)
                            dve.wait_ge(S["n_sq"], t + 1)
                            nc.vector.tensor_reduce(mv[:, p, 1:2], v[:, p], AX.X, ALU.add).then_inc(S["n_var"], 1)
                        else:
                            moments(src(t), p, "n_var", "dve_n", (f // 2) * NT + t + 1)
                    if 0 in at:
                        t, p = at[0]
                        dve.wait_ge(S["n_rstd"], n_reached("n_rstd", f, t))
                        if not isinstance(t, int) or t >= 2:
                            dve.wait_ge(S["n_out"], n_reached("n_out", f, t - 2))
                        if f == MOE0:
                            ins = ts(v[:, p], src(t), rstd[:, p, 0:1], None, ALU.mult)
                        else:
                            ins = ts(v[:, p], src(t), mv[:, p, 0:1], rstd[:, p, 0:1], ALU.subtract, ALU.mult)
                        ins.then_inc(S["n_norm"], 1)
                        if f != MOE1:
                            tt(x_tile(t), x_tile(t), src(t), ALU.add).then_inc(S["gate_p" if f == MLP else "n_base"], 1)
                    if -1 in at:
                        t, p = at[-1]
                        dve.wait_ge(S["fT_hi_sb"], n_reached("fT_hi_sb", f, t))
                        if f != MOE1:
                            dve.wait_ge(S["gate_p" if f == MLP else "n_base"], t + 1 if f == MLP else n_reached("n_base", f, t))
                        one = (lambda a: a[:, t]) if isinstance(t, int) else \
                            (lambda a: a[:, at_tile(t)].rearrange("p a c k -> p (a c) k"))
                        tt(one(fT_lo), hT[:, p], one(fT_hi).bitcast(f32), ALU.subtract).then_inc(S["fT_sb"], 1)
                    if -1 in at and f != MLP:
                        E = F_ROUTED[f]
                        dve.wait_ge(S["lg_out"], n_reached("lg_out", f, t))
                        dst = lg[:, t, 0:E] if isinstance(t, int) else lg[:, at_tile(t), 0:E].rearrange("p a e -> p (a e)")
                        nc.vector.tensor_copy(dst, ps[:, B_O, 0:E]).then_inc(S["lg_sb"], 1)
                wait(dve, "x_done", tiles_of(LAST[f], NT - 1))
                norm_pipeline(dve, step)
                b, n = buffer(f, 0), f_cols(f)
                dve.wait_ge(S["w_hi_sb"], weights_reached(f, 0))
                tt(w_lo[:, b, 0:n], w_raw[:, 0:n], w_hi[:, b, 0:n].bitcast(f32), ALU.subtract).then_inc(S["w_lo_sb"], 1)

            chain = [0]

            def link(ins):
                ins.then_inc(S["gate"], 1)
                chain[0] += 1
                dve.wait_ge(S["gate"], chain[0])

            def over(a, n):
                return a.unsqueeze(2).to_broadcast([P, NT, n])

            def softmax(f):
                E = F_ROUTED[f]
                L, pe_, se = lg[:, :, 0:E], pr[:, :, 0:E], sc[:, :, 0:E]
                dve.wait_ge(S["lg_sb"], NT * f)
                link(nc.vector.tensor_reduce(red[:], L, AX.X, ALU.max))
                tt(pe_, L, over(red[:], E), ALU.subtract).then_inc(S["gate_p"], 1)
                dve.wait_ge(S["act_gate"], 1 if f == MOE0 else 3)
                link(nc.vector.tensor_reduce(red[:], se, AX.X, ALU.add))
                link(nc.vector.reciprocal(red[:], red[:]))
                link(tt(pe_, se, over(red[:], E), ALU.mult))

            def best(values_):
                for t in range(NT):
                    last = nc.vector.max(top[:, t], values_[:, t])
                link(last)
                for t in range(NT):
                    last = nc.vector.max_index(idx[:, t], top[:, t], values_[:, t])
                link(last)
                link(nc.vector.tensor_copy(idx_f[:], idx[:, :, 0:2]))

            def one_hot(dst, k, n):
                link(tt(dst, iota[:, 0:n].unsqueeze(1).to_broadcast([P, NT, n]), over(idx_f[:, :, k], n), ALU.is_equal))

            def gate_moe0():
                softmax(MOE0)
                best(pr[:, :, 0:8])
                tt(w12[:, :, 0], top[:, :, 1], top[:, :, 0], ALU.subtract).then_inc(S["gate_p"], 1)
                dve.wait_ge(S["act_gate"], 2)
                link(ts(w12[:, :, 2], w12[:, :, 1], 1.0, None, ALU.add))
                link(nc.vector.reciprocal(w12[:, :, 3], w12[:, :, 2]))
                link(tt(w12[:, :, 2], w12[:, :, 1], w12[:, :, 3], ALU.mult))
                h = hot[:, :, 0:8]
                one_hot(h, 0, 8)
                link(tt(comb[:, :, 0:8], h, over(w12[:, :, 3], 8), ALU.mult))
                one_hot(h, 1, 8)
                link(tt(h, h, over(w12[:, :, 2], 8), ALU.mult))
                tt(comb[:, :, 0:8], comb[:, :, 0:8], h, ALU.add).then_inc(S["gate_done"], 1)
                dve.wait_ge(S["gate_done"], 1)

            def gate_moe1():
                softmax(MOE1)
                link(tt(sc[:], pr[:], gate_b[:].unsqueeze(1).to_broadcast([P, NT, 16]), ALU.add))
                s4 = sc[:].rearrange("p t (g e) -> p (t g) e", g=4)
                tt(pairs[:, :, 0:3], s4[:, :, 0:3], s4[:, :, 1:4], ALU.add)
                tt(pairs[:, :, 3:5], s4[:, :, 0:2], s4[:, :, 2:4], ALU.add)
                link(tt(pairs[:, :, 5:6], s4[:, :, 0:1], s4[:, :, 3:4], ALU.add))
                link(nc.vector.tensor_reduce(grp[:, :, 0:4], pairs[:].rearrange("p (t g) e -> p t g e", g=4), AX.X, ALU.max))
                best(grp)
                keep = hot[:, :, 0:4]
                one_hot(keep, 0, 4)
                one_hot(hot[:, :, 4:8], 1, 4)
                link(tt(keep, keep, hot[:, :, 4:8], ALU.add))
                link(ts(keep, keep, -1.0, BIG, ALU.add, ALU.mult))
                k4 = keep.unsqueeze(3).to_broadcast([P, NT, 4, 4])
                link(tt(sc[:].rearrange("p t (g e) -> p t g e", g=4), sc[:].rearrange("p t (g e) -> p t g e", g=4), k4, ALU.add))
                best(sc)
                one_hot(hot[:], 0, 16)
                one_hot(sc[:], 1, 16)
                link(tt(hot[:], hot[:], sc[:], ALU.add))
                tt(comb[:, :, 0:16], hot[:], pr[:], ALU.mult).then_inc(S["gate_done"], 1)
                dve.wait_ge(S["gate_done"], 2)

            def expert_biases():
                for g in range(GROUPS):
                    dve.wait_ge(S["bias_out"], g + 1)
                    for j in range(GT):
                        x = x_all[:, g * GT + j]
                        tt(x, ps[:, B_QK + j // 2, (j % 2) * D:(j % 2 + 1) * D], x, ALU.add).then_inc(S["bias_done"], 1)
                dve.wait_ge(S["bias_done"], NT)

            def feed_forward(f):
                n = F_CHUNKS[f]

                def hidden(e, p, g):
                    for fc in range(n):
                        q = g * n + fc
                        h = h_tmp[:, q % 2, :]
                        if f != MLP:
                            dve.wait_ge(S["up_out"], units("up_out", f, e, g, fc + 1))
                            dve.wait_ge(S["act_done"], units("act_done", f, e, g, fc + 1))
                            if f == MOE0:
                                ins = tt(h, ps[:, 2 + q % 2, :], act_sb[:, q % 2, :], ALU.mult)
                            else:
                                ins = stt(out=h, in0=ps[:, 2 + q % 2, :], scalar=f_bias[:, buffer(f, p), 1:2],
                                          in1=act_sb[:, q % 2, :], op0=ALU.add, op1=ALU.mult)
                            ins.then_inc(S["h_done"], 1)
                        dve.wait_ge(S["hi_done"], units("hi_done", f, e, g, fc + 1))
                        tt(hid_lo[:, g % 2, fc], h, hid_hi[:, g % 2, fc].bitcast(f32), ALU.subtract).then_inc(S["hid_done"], 1)

                def add(e, p, g):
                    for j in range(GT):
                        t = g * GT + j
                        dve.wait_ge(S["down_out"], units("down_out", f, e, g, j + 1))
                        if not (isinstance(e, int) and e == 0):
                            dve.wait_ge(S["acc_done"], units("acc_done", f, e - 1, g, j + 1))
                        y = ps[:, 4 + j, 0:D]
                        if f == MLP:
                            ins = tt(x_all[:, t], y, x_all[:, t], ALU.add)
                        else:
                            ins = stt(out=x_all[:, t], in0=y, scalar=comb_e[:, p, t:t + 1], in1=x_all[:, t], op0=ALU.mult, op1=ALU.add)
                        ins.then_inc(S["acc_done"], 1)

                def body(e, p):
                    if f != MLP:
                        src = comb[:, :, e:e + 1] if isinstance(e, int) else comb[:, :, bass.ds(e, 1)]
                        nc.vector.tensor_copy(comb_e[:, p].unsqueeze(2), src).then_inc(S["comb_e_sb"], 1)
                    for g in range(GROUPS):
                        hidden(e, p, g)
                        if g:
                            if g == 1 and f != MLP:
                                dve.wait_ge(S["comb_e_sb"], e + (before(f) - F_EXPERTS[MLP] + 1))
                            add(e, p, g - 1)
                        elif not (isinstance(e, int) and e == 0):
                            add(e - 1, 1 - p, GROUPS - 1)

                if f != MOE1:
                    dve.wait_ge(S["n_base"], NT * (f + 1))
                experts(dve, f, body)
                n_e = F_EXPERTS[f] - 1
                add(n_e, n_e % 2, GROUPS - 1)
                dve.wait_ge(S["acc_done"], units("acc_done", f, n_e, GROUPS - 1, GT))

            dve.wait_ge(S["const_in"], 48)
            dve.wait_ge(S["setup"], 7)
            pipeline(dve, (ATT0,), step)
            norm_stage(MLP)
            feed_forward(MLP)
            dve.wait_ge(S["late_in"], 80)
            pipeline(dve, (XATT0, ATT1), step)
            norm_stage(MOE0)
            gate_moe0()
            feed_forward(MOE0)
            pipeline(dve, (RET, XATT1), step)
            norm_stage(MOE1)
            gate_moe1()
            expert_biases()
            feed_forward(MOE1)


def kernel(**inputs):
    import concourse.bacc as _bacc
    from concourse.bass_utils import run_bass_kernel_spmd as _run

    a = {k: np.asarray(v) for k, v in inputs.items()}

    def chunked(w):
        return w.reshape(-1, P, w.shape[-1]).transpose(1, 0, 2).reshape(P, -1)

    def attention(q, k, v, o):
        return np.concatenate([chunked(np.concatenate([q, k, v], 1)), chunked(o)], 1)

    def heads_last(w):
        return w.reshape(D, D).T

    n = "L0_ffn_"
    w_att = np.stack([
        np.concatenate([chunked(a["L0_attn_w_qkv"]), chunked(a["L0_attn_w_out"])], 1),
        attention(a["L0_xattn_Wq"], a["L0_xattn_Wk"], a["L0_xattn_Wv"], a["L0_xattn_Wo"]),
        attention(a[n + "wq"], a[n + "wk"], a[n + "wv"], a[n + "wo"]),
        attention(heads_last(a["L1_attn_WQ"]), heads_last(a["L1_attn_WK"]), heads_last(a["L1_attn_WV"]), a["L1_attn_WO"]),
        attention(a["L1_xattn_Wq"].T, a["L1_xattn_Wk"].T, a["L1_xattn_Wv"].T, a["L1_xattn_Wo"].T)])
    w1, w2, b1 = a["L0_attn_w1"], a["L0_attn_w2"], a["L0_attn_b1"]
    w_mlp = np.stack([np.concatenate([chunked(w1[:, s]), chunked(w2[s]), b1[s].reshape(-1, P).T], 1)
                      for s in (slice(0, 512), slice(512, 1024))])
    w_moe0 = np.stack([np.concatenate([chunked(g), chunked(u), chunked(d)], 1) for g, u, d in
                       [(a[n + "e_gate"][e], a[n + "e_up"][e], a[n + "e_down"][e]) for e in range(8)]
                       + [(a[n + "sh_gate"], a[n + "sh_up"], a[n + "sh_down"])]])
    n = "L1_ffn_"
    halves = (slice(0, P), slice(P, 2 * P))
    w_moe1 = np.stack([np.concatenate([chunked(g), chunked(u), chunked(d), bg[:, None], bu[:, None]], 1) for g, u, d, bg, bu in
                       [(a[n + "We1"][e], a[n + "We3"][e], a[n + "We2"][e], a[n + "be1"][e], a[n + "be3"][e]) for e in range(16)]
                       + [(a[n + "ws1"][:, s], a[n + "ws3"][:, s], a[n + "ws2"][s], a[n + "bs1"][s], a[n + "bs3"][s]) for s in halves]])
    be2 = np.concatenate([a[n + "be2"], a[n + "bs2"][None], np.zeros((1, D), np.float32)])
    bq = a["L0_attn_b_qkv"]
    vectors = [a["L0_attn_ln1_g"], a["L0_attn_ln1_b"], bq[0:D], bq[D:2 * D], a["L0_attn_ln2_g"], a["L0_attn_ln2_b"],
               a["L0_xattn_bq"], a["L0_xattn_bk"], a["L0_ffn_norm1_w"], a["L0_ffn_norm2_w"], a["L1_attn_gamma"],
               a["L1_attn_beta"], a["L1_xattn_bq"], a["L1_xattn_bk"]]
    vecs = np.stack(vectors).reshape(len(VEC), KC, P).transpose(2, 0, 1).reshape(P, -1)
    rows = np.concatenate([bq[2 * D:], a["L0_attn_b_out"], a["L0_attn_b2"], a["L0_xattn_bv"], a["L0_xattn_bo"],
                           a["L1_xattn_bv"], a["L1_xattn_bo"]])[None]
    router = np.concatenate([a["L0_ffn_router_w"], a["L1_ffn_gate_w"].T], 1).reshape(KC, P, 24).transpose(1, 0, 2).reshape(P, -1)
    ctxT = a["ctx_1024"].transpose(0, 2, 1).reshape(NT, KC, P, P).transpose(0, 2, 1, 3).reshape(NT, P, KC * P)
    arrays = {"x": a["x"], "const": constants(), "vecs": vecs, "rows": rows, "router": router,
              "gate_b": a["L1_ffn_gate_b"][None], "be2": be2, "pad": a["mask_BxS2_bf0"], "w_att": w_att,
              "w_f0": w_mlp, "w_f1": w_moe0, "w_f2": w_moe1, "ctxT": ctxT}
    nc = _bacc.Bacc("TRN2", target_bir_lowering=False, num_devices=1)
    arrays = {"in_" + k: np.ascontiguousarray(v) for k, v in arrays.items()}
    A = {k[3:]: nc.dram_tensor(k, v.shape, mybir.dt.from_np(v.dtype), kind="ExternalInput").ap() for k, v in arrays.items()}
    A["out"] = nc.dram_tensor("out_0", (NT, P, D), mybir.dt.float32, kind="ExternalOutput").ap()
    build(nc, A)
    r = _run(nc, [arrays], core_ids=[0])
    return r.results[0]["out_0"]
```

```python
import numpy as np
import concourse.bass as bass
from concourse import mybir
from contextlib import ExitStack

P = 128
D = 256
KC = D // P
NT = 16
H = 16
HD = D // H
HB = 4
NG = H // HB
VW = 32
HC = P // HD
BIG = 1e30
FAR = 3e38

W_QKV, W_O = 0, KC * 3 * D
W_COLS = W_O + KC * D

ATT0, XATT0, ATT1, RET, XATT1 = range(5)
CROSS = (XATT0, XATT1)
ROTARY = (XATT0, RET)
TWO_NORMS = (ATT0, ATT1)
BRANCH = (ATT0, ATT1)
OUT_BIAS = (ATT0, XATT0, XATT1)
MLP, MOE0, MOE1 = range(3)

F_EXPERTS = {MLP: 2, MOE0: 9, MOE1: 18}
F_CHUNKS = {MLP: 4, MOE0: 4, MOE1: 1}
F_ROUTED = {MLP: 0, MOE0: 8, MOE1: 16}
GROUPS, GT = 4, 4
GN = GT * P

VEC = ["ln1_g", "ln1_b", "bq0", "bk0", "ln2_g", "ln2_b", "xbq", "xbk", "n1_w", "n2_w", "gamma",
       "beta", "ybq", "ybk"]
ROW = ["bv0", "bo0", "b2", "xbv", "xbo", "ybv", "ybo"]

C_ID, C_CAUSAL, C_BAND, C_HEAD, C_IOTA, C_CLAMP, C_ZKEYS = 0, 128, 256, 384, 392, 408, 409
C_ROT = 410
C_DECAY = C_ROT + 2 * 2 * 4 * P
C_COLS = C_DECAY + H * P


def f_cols(f):
    c, gates = F_CHUNKS[f], 1 if f == MLP else 2
    return gates * KC * c * P + c * D + (c * gates if f != MOE0 else 0)


def constants():
    c = np.zeros((P, C_COLS), np.float32)
    i = np.arange(P)
    c[:, C_ID:C_ID + P] = np.eye(P)
    c[:, C_CAUSAL:C_CAUSAL + P] = np.where(i[None] <= i[:, None], 0.0, -BIG)
    c[:, C_BAND:C_BAND + P] = np.where((i[None] <= i[:, None]) & (i[:, None] - i[None] <= 64), 0.0, -BIG)
    for j in range(HC):
        c[:, C_HEAD + j] = i // HD == j
    c[:, C_IOTA:C_IOTA + 16] = np.arange(16)
    c[:, C_CLAMP] = np.where(i < 64, 0.0, FAR)
    c[:, C_ZKEYS] = np.where(i < 64, 64.0, 0.0)
    half = HD // 2
    pos = np.arange(P, dtype=np.float32)
    pair = (i % HD) // 2
    sign = np.where(i % 2 == 0, -1.0, 1.0).astype(np.float32)
    vec = (np.arange(0, HD, 2, dtype=np.float32) + np.float32(0.4 * HD)) / np.float32(1.4 * HD)
    power = (np.arange(-(P // 2), P - P // 2, dtype=np.float32)) / np.float32(128)
    scale = (vec[None] ** power[:, None]).astype(np.float32)
    inv = (1.0 / np.float32(10000.0) ** (np.arange(half, dtype=np.float32) / np.float32(half))).astype(np.float32)
    ang = pos[:, None] * inv[None]
    rot = c[:, C_ROT:C_DECAY].reshape(P, 2, 2, 4, P)
    for m, sc in ((0, scale), (1, scale), (2, 1 / scale), (3, 1 / scale)):
        rot[:, 0, 0, m] = (np.cos(ang) * sc).T[pair]
        rot[:, 0, 1, m] = (np.sin(ang) * sc).T[pair] * sign[:, None]
    angle = (np.float32(10.0) ** (np.float32(-4.0) * (np.arange(0, HD, 2, dtype=np.float32) / HD))).astype(np.float32)
    ang = pos[:, None] * angle[None]
    rot[:, 1, 0, :] = np.cos(ang).T[pair][:, None]
    rot[:, 1, 1, :] = (np.sin(ang).T[pair] * sign[:, None])[:, None]
    g = (1.0 - 2.0 ** (-5.0 - np.arange(H))).astype(np.float32)
    diff = i[None, :] - i[:, None]
    dec = np.exp(np.maximum(diff, 0)[:, None, :].astype(np.float32) * np.log(g)[None, :, None])
    c[:, C_DECAY:] = (dec * (diff >= 0)[:, None, :]).reshape(P, H * P)
    return c


class Tile:

    def __init__(self, l, t, p):
        self.l, self.t, self.p = l, t, p

    def back(self, d):
        if isinstance(self.t, int) and self.t < d:
            return Tile(self.l - 1, self.t - d + NT, (self.p + d) % 2) if self.l else None
        return Tile(self.l, self.t - d, (self.p + d) % 2)


SOME = {"var2": TWO_NORMS, "rstd2": TWO_NORMS, "v_norm": TWO_NORMS, "base_sb": (ATT0, XATT0, ATT1, XATT1),
        "swapped": ROTARY, "zmax_sb": (ATT0,), "zero_exp": (ATT0,), "pad_mask": (XATT0,), "pad_in": (XATT0,), "gn_var": (RET,),
        "gn_eps": (RET,), "gn_rstd": (RET,)}
PER_TILE = {"scores_out": (NG,) * 5, "p_sub": (NG, NG, NG, 0, NG), "probs": (NG, NG, NG, 0, NG),
            "pT_out": (NG, NG, NG, 0, NG), "pT_sb": (NG, NG, NG, 0, NG), "ret_sb": (0, 0, 0, NG, 0),
            "dve_ln": (2, 1, 1, 1, 1), "dve_sm": (2 * NG, NG, NG, 0, NG),
            "dve_o": (2, 1, 1, 4, 1), "pool_r": (2, 1, 2, 1, 1), "pool_m": (0, 3, 0, 3, 0)}


def increments(name, l):
    if name in PER_TILE:
        return PER_TILE[name][l]
    return int(l in SOME.get(name, range(5)))


def reached(name, tile, k=None):
    per = increments(name, tile.l)
    base = sum(increments(name, l) * NT for l in range(tile.l))
    return tile.t * per + (base + (per if k is None else k))


def build(nc, A):
    f32, f32r, bf16, u32, u8 = mybir.dt.float32, mybir.dt.float32r, mybir.dt.bfloat16, mybir.dt.uint32, mybir.dt.uint8
    ALU, ACT, AX = mybir.AluOpType, mybir.ActivationFunctionType, mybir.AxisListType
    ctx = ExitStack()
    with ctx:
        def sb(name, shape, dt=f32):
            return ctx.enter_context(nc.sbuf_tensor(name, shape, dt))

        x_all = sb("x_all", [P, NT, D])
        const = sb("const", [P, C_COLS])
        vecs = sb("vecs", [P, len(VEC), KC])
        rows = sb("rows", [P, len(ROW), D])
        router = sb("router", [P, KC, 8 + 16])
        gate_b = sb("gate_b", [P, 16])
        be2 = sb("be2", [18, D])
        pad_u8 = sb("pad_u8", [P, NT, P], u8)
        id_bf = sb("id_bf", [P, P], bf16)
        mask_bf = sb("mask_bf", [P, 2, P], bf16)
        pad_bf = sb("pad_bf", [P, 2, P], bf16)
        half_neg = sb("half_neg", [P, H])
        stats = sb("stats", [P, 2, 6])
        mv = sb("mv", [P, 2, 2])
        rstd = sb("rstd", [P, 2, 2])
        eps_sum = sb("eps_sum", [P, 2, 1])
        v = sb("v", [P, 2, D])
        hT = sb("hT", [P, 2, KC, P])
        va = sb("va", [P, 2, H, VW])
        negmax = sb("negmax", [P, 2, H])
        zmax = sb("zmax", [P, 2, H])
        den = sb("den", [P, 2, H])
        gn = sb("gn", [P, 2, 3, H])
        gsq = sb("gsq", [P, D])
        sumT = sb("sumT", [P, 4 * P])
        fT_hi = sb("fT_hi", [P, NT, KC, P], f32r)
        w_hi = sb("w_hi", [P, 2, f_cols(MOE0)], f32r)
        w_lo = sb("w_lo", [P, 2, f_cols(MOE0)], f32r)
        f_bias = sb("f_bias", [P, 2, 4])
        act_sb = sb("act_sb", [P, 2, GN])
        lg = sb("lg", [P, NT, 16])
        pr = sb("pr", [P, NT, 16])
        sc = sb("sc", [P, NT, 16])
        pairs = sb("pairs", [P, NT * 4, 6])
        top = sb("top", [P, NT, 8])
        grp = sb("grp", [P, NT, 8])
        idx = sb("idx", [P, NT, 8], u32)
        idx_f = sb("idx_f", [P, NT, 2])
        w12 = sb("w12", [P, NT, 4])
        hot = sb("hot", [P, NT, 16])
        comb = sb("comb", [P, NT, 18])
        comb_e = sb("comb_e", [P, 2, NT])
        red = sb("red", [P, NT])
        w_odd = sb("w_odd", [P, W_COLS])
        with ExitStack() as shared:
            def at_attention(name, shape):
                return shared.enter_context(nc.sbuf_tensor(name, shape, f32))
            r_all = at_attention("r_all", [P, NT, D])
            w_even = at_attention("w_even", [P, W_COLS])
            o = at_attention("o", [P, 2, D])
            oT = at_attention("oT", [P, 2, KC, P])
            probs_all = at_attention("probs_all", [P, H * P])
            probsT_all = at_attention("probsT_all", [P, H * P])
            km = at_attention("km", [P, KC, HC, P])
            qk = at_attention("qk", [P, 2, 2 * KC, P])
            u = at_attention("u", [P, 2, D])
            ctxT = at_attention("ctxT", [P, 2, KC, P])
            qk_swap = at_attention("qk_swap", [P, 2 * KC, P])
            qk_cos = at_attention("qk_cos", [P, 2 * KC, P])
        fT_lo = sb("fT_lo", [P, NT, KC, P], f32r)
        w_raw = sb("w_raw", [P, f_cols(MOE0)])
        hid_hi = sb("hid_hi", [P, 2, 4, GN], f32r)
        hid_lo = sb("hid_lo", [P, 2, 4, GN], f32r)
        h_tmp = sb("h_tmp", [P, 2, GN])
        w_of = (w_even, w_odd)
        combT = w_odd[0:18, :]
        probs = probs_all[:].rearrange("p (g h k) -> p g h k", g=NG, h=HB)
        probsT = probsT_all[:].rearrange("p (g h k) -> p g h k", g=NG, h=HB)

        ps = ctx.enter_context(nc.psum_tensor("ps", [P, 8, 512], f32))
        B_O, B_T, B_QK, B_V = 4, 5, 6, 7

        ident = const[:, C_ID:C_ID + P]
        head_mask = const[:, C_HEAD:C_HEAD + HC]
        iota = const[:, C_IOTA:C_IOTA + 16]

        def vec(name, c):
            return vecs[:, VEC.index(name), c:c + 1]

        def row(name):
            return rows[:, ROW.index(name), :]

        S = {}

        def sem(name):
            if name not in S:
                S[name] = ctx.enter_context(nc.semaphore(name))
            return S[name]

        for name in ("var1 rstd1 u_norm var2 rstd2 v_norm base_sb uT_out hT_sb qk_out v_out qk_sb swapped km_sb va_sb "
                     "scores_out p_sub probs pT_out pT_sb ret_sb pv_out zero_exp o_norm oT_out oT_sb y_out x_done "
                     "sum_sb sum_out ctx_in0 ctx_in1 pad_mask pad_in gn_var gn_rstd zmax_sb gn_eps dve_ln dve_sm dve_o pool_r pool_m "
                     "n_sq n_var n_rstd n_norm n_base n_out n_sb fT_hi_sb fT_sb lg_out lg_sb dve_n pool_n "
                     "x_in0 x_in1 x_in2 x_in3 const_in rows_in late_in w_att0 w_att1 w_att2 w_att3 w_att4 w_raw_in f_bias_sb w_hi_sb w_lo_sb setup passed gate gate_p gate_done comb_out comb_sb bias_done "
                     "gate_out up_out act_done h_done hi_done hid_done down_out acc_done comb_e_sb act_gate stored").split():
            sem(name)

        def wait(eng, name, tile, k=None):
            if tile is not None:
                eng.wait_ge(S[name], reached(name, tile, k))

        def wait_apart(eng, *waits):
            for name, n in waits:
                eng.wait_ge(S[name], n)
            eng.sem_inc(S["passed"], 1)

        def n_reached(name, f, t, k=None):
            per = {"dve_n": 1}.get(name, 1)
            layers = {"n_base": (MLP, MOE0), "lg_out": (MOE0, MOE1), "lg_sb": (MOE0, MOE1)}.get(name, (MLP, MOE0, MOE1))
            return t * per + NT * per * sum(1 for g in layers if g < f) + (per if k is None else k)

        def pipeline(eng, layers, step):
            first, end = NT * layers[0], NT * (layers[-1] + 1)

            def written_out(a, b):
                for s in range(a, b):
                    step({d: Tile((s + d) // NT, (s + d) % NT, (s + d) % 2) for d in range(-1, 4) if first <= s + d < end})

            for l in layers:
                written_out(NT * l - 3 if l == layers[0] else NT * l, NT * l + 3)
                with eng.Fori(0, 5) as i:
                    for j in range(2):
                        step({d: Tile(l, i * 2 + (3 + j + d), (3 + j + d) % 2) for d in range(-1, 4)})
                written_out(NT * l + 13, NT * (l + 1))
            written_out(end, end + 1)

        def norm_pipeline(eng, step, near_end=None):
            def written_out(a, b):
                for s in range(a, b):
                    step({d: (s + d, (s + d) % 2) for d in range(-1, 3) if 0 <= s + d < NT})
            written_out(-2, 2)
            with eng.Fori(0, 6) as i:
                for j in range(2):
                    step({d: (i * 2 + (2 + j + d), (2 + j + d) % 2) for d in range(-1, 3)})
            if near_end:
                near_end()
            written_out(14, 17)

        def experts(eng, f, body):
            n, first = F_EXPERTS[f], 2 if f == MOE1 else 1
            for e in range(first):
                body(e, e % 2)
            pairs_ = (n - first - 1) // 2
            if pairs_ > 1:
                with eng.Fori(0, pairs_) as i:
                    for j in range(2):
                        body(i * 2 + (first + j), (first + j) % 2)
            else:
                pairs_ = 0
            for e in range(first + 2 * pairs_, n):
                body(e, e % 2)

        def bias_expert(f, e):
            return f == MOE1 and isinstance(e, int) and e == F_EXPERTS[f] - 2

        def before(f):
            return sum(F_EXPERTS[g] for g in range(f))

        def buffer(f, p):
            return (before(f) + p) % 2

        def weights_reached(f, e):
            return e + (before(f) + 1)

        def units(name, f, e, g, k):
            def per(fl):
                c = F_CHUNKS[fl]
                return {"gate_out": c, "up_out": 0 if fl == MLP else c, "act_done": c, "h_done": 0 if fl == MLP else c,
                        "hi_done": c, "hid_done": c,
                        "down_out": GT, "acc_done": GT}[name]
            base = sum(per(fl) * F_EXPERTS[fl] * GROUPS for fl in range(f))
            return e * (per(f) * GROUPS) + (base + per(f) * g + k)

        def tiles_of(l, t):
            return Tile(l, t, t % 2)

        def at_tile(t):
            return bass.ds(t, 1)

        def output(tile):
            return ps[:, B_V, D:2 * D] if tile.l == RET else ps[:, B_QK, 0:D]

        def logits(f):
            return ps[:, B_O, 0:NT * F_ROUTED[f]].rearrange("p (t e) -> p t e", t=NT)

        LAST = {MLP: ATT0, MOE0: ATT1, MOE1: XATT1}
        block = ctx.enter_context(nc.Block())

        @block.sync
        def _(sp):
            def load_attention(l):
                sp.dma_start(w_of[l % 2][:], A["w_att"][l]).then_inc(S["w_att%d" % l], 16)

            xv = A["x"].rearrange("s t d -> t s d")
            sp.dma_start(x_all[:, 0:GT, :], xv[:, 0:GT, :]).then_inc(S["x_in0"], 16)
            sp.dma_start(const[:, 0:C_ROT], A["const"][:, 0:C_ROT]).then_inc(S["const_in"], 16)
            sp.dma_start(vecs[:], A["vecs"].rearrange("p (v c) -> p v c", c=KC)).then_inc(S["const_in"], 16)
            load_attention(ATT0)
            sp.dma_start(rows[:], A["rows"].rearrange("a (r d) -> a r d", d=D).to_broadcast([P, len(ROW), D])).then_inc(S["rows_in"], 16)
            for g in range(1, GROUPS):
                sp.dma_start(x_all[:, g * GT:(g + 1) * GT, :], xv[:, g * GT:(g + 1) * GT, :]).then_inc(S["x_in%d" % g], 16)
            sp.dma_start(const[:, C_ROT:C_COLS], A["const"][:, C_ROT:C_COLS]).then_inc(S["late_in"], 16)
            sp.dma_start(router[:], A["router"].rearrange("p (c e) -> p c e", c=KC)).then_inc(S["late_in"], 16)
            sp.dma_start(gate_b[:], A["gate_b"].to_broadcast([P, 16])).then_inc(S["late_in"], 16)
            sp.dma_start(be2[:], A["be2"]).then_inc(S["late_in"], 16)
            sp.dma_start(pad_u8[:], A["pad"].rearrange("(a s) k -> a s k", a=1).to_broadcast([P, NT, P])).then_inc(S["late_in"], 16)
            load_attention(XATT0)

            def load_experts(f):
                def load(e, p):
                    if isinstance(e, int) and e == 0:
                        wait(sp, "x_done", tiles_of(LAST[f], NT - 1))
                    else:
                        sp.wait_ge(S["w_lo_sb"], weights_reached(f, e - 1))
                    src = A["w_f%d" % f]
                    src = src[e] if isinstance(e, int) else src[bass.ds(e, 1)].rearrange("a p n -> (a p) n")
                    sp.dma_start(w_raw[:, 0:f_cols(f)], src).then_inc(S["w_raw_in"], 16)
                experts(sp, f, load)
                sp.wait_ge(S["acc_done"], units("acc_done", f, F_EXPERTS[f] - 1, GROUPS - 1, GT))

            def load_ctx(layers):
                def step(at):
                    if 2 in at and at[2].l in CROSS:
                        wait(sp, "v_out", at[2].back(2))
                        src = A["ctxT"][at[2].t] if isinstance(at[2].t, int) else \
                            A["ctxT"][bass.ds(at[2].t, 1)].rearrange("a p n -> (a p) n")
                        sp.dma_start(ctxT[:, at[2].p].rearrange("p c k -> p (c k)"), src).then_inc(S["ctx_in%d" % at[2].p], 16)
                pipeline(sp, layers, step)

            load_experts(MLP)
            load_attention(ATT1)
            load_ctx((XATT0, ATT1))
            wait(sp, "x_done", tiles_of(XATT0, NT - 1))
            load_attention(RET)
            load_experts(MOE0)
            load_attention(XATT1)
            load_ctx((RET, XATT1))
            load_experts(MOE1)
            out = A["out"].rearrange("s t d -> t s d")
            for g in range(GROUPS):
                sp.dma_start(out[:, g * GT:(g + 1) * GT, :], x_all[:, g * GT:(g + 1) * GT, :]).then_inc(S["stored"], 16)
            sp.wait_ge(S["stored"], 16 * GROUPS)

        @block.gpsimd
        def _(pool):
            for ins in (nc.gpsimd.memset(half_neg[:], -0.5), nc.gpsimd.memset(va[:], 1.0), nc.gpsimd.memset(grp[:], -FAR),
                        nc.gpsimd.memset(comb[:], 1.0)):
                ins.then_inc(S["setup"], 1)
            pool.wait_ge(S["const_in"], 32)
            for ins in (nc.gpsimd.tensor_copy(id_bf[:], ident),
                        nc.gpsimd.tensor_copy(mask_bf[:, 0], const[:, C_CAUSAL:C_CAUSAL + P]),
                        nc.gpsimd.tensor_copy(mask_bf[:, 1], const[:, C_BAND:C_BAND + P])):
                ins.then_inc(S["setup"], 1)
            pool.wait_ge(S["setup"], 7)

            def inverse_root(tile, which, p):
                var_, eps = ("var1", 1e-5) if which == 0 else ("var2", 1e-6 if tile.l == ATT1 else 1e-5)
                wait_apart(pool, (var_, reached(var_, tile)))
                nc.gpsimd.tensor_scalar(eps_sum[:, p], mv[:, p, 1:2], eps, None, ALU.add).then_inc(S["pool_r"], 1)
                wait(pool, "pool_r", tile, which + 1)
                nc.gpsimd.tensor_tensor(rstd[:, p, which:which + 1], eps_sum[:, p], half_neg[:, 0:1],
                                        ALU.pow).then_inc(S["rstd1" if which == 0 else "rstd2"], 1)

            def rotation(l):
                return const[:, C_ROT:C_DECAY].rearrange("p (l s m k) -> p l s m k", l=2, s=2, m=2 * KC)[:, ROTARY.index(l)]

            def cosines(tile):
                if tile.l in ROTARY:
                    wait(pool, "qk_sb", tile)
                    nc.gpsimd.tensor_tensor(qk_cos[:], qk[:, tile.p], rotation(tile.l)[:, 0], ALU.mult).then_inc(S["pool_m"], 1)

            def keys(tile):
                p = tile.p
                if tile.l in ROTARY:
                    r = rotation(tile.l)
                    wait(pool, "swapped", tile)
                    nc.gpsimd.tensor_tensor(qk_swap[:], qk_swap[:], r[:, 1], ALU.mult).then_inc(S["pool_m"], 1)
                    wait(pool, "pool_m", tile, 2)
                    nc.gpsimd.tensor_tensor(qk[:, p], qk_cos[:], qk_swap[:], ALU.add).then_inc(S["pool_m"], 1)
                if tile.l == XATT0:
                    two = tile.back(2)
                    if two is not None:
                        wait_apart(pool, ("scores_out", reached("scores_out", two)))
                    nc.gpsimd.tensor_copy(pad_bf[:, p:p + 1], pad_u8[:, at_tile(tile.t), :]).then_inc(S["pad_in"], 1)
                    wait_apart(pool, ("pad_in", reached("pad_in", tile)))
                    nc.gpsimd.tensor_scalar(pad_bf[:, p], pad_bf[:, p], -BIG, None, ALU.mult).then_inc(S["pad_mask"], 1)

            def base(tile):
                if tile.l == RET:
                    return
                t = at_tile(tile.t)
                if tile.l == ATT0 and isinstance(tile.t, int) and tile.t == 0:
                    pool.wait_ge(S["rows_in"], 16)
                wait_apart(pool, ("u_norm", reached("u_norm", tile)))
                dst = r_all if tile.l in BRANCH else x_all
                src = u[:, tile.p:tile.p + 1] if tile.l in BRANCH else x_all[:, t]
                if tile.l == ATT1:
                    nc.gpsimd.tensor_copy(dst[:, t], src).then_inc(S["base_sb"], 1)
                else:
                    b = {ATT0: "bo0", XATT0: "xbo", XATT1: "ybo"}[tile.l]
                    nc.gpsimd.tensor_tensor(dst[:, t], src, row(b).unsqueeze(1), ALU.add).then_inc(S["base_sb"], 1)

            def step(at):
                if 1 in at:
                    cosines(at[1])
                if -1 in at and at[-1].l == RET:
                    tile = at[-1]
                    wait_apart(pool, ("gn_var", reached("gn_var", tile)))
                    nc.gpsimd.tensor_scalar(gn[:, tile.p, 1], gn[:, tile.p, 0], 1.0 / HD, 1e-5, ALU.mult,
                                            ALU.add).then_inc(S["gn_eps"], 1)
                    wait(pool, "gn_eps", tile)
                    nc.gpsimd.tensor_tensor(gn[:, tile.p, 2], gn[:, tile.p, 1], half_neg[:], ALU.pow).then_inc(S["gn_rstd"], 1)
                if 1 in at:
                    keys(at[1])
                if 3 in at:
                    inverse_root(at[3], 0, at[3].p)
                    if at[3].l in TWO_NORMS:
                        inverse_root(at[3], 1, at[3].p)
                    base(at[3])

            def norm_stage(f):
                def step(at):
                    if 2 in at:
                        t, p = at[2]
                        wait_apart(pool, ("n_var", n_reached("n_var", f, t)))
                        per, eps = (1.0 / D, 1e-6) if f == MOE0 else (1.0, 1e-5)
                        nc.gpsimd.tensor_scalar(eps_sum[:, p], mv[:, p, 1:2], per, eps, ALU.mult,
                                                ALU.add).then_inc(S["pool_n"], 1)
                        pool.wait_ge(S["pool_n"], n_reached("pool_n", f, t))
                        nc.gpsimd.tensor_tensor(rstd[:, p, 0:1], eps_sum[:, p], half_neg[:, 0:1], ALU.pow).then_inc(S["n_rstd"], 1)
                wait(pool, "x_done", tiles_of(LAST[f], NT - 1))
                norm_pipeline(pool, step)
                if f == MLP:
                    pool.wait_ge(S["gate_p"], NT)
                    with pool.Fori(0, NT) as t:
                        x = x_all[:, at_tile(t)]
                        nc.gpsimd.tensor_tensor(x, x, row("b2").unsqueeze(1), ALU.add).then_inc(S["n_base"], 1)

            def split_weights(f):
                def body(e, p):
                    if isinstance(e, int) and e == F_EXPERTS[f] - 1:
                        return
                    b, n = buffer(f, 1 - p), f_cols(f)
                    pool.wait_ge(S["w_hi_sb"], weights_reached(f, e + 1))
                    nc.gpsimd.tensor_tensor(w_lo[:, b, 0:n], w_raw[:, 0:n], w_hi[:, b, 0:n].bitcast(f32),
                                            ALU.subtract).then_inc(S["w_lo_sb"], 1)
                experts(pool, f, body)

            pipeline(pool, (ATT0,), step)
            norm_stage(MLP)
            split_weights(MLP)
            pool.wait_ge(S["late_in"], 80)
            pool.wait_ge(S["acc_done"], units("acc_done", MLP, F_EXPERTS[MLP] - 1, GROUPS - 1, GT))
            pipeline(pool, (XATT0, ATT1), step)
            norm_stage(MOE0)
            split_weights(MOE0)
            pool.wait_ge(S["acc_done"], units("acc_done", MOE0, F_EXPERTS[MOE0] - 1, GROUPS - 1, GT))
            pipeline(pool, (RET, XATT1), step)
            norm_stage(MOE1)
            split_weights(MOE1)

        @block.tensor
        def _(pe):
            mm, tr = nc.tensor.matmul, nc.tensor.transpose

            def scores(tile, groups):
                p, last = tile.p, tile.back(1)
                mask = {ATT0: mask_bf[:, 0:1], XATT0: pad_bf[:, p:p + 1], XATT1: mask_bf[:, 1:2]}.get(tile.l)
                stationary = KC if tile.l == RET else 0
                for g in groups:
                    if g == 0:
                        wait(pe, "km_sb", tile)
                        if tile.l == XATT0:
                            wait(pe, "pad_mask", tile)
                    if last is not None:
                        wait(pe, "ret_sb" if last.l == RET else "pT_sb", last, g + 1)
                    c, j = g // 2, HB * (g % 2)
                    if mask is not None:
                        mm(ps[:, g, :].rearrange("p (h k) -> p h k", h=HB), id_bf[:], mask.to_broadcast([P, HB, P]),
                           start=True, stop=False)
                    mm(ps[:, g, :], qk[:, p, stationary + c, :], km[:, c, j:j + HB, :].rearrange("p h k -> p (h k)"),
                       start=mask is None, stop=True).then_inc(S["scores_out"], 1)

            def turn_in(tile):
                wait(pe, "v_norm" if tile.l in TWO_NORMS else "u_norm", tile)
                wait(pe, "hT_sb", tile.back(1))
                wait(pe, "oT_sb", tile.back(4))
                src = v if tile.l in TWO_NORMS else u
                for c in range(KC):
                    last = tr(ps[:, B_T, c * P:(c + 1) * P], src[:, tile.p, c * P:(c + 1) * P], ident)
                last.then_inc(S["uT_out"], 1)

            def turn_out(tile, at):
                wait(pe, "o_norm", tile)
                if 2 in at and tile.l == RET:
                    wait(pe, "hT_sb", at[2])
                if 2 not in at:
                    wait(pe, "hT_sb", last_of(tile))
                    wait(pe, "oT_sb", tile.back(1))
                for c in range(KC):
                    last = tr(ps[:, B_T, D + c * P:D + (c + 1) * P], o[:, tile.p, c * P:(c + 1) * P], ident)
                last.then_inc(S["oT_out"], 1)

            def last_of(tile):
                return tiles_of({ATT0: ATT0, XATT0: ATT1, ATT1: ATT1}.get(tile.l, XATT1), NT - 1)

            def project(tile):
                p = tile.p
                w = w_of[tile.l % 2][:, W_QKV:W_O].rearrange("p (c n) -> p c n", c=KC)
                if isinstance(tile.t, int) and tile.t == 0:
                    pe.wait_ge(S["w_att%d" % tile.l], 16)
                wait(pe, "hT_sb", tile)
                if tile.l in CROSS:
                    pe.wait_ge(S["ctx_in%d" % p], (tile.t - p) * 8 + 16 + 16 * (NT // 2) * CROSS.index(tile.l))
                wait(pe, "qk_sb", tile.back(1))
                if tile.back(3) is not None and tile.back(3).l != RET:
                    wait(pe, "x_done", tile.back(3))
                kv = ctxT if tile.l in CROSS else hT
                for m in range(2 * KC):
                    for c in range(KC):
                        src = hT if m < KC else kv
                        last = mm(ps[:, B_QK, m * P:(m + 1) * P], w[:, c, m * P:(m + 1) * P], src[:, p, c, :],
                                  start=(c == 0), stop=(c == KC - 1))
                last.then_inc(S["qk_out"], 1)

            def project_values(tile):
                p = tile.p
                w = w_of[tile.l % 2][:, W_QKV:W_O].rearrange("p (c n) -> p c n", c=KC)
                kv = ctxT if tile.l in CROSS else hT
                wait(pe, "va_sb", tile.back(1))
                if tile.back(3) is not None and tile.back(3).l == RET:
                    wait(pe, "x_done", tile.back(3))
                for c in range(KC):
                    last = mm(ps[:, B_V, 0:D], kv[:, p, c, :], w[:, c, 2 * D:3 * D], start=(c == 0), stop=(c == KC - 1))
                last.then_inc(S["v_out"], 1)

            def out_project(tile, at):
                w = w_of[tile.l % 2][:, W_O:W_COLS].rearrange("p (c n) -> p c n", c=KC)
                wait(pe, "oT_sb", tile)
                if tile.l == RET:
                    wait(pe, "va_sb", at[1])
                else:
                    wait(pe, "qk_sb", at[1] if 1 in at else last_of(tile))
                if 1 not in at:
                    wait(pe, "x_done", tile.back(1))
                for c in range(KC):
                    last = mm(output(tile), oT[:, tile.p, c, :], w[:, c, :], start=(c == 0), stop=(c == KC - 1))
                last.then_inc(S["y_out"], 1)

            def turn_probs(tile, g):
                if tile.l != RET:
                    wait(pe, "probs", tile, g + 1)
                    for j in range(HB):
                        last = tr(ps[:, g, j * P:(j + 1) * P], probs[:, g, j, :], ident)
                    last.then_inc(S["pT_out"], 1)

            def weigh_values(tile, g):
                if g == 0:
                    wait(pe, "va_sb", tile)
                    last = tile.back(1)
                    if last is not None and last.l == RET:
                        wait(pe, "dve_o", last, 3)
                    else:
                        wait(pe, "o_norm", last)
                wait(pe, "ret_sb" if tile.l == RET else "pT_sb", tile, g + 1)
                for j in range(HB):
                    last = mm(ps[VW * j:VW * (j + 1), B_O, g * P:(g + 1) * P], va[:, tile.p, g * HB + j, :],
                              probsT[:, g, j, :], start=True, stop=True)
                if g == NG - 1:
                    last.then_inc(S["pv_out"], 1)

            def turn_sums(tile):
                wait(pe, "sum_sb", tile)
                for g in range(NG):
                    last = tr(ps[:, B_O, g * P:(g + 1) * P], sumT[:, g * P:(g + 1) * P], ident)
                last.then_inc(S["sum_out"], 1)

            def step(at):
                now, out = at.get(0), at.get(-1)
                if 1 in at:
                    project(at[1])
                late = out is not None and out.l == RET
                if late:
                    turn_sums(out)
                if now:
                    scores(now, (0, 1))
                if out and not late:
                    turn_sums(out)
                if now:
                    scores(now, (2, 3))
                if 2 in at:
                    turn_in(at[2])
                if now:
                    turn_probs(now, 0)
                if out and not late:
                    turn_out(out, at)
                if now:
                    turn_probs(now, 1)
                if out and not late:
                    out_project(out, at)
                if now:
                    weigh_values(now, 0)
                    turn_probs(now, 2)
                    weigh_values(now, 1)
                    turn_probs(now, 3)
                if 1 in at:
                    project_values(at[1])
                if now:
                    weigh_values(now, 2)
                    weigh_values(now, 3)
                if late:
                    turn_out(out, at)
                    out_project(out, at)

            def norm_stage(f):
                def step(at):
                    if 0 in at:
                        t, p = at[0]
                        pe.wait_ge(S["n_norm"], n_reached("n_norm", f, t))
                        if not isinstance(t, int) or t >= 2:
                            pe.wait_ge(S["n_sb"], n_reached("n_sb", f, t - 2))
                        for c in range(KC):
                            last = tr(ps[:, (B_T, B_QK)[p], c * P:(c + 1) * P], v[:, p, c * P:(c + 1) * P], ident)
                        last.then_inc(S["n_out"], 1)
                    if -1 in at and f != MLP:
                        t, p = at[-1]
                        w = router[:, :, 0:8] if f == MOE0 else router[:, :, 8:24]
                        pe.wait_ge(S["n_sb"], n_reached("n_sb", f, t))
                        for c in range(KC):
                            last = mm(logits(f)[:, at_tile(t)].rearrange("p a e -> p (a e)"), hT[:, p, c, :], w[:, c, :], start=(c == 0), stop=(c == KC - 1))
                        last.then_inc(S["lg_out"], 1)
                wait(pe, "x_done", tiles_of(LAST[f], NT - 1))
                norm_pipeline(pe, step)

            def feed_forward(f):
                n = F_CHUNKS[f]

                def three(out, parts, first, last):
                    for k, (a, b) in enumerate(parts):
                        ins = mm(out, a, b, start=first and k == 0, stop=last and k == 2)
                    return ins

                def up(e, p, g):
                    b = buffer(f, p)
                    if g == 0:
                        pe.wait_ge(S["w_lo_sb"], weights_reached(f, e))
                    if bias_expert(f, e) and g in (1, 2):
                        pe.wait_ge(S["comb_sb"], 2 * g)
                    for fc in range(n):
                        q = g * n + fc
                        for which, name, free in ((0, "gate_out", "act_done"), (1, "up_out", "h_done"))[:1 if f == MLP else 2]:
                            before_two = units(free, f, e, g, fc + 1 - 2)
                            if not (isinstance(before_two, int) and before_two <= 0):
                                pe.wait_ge(S[free], before_two)
                            for c in range(KC):
                                at = (which * KC + c) * n * P + fc * P
                                wh, wl = w_hi[:, b, at:at + P], w_lo[:, b, at:at + P]
                                xh, xl = fT_hi[:, g * GT:(g + 1) * GT, c, :], fT_lo[:, g * GT:(g + 1) * GT, c, :]
                                last = three(ps[:, 2 * which + q % 2, :].rearrange("p (t k) -> p t k", t=GT),
                                             ((wh, xh), (wh, xl), (wl, xh)), c == 0, c == KC - 1)
                            last.then_inc(S[name], 1)

                def down(e, p, g):
                    b = buffer(f, p)
                    at = (1 if f == MLP else 2) * KC * n * P
                    pe.wait_ge(S["hid_done"], units("hid_done", f, e, g, n))
                    for j in range(GT):
                        free = units("acc_done", f, e, g, j + 1 - GT)
                        if not (isinstance(free, int) and free <= 0):
                            pe.wait_ge(S["acc_done"], free)
                        for fc in range(n):
                            hh, hl = hid_hi[:, g % 2, fc, j * P:(j + 1) * P], hid_lo[:, g % 2, fc, j * P:(j + 1) * P]
                            wh, wl = w_hi[:, b, at + fc * D:at + (fc + 1) * D], w_lo[:, b, at + fc * D:at + (fc + 1) * D]
                            last = three(ps[:, 4 + j, 0:D], ((hh, wh), (hh, wl), (hl, wh)), fc == 0, fc == n - 1)
                        if f == MOE1 and isinstance(e, int) and e == F_EXPERTS[f] - 1:
                            t = g * GT + j
                            last = mm(ps[:, 4 + j, D:2 * D], combT[:, t * P:(t + 1) * P], be2[:], start=True, stop=True)
                        last.then_inc(S["down_out"], 1)

                def body(e, p):
                    for g in range(GROUPS):
                        up(e, p, g)
                        if g:
                            down(e, p, g - 1)
                        elif not (isinstance(e, int) and e == 0):
                            down(e - 1, 1 - p, GROUPS - 1)
                        if bias_expert(f, e) and g < 2:
                            turn_comb(e, g)

                def turn_comb(e, g):
                    pe.wait_ge(S["gate_done"], 2)
                    if g == 0:
                        pe.wait_ge(S["h_done"], units("h_done", f, e - 1, GROUPS - 1, 1))
                    else:
                        pe.wait_ge(S["h_done"], units("h_done", f, e, g - 1, 1))
                    for k in range(2):
                        for j in range(GT):
                            last = tr(ps[0:18, 1 - g + 2 * k, j * P:(j + 1) * P], comb[:, (2 * g + k) * GT + j, :], ident)
                        last.then_inc(S["comb_out"], 1)

                pe.wait_ge(S["fT_sb"], NT * (f + 1))
                if f != MLP:
                    pe.wait_ge(S["lg_sb"], f)
                experts(pe, f, body)
                n_e = F_EXPERTS[f] - 1
                down(n_e, n_e % 2, GROUPS - 1)
                pe.wait_ge(S["acc_done"], units("acc_done", f, n_e, GROUPS - 1, GT))

            pe.wait_ge(S["const_in"], 32)
            pe.wait_ge(S["setup"], 7)
            pipeline(pe, (ATT0,), step)
            norm_stage(MLP)
            feed_forward(MLP)
            pe.wait_ge(S["late_in"], 80)
            pipeline(pe, (XATT0, ATT1), step)
            norm_stage(MOE0)
            feed_forward(MOE0)
            pipeline(pe, (RET, XATT1), step)
            norm_stage(MOE1)
            feed_forward(MOE1)

        @block.scalar
        def _(act):
            def copy(dst, src, scale=None, bias=None):
                if scale is None and bias is None:
                    return nc.scalar.activation(dst, src, ACT.Copy)
                return nc.scalar.activation(dst, src, ACT.Identity, scale=1.0 if scale is None else scale,
                                            bias=0.0 if bias is None else bias)

            def exp(tile, g):
                if tile.l != RET:
                    wait(act, "p_sub", tile, g + 1)
                    nc.scalar.activation(probs[:, g], probs[:, g], ACT.Exp, scale=HD ** -0.5).then_inc(S["probs"], 1)

            def exp_zero_keys(tile):
                if tile.l == ATT0:
                    wait(act, "zmax_sb", tile)
                    nc.scalar.activation(den[:, tile.p], zmax[:, tile.p], ACT.Exp, scale=HD ** -0.5).then_inc(S["zero_exp"], 1)

            def turn_in(tile):
                p = tile.p
                wait(act, "uT_out", tile)
                if tile.back(3) is not None and tile.back(3).l != RET:
                    wait(act, "oT_out", tile.back(3))
                wait(act, "v_out", tile.back(2))
                gain, shift = {ATT0: ("ln1_g", "ln1_b"), ATT1: ("n1_w", None)}.get(tile.l, (None, None))
                if gain is None:
                    last = copy(hT[:, p].rearrange("p c k -> p (c k)"), ps[:, B_T, 0:D])
                else:
                    for c in range(KC):
                        last = copy(hT[:, p, c], ps[:, B_T, c * P:(c + 1) * P], vec(gain, c), shift and vec(shift, c))
                last.then_inc(S["hT_sb"], 1)

            def turn_out(tile):
                p = tile.p
                wait(act, "oT_out", tile)
                wait(act, "y_out", tile.back(2))
                if tile.l == RET:
                    for c in range(KC):
                        last = copy(oT[:, p, c], ps[:, B_T, D + c * P:D + (c + 1) * P], vec("gamma", c), vec("beta", c))
                else:
                    last = copy(oT[:, p].rearrange("p c k -> p (c k)"), ps[:, B_T, D:2 * D])
                last.then_inc(S["oT_sb"], 1)

            def queries_keys(tile):
                p = tile.p
                wait(act, "qk_out", tile)
                wait(act, "scores_out", tile.back(2))
                wait(act, "km_sb", tile.back(2))
                names = {ATT0: ("bq0", "bk0"), XATT0: ("xbq", "xbk"), XATT1: ("ybq", "ybk")}.get(tile.l)
                if names is None:
                    last = copy(qk[:, p].rearrange("p c k -> p (c k)"), ps[:, B_QK, :])
                else:
                    for m in range(2 * KC):
                        last = copy(qk[:, p, m], ps[:, B_QK, m * P:(m + 1) * P], None, vec(names[m // KC], m % KC))
                last.then_inc(S["qk_sb"], 1)

            def turned_probs(tile, g):
                if tile.l != RET:
                    last = tile.back(1)
                    wait(act, "pT_out", tile, g + 1)
                    if g == 0:
                        wait(act, "pv_out", last)
                    copy(probsT[:, g].rearrange("p h k -> p (h k)"), ps[:, g, :]).then_inc(S["pT_sb"], 1)

            def weighed(tile):
                wait(act, "pv_out", tile)
                wait(act, "sum_out", tile.back(1))
                copy(sumT[:], ps[:, B_O, :]).then_inc(S["sum_sb"], 1)

            def step(at):
                now = at.get(0)
                if 1 in at:
                    queries_keys(at[1])
                if now:
                    exp(now, 0)
                    exp(now, 1)
                late = -1 in at and at[-1].l == RET
                if late and 2 in at:
                    turn_in(at[2])
                if -1 in at and not late:
                    turn_out(at[-1])
                if now:
                    turned_probs(now, 0)
                    exp(now, 2)
                    turned_probs(now, 1)
                    exp(now, 3)
                if 2 in at and not late:
                    turn_in(at[2])
                if now:
                    exp_zero_keys(now)
                    turned_probs(now, 2)
                    turned_probs(now, 3)
                if late:
                    turn_out(at[-1])
                if now:
                    weighed(now)

            def norm_stage(f):
                def step(at):
                    if 0 in at:
                        t, p = at[0]
                        act.wait_ge(S["n_out"], n_reached("n_out", f, t))
                        if not isinstance(t, int) or t >= 2:
                            act.wait_ge(S["fT_sb"], n_reached("fT_sb", f, t - 2))
                            if f != MLP:
                                act.wait_ge(S["lg_out"], n_reached("lg_out", f, t - 2))
                        if f == MOE1:
                            last = copy(hT[:, p].rearrange("p c k -> p (c k)"), ps[:, (B_T, B_QK)[p], 0:D])
                        else:
                            for c in range(KC):
                                last = copy(hT[:, p, c], ps[:, (B_T, B_QK)[p], c * P:(c + 1) * P], vec("ln2_g" if f == MLP else "n2_w", c),
                                            vec("ln2_b", c) if f == MLP else None)
                        last.then_inc(S["n_sb"], 1)
                        act.wait_ge(S["n_sb"], n_reached("n_sb", f, t))
                        copy(fT_hi[:, at_tile(t)], hT[:, p:p + 1]).then_inc(S["fT_hi_sb"], 1)
                norm_pipeline(act, step, lambda: high_weights(f, 0, 0, 0, 1))

            def gate(f, step_):
                if step_ == 0:
                    E = F_ROUTED[f]
                    act.wait_ge(S["gate_p"], NT + (1 if f == MOE0 else 3))
                    nc.scalar.activation(sc[:, :, 0:E], pr[:, :, 0:E], ACT.Exp).then_inc(S["act_gate"], 1)
                if step_ == 1 and f == MOE0:
                    act.wait_ge(S["gate_p"], NT + 2)
                    nc.scalar.activation(w12[:, :, 1:2], w12[:, :, 0:1], ACT.Exp).then_inc(S["act_gate"], 1)

            def high_weights(f, e, p, piece, pieces):
                b, n = buffer(f, p), f_cols(f)
                if piece == 0:
                    act.wait_ge(S["w_raw_in"], e * 16 + 16 * (before(f) + 1))
                    if not isinstance(e, int) or e >= 2:
                        act.wait_ge(S["down_out"], units("down_out", f, e - 2, GROUPS - 1, GT))
                    if f != MOE0:
                        k = F_CHUNKS[f] * (1 if f == MLP else 2)
                        copy(f_bias[:, b, 0:k], w_raw[:, n - k:n]).then_inc(S["f_bias_sb"], 1)
                step_ = n // pieces
                last = copy(w_hi[:, b, piece * step_:(piece + 1) * step_], w_raw[:, piece * step_:(piece + 1) * step_])
                if piece == pieces - 1:
                    last.then_inc(S["w_hi_sb"], 1)

            def feed_forward(f):
                n = F_CHUNKS[f]

                def body(e, p):
                    last_expert = isinstance(e, int) and e == F_EXPERTS[f] - 1
                    for g in range(GROUPS):
                        for fc in range(n):
                            q = g * n + fc
                            act.wait_ge(S["gate_out"], units("gate_out", f, e, g, fc + 1))
                            src = ps[:, q % 2, :]
                            bias = f_bias[:, buffer(f, p), fc:fc + 1]
                            free = "hid_done" if f == MLP else "h_done"
                            used = units(free, f, e, g, fc + 1 - 2)
                            if not (isinstance(used, int) and used <= 0):
                                act.wait_ge(S[free], used)
                            if f == MLP:
                                nc.scalar.activation(h_tmp[:, q % 2, :], src, ACT.Gelu, bias=bias).then_inc(S["act_done"], 1)
                                act.wait_ge(S["act_done"], units("act_done", f, e, g, fc + 1))
                            else:
                                nc.scalar.activation(act_sb[:, q % 2, :], src, ACT.Silu,
                                                     bias=bias if f == MOE1 else 0.0).then_inc(S["act_done"], 1)
                                act.wait_ge(S["h_done"], units("h_done", f, e, g, fc + 1))
                            used = units("down_out", f, e, g, 0) - GT
                            if fc == 0 and not (isinstance(used, int) and used <= 0):
                                act.wait_ge(S["down_out"], used)
                            copy(hid_hi[:, g % 2, fc], h_tmp[:, q % 2, :]).then_inc(S["hi_done"], 1)
                        if f != MLP and isinstance(e, int) and e == 0:
                            gate(f, g)
                        if bias_expert(f, e) and g < 2:
                            for k in range(2):
                                i = 2 * g + k
                                act.wait_ge(S["comb_out"], i + 1)
                                copy(combT[:, i * GN:(i + 1) * GN], ps[0:18, 1 - g + 2 * k, :]).then_inc(S["comb_sb"], 1)
                        if g in (1, 2) and not last_expert:
                            high_weights(f, e + 1, 1 - p, g - 1, 2)
                if f != MOE0:
                    act.wait_ge(S["f_bias_sb"], 1 if f == MLP else F_EXPERTS[MLP] + 1)
                experts(act, f, body)
                act.wait_ge(S["acc_done"], units("acc_done", f, F_EXPERTS[f] - 1, GROUPS - 1, GT))

            act.wait_ge(S["const_in"], 32)
            pipeline(act, (ATT0,), step)
            norm_stage(MLP)
            feed_forward(MLP)
            pipeline(act, (XATT0, ATT1), step)
            norm_stage(MOE0)
            feed_forward(MOE0)
            pipeline(act, (RET, XATT1), step)
            norm_stage(MOE1)
            feed_forward(MOE1)

        @block.vector
        def _(dve):
            tt, ts, stt = nc.vector.tensor_tensor, nc.vector.tensor_scalar, nc.vector.scalar_tensor_tensor

            def moments(x, p, done, own, value):
                nc.vector.bn_stats(stats[:, p], x).then_inc(S[own], 1)
                wait_apart(dve, (own, value))
                nc.vector.bn_aggr(mv[:, p], stats[:, p]).then_inc(S[done], 1)

            def variance(tile):
                l, t = tile.l, tile.t
                if l == ATT0 and isinstance(t, int):
                    if t in (0, 4):
                        dve.wait_ge(S["x_in%d" % (t // 4)], 16)
                    if t == 5:
                        dve.wait_ge(S["x_in2"], 16)
                        dve.wait_ge(S["x_in3"], 16)
                if l in (ATT1, XATT1):
                    wait(dve, "x_done", Tile(l - 1, t, tile.p))
                moments(x_tile(t), tile.p, "var1", "dve_ln", reached("dve_ln", tile, 1))

            def x_tile(t):
                return x_all[:, t] if isinstance(t, int) else x_all[:, at_tile(t)].rearrange("p a d -> p (a d)")

            def r_tile(t):
                return r_all[:, t] if isinstance(t, int) else r_all[:, at_tile(t)].rearrange("p a d -> p (a d)")

            def normalise(tile):
                p, two = tile.p, tile.back(2)
                wait(dve, "rstd1", tile)
                if two is not None:
                    wait(dve, "uT_out", two)
                    if two.l != RET:
                        wait(dve, "base_sb", two)
                ts(u[:, p], x_tile(tile.t), mv[:, p, 0:1], rstd[:, p, 0:1], ALU.subtract, ALU.mult).then_inc(S["u_norm"], 1)

            def second_variance(tile):
                p = tile.p
                wait(dve, "u_norm", tile)
                if tile.l == ATT0:
                    moments(u[:, p], p, "var2", "dve_ln", reached("dve_ln", tile, 2))
                elif tile.l == ATT1:
                    nc.vector.tensor_tensor_reduce(v[:, p], u[:, p], u[:, p], 1.0 / D, 0.0, ALU.mult, ALU.add,
                                                   mv[:, p, 1:2]).then_inc(S["var2"], 1)

            def second_norm(tile):
                p = tile.p
                if tile.l in TWO_NORMS:
                    wait(dve, "rstd2", tile)
                    if tile.l == ATT0:
                        ts(v[:, p], u[:, p], mv[:, p, 0:1], rstd[:, p, 1:2], ALU.subtract, ALU.mult).then_inc(S["v_norm"], 1)
                    else:
                        ts(v[:, p], u[:, p], rstd[:, p, 1:2], None, ALU.mult).then_inc(S["v_norm"], 1)

            def shift(tile, g):
                p = tile.p
                bank = ps[:, g, :].rearrange("p (h k) -> p h k", h=HB)
                wait(dve, "scores_out", tile, g + 1)
                if tile.l == RET:
                    if g == 0:
                        wait(dve, "pv_out", tile.back(1))
                    tt(probsT[:, g], bank, const[:, C_DECAY + g * GN:C_DECAY + (g + 1) * GN].rearrange("p (h k) -> p h k", h=HB),
                       ALU.mult).then_inc(S["ret_sb"], 1)
                    return
                m = negmax[:, p, g * HB:(g + 1) * HB]
                k = 2 if tile.l == ATT0 else 1
                nc.vector.tensor_reduce(m, bank, AX.X, ALU.max, negate=True).then_inc(S["dve_sm"], 1)
                wait(dve, "dve_sm", tile, k * g + 1)
                if tile.l == ATT0:
                    ts(m, m, const[:, C_CLAMP:C_CLAMP + 1], None, ALU.min).then_inc(S["dve_sm"], 1)
                    wait(dve, "dve_sm", tile, k * g + 2)
                last = tile.back(1)
                if last is not None and last.l != RET:
                    wait(dve, "pT_out", last, g + 1)
                tt(probs[:, g], bank, m.unsqueeze(2).to_broadcast([P, HB, P]), ALU.add).then_inc(S["p_sub"], 1)

            def zero_keys(tile):
                if tile.l == ATT0:
                    wait(dve, "zero_exp", tile.back(2))
                    ts(zmax[:, tile.p], negmax[:, tile.p], 0.0, None, ALU.min).then_inc(S["zmax_sb"], 1)

            def values(tile):
                p = tile.p
                if tile.l == ATT0 and isinstance(tile.t, int) and tile.t == 0:
                    dve.wait_ge(S["rows_in"], 16)
                wait(dve, "v_out", tile)
                wait(dve, "pv_out", tile.back(2))
                dst = va[:, p, :, 0:HD]
                src = ps[:, B_V, 0:D].rearrange("p (h d) -> p h d", h=H)
                b = {ATT0: "bv0", XATT0: "xbv", XATT1: "ybv"}.get(tile.l)
                if b is None:
                    nc.vector.tensor_copy(dst, src).then_inc(S["va_sb"], 1)
                else:
                    tt(dst, src, row(b).rearrange("p (h d) -> p h d", h=H), ALU.add).then_inc(S["va_sb"], 1)

            def swap(tile):
                if tile.l in ROTARY:
                    prev = tile.back(1)
                    free = [("pool_m", reached("pool_m", prev, 3))] if prev is not None and prev.l in ROTARY else []
                    wait_apart(dve, ("qk_sb", reached("qk_sb", tile)), *free)
                    nc.vector.stream_shuffle(qk_swap[:], qk[:, tile.p], [i ^ 1 for i in range(32)]).then_inc(S["swapped"], 1)

            def keys(tile):
                if tile.l in ROTARY:
                    wait(dve, "pool_m", tile, 3)
                wait(dve, "qk_sb", tile)
                wait(dve, "scores_out", tile.back(1))
                src = qk[:, tile.p, 0:KC] if tile.l == RET else qk[:, tile.p, KC:2 * KC]
                for j in range(HC):
                    last = ts(km[:, :, j, :], src, head_mask[:, j:j + 1], None, ALU.mult)
                last.then_inc(S["km_sb"], 1)

            def attended(tile):
                p = tile.p
                O = ps[:, B_O, 0:H * VW].rearrange("p (h d) -> p h d", h=H)
                oh = o[:, p].rearrange("p (h d) -> p h d", h=H)
                wait(dve, "sum_out", tile)
                wait(dve, "oT_out", tile.back(2))

                def link(ins, k):
                    ins.then_inc(S["dve_o"], 1)
                    wait(dve, "dve_o", tile, k)

                if tile.l == RET:
                    g = gn[:, p]
                    link(nc.vector.tensor_reduce(g[:, 0], O[:, :, 0:HD], AX.X, ALU.add), 1)
                    link(ts(g[:, 1], g[:, 0], -1.0 / HD, None, ALU.mult), 2)
                    link(tt(oh, O[:, :, 0:HD], g[:, 1].unsqueeze(2).to_broadcast([P, H, HD]), ALU.add), 3)
                    link(tt(gsq[:], o[:, p], o[:, p], ALU.mult), 4)
                    nc.vector.tensor_reduce(g[:, 0], gsq[:].rearrange("p (h d) -> p h d", h=H), AX.X,
                                            ALU.add).then_inc(S["gn_var"], 1)
                    return
                total, k = O[:, :, HD], 1
                if tile.l == ATT0:
                    wait(dve, "zero_exp", tile)
                    total = den[:, p]
                    link(stt(out=total, in0=total, scalar=const[:, C_ZKEYS:C_ZKEYS + 1], in1=O[:, :, HD], op0=ALU.mult,
                             op1=ALU.add), 1)
                    k = 2
                link(nc.vector.reciprocal(zmax[:, p] if tile.l == ATT0 else den[:, p], total), k)
                inv = zmax[:, p] if tile.l == ATT0 else den[:, p]
                tt(oh, O[:, :, 0:HD], inv.unsqueeze(2).to_broadcast([P, H, HD]), ALU.mult).then_inc(S["o_norm"], 1)

            def head_norm(tile):
                if tile.l == RET:
                    oh = o[:, tile.p].rearrange("p (h d) -> p h d", h=H)
                    wait(dve, "gn_rstd", tile)
                    tt(oh, oh, gn[:, tile.p, 2].unsqueeze(2).to_broadcast([P, H, HD]), ALU.mult).then_inc(S["o_norm"], 1)

            def residual(tile):
                dst = (r_tile if tile.l in BRANCH else x_tile)(tile.t)
                wait(dve, "y_out", tile)
                if tile.l != RET:
                    wait(dve, "base_sb", tile)
                tt(dst, output(tile), dst, ALU.add).then_inc(S["x_done"], 1)

            def late_step(at, now, out):
                attended(out)
                if 1 in at:
                    swap(at[1])
                if now:
                    for g in range(NG):
                        shift(now, g)
                if 3 in at:
                    variance(at[3])
                head_norm(out)
                if 1 in at:
                    values(at[1])
                    keys(at[1])
                residual(out)
                if 3 in at:
                    normalise(at[3])

            def step(at):
                now, out = at.get(0), at.get(-1)
                if out and out.l == RET:
                    late_step(at, now, out)
                    return
                if 1 in at:
                    swap(at[1])
                if now:
                    shift(now, 0)
                    shift(now, 1)
                if out:
                    attended(out)
                if now:
                    shift(now, 2)
                if now:
                    shift(now, 3)
                    zero_keys(now)
                if 3 in at:
                    variance(at[3])
                if out:
                    residual(out)
                if 1 in at:
                    keys(at[1])
                if 3 in at:
                    normalise(at[3])
                    if at[3].l in TWO_NORMS:
                        second_variance(at[3])
                if 1 in at:
                    values(at[1])
                if 3 in at:
                    second_norm(at[3])

            def norm_stage(f):
                def step(at):
                    src = x_tile if f == MOE1 else r_tile
                    if 0 in at:
                        t, p = at[0]
                        dve.wait_ge(S["n_rstd"], n_reached("n_rstd", f, t))
                        if not isinstance(t, int) or t >= 2:
                            dve.wait_ge(S["n_out"], n_reached("n_out", f, t - 2))
                        if f == MOE0:
                            ins = ts(v[:, p], src(t), rstd[:, p, 0:1], None, ALU.mult)
                        else:
                            ins = ts(v[:, p], src(t), mv[:, p, 0:1], rstd[:, p, 0:1], ALU.subtract, ALU.mult)
                        ins.then_inc(S["n_norm"], 1)
                        if f != MOE1:
                            tt(x_tile(t), x_tile(t), src(t), ALU.add).then_inc(S["gate_p" if f == MLP else "n_base"], 1)
                    if 2 in at:
                        t, p = at[2]
                        if f == MOE0:
                            if not (isinstance(t, int) and t == 0):
                                dve.wait_ge(S["n_var"], n_reached("n_var", f, t - 1))
                            tt(gsq[:], src(t), src(t), ALU.mult).then_inc(S["n_sq"], 1)
                            dve.wait_ge(S["n_sq"], t + 1)
                            nc.vector.tensor_reduce(mv[:, p, 1:2], gsq[:], AX.X, ALU.add).then_inc(S["n_var"], 1)
                        else:
                            moments(src(t), p, "n_var", "dve_n", (f // 2) * NT + t + 1)
                    if -1 in at:
                        t, p = at[-1]
                        dve.wait_ge(S["fT_hi_sb"], n_reached("fT_hi_sb", f, t))
                        if f != MOE1:
                            dve.wait_ge(S["gate_p" if f == MLP else "n_base"], t + 1 if f == MLP else n_reached("n_base", f, t))
                        one = (lambda a: a[:, t]) if isinstance(t, int) else \
                            (lambda a: a[:, at_tile(t)].rearrange("p a c k -> p (a c) k"))
                        tt(one(fT_lo), hT[:, p], one(fT_hi).bitcast(f32), ALU.subtract).then_inc(S["fT_sb"], 1)
                wait(dve, "x_done", tiles_of(LAST[f], NT - 1))
                norm_pipeline(dve, step)
                b, n = buffer(f, 0), f_cols(f)
                dve.wait_ge(S["w_hi_sb"], weights_reached(f, 0))
                tt(w_lo[:, b, 0:n], w_raw[:, 0:n], w_hi[:, b, 0:n].bitcast(f32), ALU.subtract).then_inc(S["w_lo_sb"], 1)

            chain = [0]

            def link(ins):
                ins.then_inc(S["gate"], 1)
                chain[0] += 1
                dve.wait_ge(S["gate"], chain[0])

            def over(a, n):
                return a.unsqueeze(2).to_broadcast([P, NT, n])

            def take_logits(f):
                dve.wait_ge(S["lg_out"], NT * f)
                nc.vector.tensor_copy(lg[:, :, 0:F_ROUTED[f]], logits(f)).then_inc(S["lg_sb"], 1)
                dve.wait_ge(S["lg_sb"], f)

            def softmax(f):
                E = F_ROUTED[f]
                L, pe_, se = lg[:, :, 0:E], pr[:, :, 0:E], sc[:, :, 0:E]
                link(nc.vector.tensor_reduce(red[:], L, AX.X, ALU.max))
                tt(pe_, L, over(red[:], E), ALU.subtract).then_inc(S["gate_p"], 1)
                dve.wait_ge(S["act_gate"], 1 if f == MOE0 else 3)
                link(nc.vector.tensor_reduce(red[:], se, AX.X, ALU.add))
                link(nc.vector.reciprocal(red[:], red[:]))
                link(tt(pe_, se, over(red[:], E), ALU.mult))

            def best(values_):
                for t in range(NT):
                    last = nc.vector.max(top[:, t], values_[:, t])
                link(last)
                for t in range(NT):
                    last = nc.vector.max_index(idx[:, t], top[:, t], values_[:, t])
                link(last)
                link(nc.vector.tensor_copy(idx_f[:], idx[:, :, 0:2]))

            def one_hot(dst, k, n):
                link(tt(dst, iota[:, 0:n].unsqueeze(1).to_broadcast([P, NT, n]), over(idx_f[:, :, k], n), ALU.is_equal))

            def gate_moe0(step_):
                h = hot[:, :, 0:8]
                if step_ == 0:
                    softmax(MOE0)
                if step_ == 1:
                    best(pr[:, :, 0:8])
                    tt(w12[:, :, 0], top[:, :, 1], top[:, :, 0], ALU.subtract).then_inc(S["gate_p"], 1)
                if step_ == 2:
                    dve.wait_ge(S["act_gate"], 2)
                    link(ts(w12[:, :, 2], w12[:, :, 1], 1.0, None, ALU.add))
                    link(nc.vector.reciprocal(w12[:, :, 3], w12[:, :, 2]))
                    link(tt(w12[:, :, 2], w12[:, :, 1], w12[:, :, 3], ALU.mult))
                    one_hot(h, 0, 8)
                    link(tt(comb[:, :, 2:10], h, over(w12[:, :, 3], 8), ALU.mult))
                    one_hot(h, 1, 8)
                    link(tt(h, h, over(w12[:, :, 2], 8), ALU.mult))
                    tt(comb[:, :, 2:10], comb[:, :, 2:10], h, ALU.add).then_inc(S["gate_done"], 1)
                    dve.wait_ge(S["gate_done"], 1)

            def gate_moe1(step_):
                s4 = sc[:].rearrange("p t (g e) -> p (t g) e", g=4)
                keep = hot[:, :, 0:4]
                if step_ == 0:
                    softmax(MOE1)
                if step_ == 1:
                    link(tt(sc[:], pr[:], gate_b[:].unsqueeze(1).to_broadcast([P, NT, 16]), ALU.add))
                    tt(pairs[:, :, 0:3], s4[:, :, 0:3], s4[:, :, 1:4], ALU.add)
                    tt(pairs[:, :, 3:5], s4[:, :, 0:2], s4[:, :, 2:4], ALU.add)
                    link(tt(pairs[:, :, 5:6], s4[:, :, 0:1], s4[:, :, 3:4], ALU.add))
                    link(nc.vector.tensor_reduce(grp[:, :, 0:4], pairs[:].rearrange("p (t g) e -> p t g e", g=4), AX.X, ALU.max))
                if step_ == 2:
                    best(grp)
                if step_ == 3:
                    one_hot(keep, 0, 4)
                    one_hot(hot[:, :, 4:8], 1, 4)
                    link(tt(keep, keep, hot[:, :, 4:8], ALU.add))
                    link(ts(keep, keep, -1.0, BIG, ALU.add, ALU.mult))
                    k4 = keep.unsqueeze(3).to_broadcast([P, NT, 4, 4])
                    link(tt(sc[:].rearrange("p t (g e) -> p t g e", g=4), sc[:].rearrange("p t (g e) -> p t g e", g=4), k4, ALU.add))
                if step_ == 4:
                    best(sc)
                if step_ == 5:
                    one_hot(hot[:], 0, 16)
                    one_hot(sc[:], 1, 16)
                    link(tt(hot[:], hot[:], sc[:], ALU.add))
                    tt(comb[:, :, 2:18], hot[:], pr[:], ALU.mult).then_inc(S["gate_done"], 1)
                    dve.wait_ge(S["gate_done"], 2)

            def feed_forward(f):
                n = F_CHUNKS[f]

                def hidden(e, p, g):
                    for fc in range(n):
                        q = g * n + fc
                        h = h_tmp[:, q % 2, :]
                        if f != MLP:
                            dve.wait_ge(S["up_out"], units("up_out", f, e, g, fc + 1))
                            dve.wait_ge(S["act_done"], units("act_done", f, e, g, fc + 1))
                            if f == MOE0:
                                ins = tt(h, ps[:, 2 + q % 2, :], act_sb[:, q % 2, :], ALU.mult)
                            else:
                                ins = stt(out=h, in0=ps[:, 2 + q % 2, :], scalar=f_bias[:, buffer(f, p), 1:2],
                                          in1=act_sb[:, q % 2, :], op0=ALU.add, op1=ALU.mult)
                            ins.then_inc(S["h_done"], 1)
                        dve.wait_ge(S["hi_done"], units("hi_done", f, e, g, fc + 1))
                        tt(hid_lo[:, g % 2, fc], h, hid_hi[:, g % 2, fc].bitcast(f32), ALU.subtract).then_inc(S["hid_done"], 1)

                def add(e, p, g):
                    biases = f == MOE1 and isinstance(e, int) and e == F_EXPERTS[f] - 1
                    if biases:
                        for j in range(GT):
                            t = g * GT + j
                            dve.wait_ge(S["down_out"], units("down_out", f, e, g, j + 1))
                            dve.wait_ge(S["acc_done"], units("acc_done", f, e - 1, g, j + 1))
                            tt(x_all[:, t], ps[:, 4 + j, D:2 * D], x_all[:, t], ALU.add).then_inc(S["bias_done"], 1)
                    for j in range(GT):
                        t = g * GT + j
                        if biases:
                            dve.wait_ge(S["bias_done"], t + 1)
                        dve.wait_ge(S["down_out"], units("down_out", f, e, g, j + 1))
                        if not (isinstance(e, int) and e == 0):
                            dve.wait_ge(S["acc_done"], units("acc_done", f, e - 1, g, j + 1))
                        y = ps[:, 4 + j, 0:D]
                        if f == MLP and isinstance(e, int) and e == 0:
                            dve.wait_ge(S["n_base"], t + 1)
                        if f == MLP:
                            ins = tt(x_all[:, t], y, x_all[:, t], ALU.add)
                        else:
                            ins = stt(out=x_all[:, t], in0=y, scalar=comb_e[:, p, t:t + 1], in1=x_all[:, t], op0=ALU.mult, op1=ALU.add)
                        ins.then_inc(S["acc_done"], 1)

                def body(e, p):
                    if f != MLP:
                        k = 1 if f == MOE0 else 0
                        src = comb[:, :, e + k:e + k + 1] if isinstance(e, int) else comb[:, :, bass.ds(e + k, 1)]
                        nc.vector.tensor_copy(comb_e[:, p].unsqueeze(2), src).then_inc(S["comb_e_sb"], 1)
                    for g in range(GROUPS):
                        hidden(e, p, g)
                        if g:
                            if g == 1 and f != MLP:
                                dve.wait_ge(S["comb_e_sb"], e + (before(f) - F_EXPERTS[MLP] + 1))
                            add(e, p, g - 1)
                        elif not (isinstance(e, int) and e == 0):
                            add(e - 1, 1 - p, GROUPS - 1)
                        if f == MOE0 and isinstance(e, int) and e == 0:
                            gate_moe0(g)
                        if f == MOE1 and isinstance(e, int) and e < 2:
                            gate_moe1(e * GROUPS + g)

                if f == MOE0:
                    dve.wait_ge(S["n_base"], NT * 2)
                experts(dve, f, body)
                n_e = F_EXPERTS[f] - 1
                add(n_e, n_e % 2, GROUPS - 1)
                dve.wait_ge(S["acc_done"], units("acc_done", f, n_e, GROUPS - 1, GT))

            dve.wait_ge(S["const_in"], 32)
            dve.wait_ge(S["setup"], 7)
            pipeline(dve, (ATT0,), step)
            norm_stage(MLP)
            feed_forward(MLP)
            dve.wait_ge(S["late_in"], 80)
            pipeline(dve, (XATT0, ATT1), step)
            norm_stage(MOE0)
            take_logits(MOE0)
            feed_forward(MOE0)
            pipeline(dve, (RET, XATT1), step)
            norm_stage(MOE1)
            take_logits(MOE1)
            feed_forward(MOE1)


def kernel(**inputs):
    import concourse.bacc as _bacc
    from concourse.bass_utils import run_bass_kernel_spmd as _run

    a = {k: np.asarray(v) for k, v in inputs.items()}

    def chunked(w):
        return w.reshape(-1, P, w.shape[-1]).transpose(1, 0, 2).reshape(P, -1)

    def attention(q, k, v, o):
        return np.concatenate([chunked(np.concatenate([q, k, v], 1)), chunked(o)], 1)

    def heads_last(w):
        return w.reshape(D, D).T

    n = "L0_ffn_"
    w_att = np.stack([
        np.concatenate([chunked(a["L0_attn_w_qkv"]), chunked(a["L0_attn_w_out"])], 1),
        attention(a["L0_xattn_Wq"], a["L0_xattn_Wk"], a["L0_xattn_Wv"], a["L0_xattn_Wo"]),
        attention(a[n + "wq"], a[n + "wk"], a[n + "wv"], a[n + "wo"]),
        attention(heads_last(a["L1_attn_WQ"]), heads_last(a["L1_attn_WK"]), heads_last(a["L1_attn_WV"]), a["L1_attn_WO"]),
        attention(a["L1_xattn_Wq"].T, a["L1_xattn_Wk"].T, a["L1_xattn_Wv"].T, a["L1_xattn_Wo"].T)])
    w1, w2, b1 = a["L0_attn_w1"], a["L0_attn_w2"], a["L0_attn_b1"]
    w_mlp = np.stack([np.concatenate([chunked(w1[:, s]), chunked(w2[s]), b1[s].reshape(-1, P).T], 1)
                      for s in (slice(0, 512), slice(512, 1024))])
    w_moe0 = np.stack([np.concatenate([chunked(g), chunked(u), chunked(d)], 1) for g, u, d in
                       [(a[n + "sh_gate"], a[n + "sh_up"], a[n + "sh_down"])]
                       + [(a[n + "e_gate"][e], a[n + "e_up"][e], a[n + "e_down"][e]) for e in range(8)]])
    n = "L1_ffn_"
    halves = (slice(0, P), slice(P, 2 * P))
    w_moe1 = np.stack([np.concatenate([chunked(g), chunked(u), chunked(d), bg[:, None], bu[:, None]], 1) for g, u, d, bg, bu in
                       [(a[n + "ws1"][:, s], a[n + "ws3"][:, s], a[n + "ws2"][s], a[n + "bs1"][s], a[n + "bs3"][s]) for s in halves]
                       + [(a[n + "We1"][e], a[n + "We3"][e], a[n + "We2"][e], a[n + "be1"][e], a[n + "be3"][e]) for e in range(16)]])
    be2 = np.concatenate([a[n + "bs2"][None], np.zeros((1, D), np.float32), a[n + "be2"]])
    bq = a["L0_attn_b_qkv"]
    vectors = [a["L0_attn_ln1_g"], a["L0_attn_ln1_b"], bq[0:D], bq[D:2 * D], a["L0_attn_ln2_g"], a["L0_attn_ln2_b"],
               a["L0_xattn_bq"], a["L0_xattn_bk"], a["L0_ffn_norm1_w"], a["L0_ffn_norm2_w"], a["L1_attn_gamma"],
               a["L1_attn_beta"], a["L1_xattn_bq"], a["L1_xattn_bk"]]
    vecs = np.stack(vectors).reshape(len(VEC), KC, P).transpose(2, 0, 1).reshape(P, -1)
    rows = np.concatenate([bq[2 * D:], a["L0_attn_b_out"], a["L0_attn_b2"], a["L0_xattn_bv"], a["L0_xattn_bo"],
                           a["L1_xattn_bv"], a["L1_xattn_bo"]])[None]
    router = np.concatenate([a["L0_ffn_router_w"], a["L1_ffn_gate_w"].T], 1).reshape(KC, P, 24).transpose(1, 0, 2).reshape(P, -1)
    ctxT = a["ctx_1024"].transpose(0, 2, 1).reshape(NT, KC, P, P).transpose(0, 2, 1, 3).reshape(NT, P, KC * P)
    arrays = {"x": a["x"], "const": constants(), "vecs": vecs, "rows": rows, "router": router,
              "gate_b": a["L1_ffn_gate_b"][None], "be2": be2, "pad": a["mask_BxS2_bf0"], "w_att": w_att,
              "w_f0": w_mlp, "w_f1": w_moe0, "w_f2": w_moe1, "ctxT": ctxT}
    nc = _bacc.Bacc("TRN2", target_bir_lowering=False, num_devices=1)
    arrays = {"in_" + k: np.ascontiguousarray(v) for k, v in arrays.items()}
    A = {k[3:]: nc.dram_tensor(k, v.shape, mybir.dt.from_np(v.dtype), kind="ExternalInput").ap() for k, v in arrays.items()}
    A["out"] = nc.dram_tensor("out_0", (NT, P, D), mybir.dt.float32, kind="ExternalOutput").ap()
    build(nc, A)
    r = _run(nc, [arrays], core_ids=[0])
    return r.results[0]["out_0"]
```
